# Optimizing a Trainium2 kernel written in Bass

```python
import numpy as np
import jax
import jax.numpy as jnp

def _softmax(x, axis=-1):
    return jax.nn.softmax(x, axis=axis)

def _gelu(x):
    return jax.nn.gelu(x, approximate=True)

def _silu(x):
    return jax.nn.silu(x)

def _sigmoid(x):
    return jax.nn.sigmoid(x)

def _layernorm(x, axis=-1, eps=1e-05):
    m = jnp.mean(x, axis=axis, keepdims=True)
    v = jnp.var(x, axis=axis, keepdims=True)
    return (x - m) / jnp.sqrt(v + eps)

def _scatter_add(tgt, idx, src, axis=0):
    return tgt.at[idx].add(src)

def _segment_sum(src, seg, n):
    return jax.ops.segment_sum(src, seg, n)
kernel_name = 'mk_perceiver_d1_seqx_r8_3fe034'

def setup_inputs(seed: int=0):
    np.random.seed(seed)
    _w = jnp.asarray

    def _rec_inputs():
        import jax
        import jax.numpy as jnp
        _rk = jax.random.key(seed)
        x = 7.22e-05 + 1 * jax.random.normal(jax.random.fold_in(_rk, 1), (128, 32, 128), jnp.float32)
        _lenS = 32 - jax.random.randint(jax.random.fold_in(_rk, 7), (128,), 0, max(1, 32 // 4) + 1, jnp.int32)
        _lenS2 = 257 - jax.random.randint(jax.random.fold_in(_rk, 8), (128,), 0, max(1, 257 // 4) + 1, jnp.int32)
        _ctx_1024P = jax.random.normal(jax.random.fold_in(_rk, 11), (128, 16, 128), jnp.float32)
        _ctx_1024c = jax.random.dirichlet(jax.random.fold_in(_rk, 511), 0.3 * jnp.ones((16,), jnp.float32), (128, 257))
        _ctx_1024t = jnp.einsum('bsk,bkd->bsd', _ctx_1024c, _ctx_1024P)
        _ctx_1024t = _ctx_1024t * jax.lax.rsqrt(jnp.mean(jnp.square(_ctx_1024t)) + 1e-12) * 0.953939
        ctx_1024 = -1.52775e-05 + 0.999936 * (_ctx_1024t + 0.3 * jax.random.normal(jax.random.fold_in(_rk, 611), (128, 257, 128), jnp.float32))
        _validS = jnp.arange(32)[None, :] < _lenS[:, None]
        _validS2 = jnp.arange(257)[None, :] < _lenS2[:, None]
        _causal = jnp.tril(jnp.ones((32, 32), dtype=bool))
        mask_BxS_bf1 = jnp.ones((128, 32), dtype=bool)
        return (x, ctx_1024, mask_BxS_bf1)
    x, ctx_1024, mask_BxS_bf1 = _rec_inputs()

    def _L0_xattn_setup():
        import jax, jax.numpy as jnp
        import numpy as np
        L = 2
        D = 128
        HS = 128
        NH = 16
        DH = 64
        FF = 512
        ROT = 32
        B, SQ, SK = (64, 128, 64)
        EPS = 1e-08

        def rmsnorm(x, w):
            norm = jnp.sqrt(jnp.sum(x * x, axis=-1, keepdims=True)) * x.shape[-1] ** (-0.5)
            return x / jnp.maximum(norm, EPS) * w

        def rope_freqs(n):
            inv_freq = 1.0 / 10000.0 ** (jnp.arange(0, ROT, 2, dtype=jnp.float32) / ROT)
            f = jnp.arange(n, dtype=jnp.float32)[:, None] * inv_freq[None, :]
            return jnp.concatenate([f, f], axis=-1)[None, None]

        def apply_rope(t, freqs):
            rd = freqs.shape[-1]
            t1, tp = (t[..., :rd], t[..., rd:])
            half = rd // 2
            a, b = (t1[..., :half], t1[..., half:])
            rot = jnp.concatenate([-b, a], axis=-1)
            t1 = t1 * jnp.cos(freqs) + rot * jnp.sin(freqs)
            return jnp.concatenate([t1, tp], axis=-1)

        def attention(x, ctx, Wq, Wk, Wv, Wo, bo, pe_q, pe_k, mask):
            b, n, _ = x.shape
            m = ctx.shape[1]
            q = (x @ Wq).reshape(b, n, NH, DH).transpose(0, 2, 1, 3) * DH ** (-0.5)
            k = (ctx @ Wk).reshape(b, m, NH, DH).transpose(0, 2, 1, 3)
            v = (ctx @ Wv).reshape(b, m, NH, DH).transpose(0, 2, 1, 3)
            q = apply_rope(q, pe_q)
            k = apply_rope(k, pe_k)
            sim = jnp.einsum('bhid,bhjd->bhij', q, k)
            if mask is not None:
                sim = jnp.where(mask[:, None, None, :], sim, -jnp.finfo(sim.dtype).max)
            attn = jax.nn.softmax(sim, axis=-1)
            out = jnp.einsum('bhij,bhjd->bhid', attn, v)
            out = out.transpose(0, 2, 1, 3).reshape(b, n, NH * DH)
            return out @ Wo + bo
        key = jax.random.key(seed)
        ks = jax.random.split(key, 24)
        s = 0.02
        inp = {'x': jax.random.normal(ks[0], (B, SQ, D), jnp.float32), 'chunked_seq': jax.random.normal(ks[1], (B, SK, HS), jnp.float32), 'mask': jnp.ones((B, SQ), dtype=bool), 'attn_norm_w': jnp.ones((L, D), jnp.float32), 'Wq': jax.random.normal(ks[2], (L, D, NH * DH), jnp.float32) * s, 'Wk': jax.random.normal(ks[3], (L, D, NH * DH), jnp.float32) * s, 'Wv': jax.random.normal(ks[4], (L, D, NH * DH), jnp.float32) * s, 'Wo': jax.random.normal(ks[5], (L, NH * DH, D), jnp.float32) * s, 'bo': jnp.zeros((L, D), jnp.float32), 'cross_norm_w': jnp.ones((L, D), jnp.float32), 'cWq': jax.random.normal(ks[6], (L, D, NH * DH), jnp.float32) * s, 'cWk': jax.random.normal(ks[7], (HS, NH * DH), jnp.float32) * s if False else jax.random.normal(ks[7], (L, HS, NH * DH), jnp.float32) * s, 'cWv': jax.random.normal(ks[8], (L, HS, NH * DH), jnp.float32) * s, 'cWo': jax.random.normal(ks[9], (L, NH * DH, D), jnp.float32) * s, 'cbo': jnp.zeros((L, D), jnp.float32), 'ff_norm_w': jnp.ones((L, D), jnp.float32), 'ff_w1': jax.random.normal(ks[10], (L, D, FF), jnp.float32) * s, 'ff_b1': jnp.zeros((L, FF), jnp.float32), 'ff_w2': jax.random.normal(ks[11], (L, FF, D), jnp.float32) * s, 'ff_b2': jnp.zeros((L, D), jnp.float32), 'norm_out_w': jnp.ones((D,), jnp.float32), 'proj_w': jax.random.normal(ks[12], (D, HS), jnp.float32) * s, 'proj_b': jnp.zeros((HS,), jnp.float32)}
        return inp
    _L0_xattn_all = _L0_xattn_setup()
    _L0_xattn_in = {k: v for k, v in _L0_xattn_all.items() if k in ('attn_norm_w', 'Wq', 'Wk', 'Wv', 'Wo', 'bo', 'cross_norm_w', 'cWq', 'cWk', 'cWv', 'cWo', 'cbo', 'ff_norm_w', 'ff_w1', 'ff_b1', 'ff_w2', 'ff_b2', 'norm_out_w', 'proj_w', 'proj_b')}
    del _L0_xattn_all

    def _L0_attn_setup():
        import jax, jax.numpy as jnp
        import numpy as np
        H_DIM = 128
        N_HEADS = 16
        HEAD_DIM = H_DIM // N_HEADS
        MAX_POS = 256
        BASE = 10000.0
        SCALING_FACTOR = 1.0

        def rotate_half(x):
            return jnp.concatenate([-x[..., 1::2], x[..., ::2]], axis=-1)

        def rope_cos_sin(seq_len, dtype):
            base = BASE
            if seq_len > MAX_POS:
                base = BASE * (SCALING_FACTOR * seq_len / MAX_POS - (SCALING_FACTOR - 1.0)) ** (HEAD_DIM / (HEAD_DIM - 2))
            inv_freq = 1.0 / base ** (jnp.arange(0, HEAD_DIM, 2, dtype=jnp.float32) / HEAD_DIM)
            t = jnp.arange(seq_len, dtype=jnp.float32)
            freqs = jnp.einsum('i,j->ij', t, inv_freq)
            emb = jnp.concatenate([freqs, freqs], axis=-1)
            return (emb.astype(dtype), jnp.cos(emb).astype(dtype), jnp.sin(emb).astype(dtype))
        key = jax.random.key(seed)
        ks = jax.random.split(key, 5)
        B, S = (1, 512)
        scale_w = 0.02
        return {'hidden_states': jax.random.normal(ks[0], (B, S, H_DIM), dtype=jnp.float32), 'Wq': jax.random.normal(ks[1], (H_DIM, H_DIM), dtype=jnp.float32) * scale_w, 'Wk': jax.random.normal(ks[2], (H_DIM, H_DIM), dtype=jnp.float32) * scale_w, 'Wv': jax.random.normal(ks[3], (H_DIM, H_DIM), dtype=jnp.float32) * scale_w, 'Wo': jax.random.normal(ks[4], (H_DIM, H_DIM), dtype=jnp.float32) * scale_w}
    _L0_attn_all = _L0_attn_setup()
    _L0_attn_in = {k: v for k, v in _L0_attn_all.items() if k in ('Wq', 'Wk', 'Wv', 'Wo')}
    del _L0_attn_all

    def _L0_ffn_setup():
        import jax, jax.numpy as jnp
        import numpy as np
        D_MODEL = 128
        N_HEADS = 16
        HEAD_DIM = D_MODEL // N_HEADS
        FFN_DIM = 512
        N_EXPERTS = 8
        CAP_FRAC = 0.25
        MOE_TOKEN_DROPOUT = 0.2
        LN_EPS = 1e-05
        B, S = (4, 64)

        def _layer_norm(x, g, b):
            mu = x.mean(-1, keepdims=True)
            var = ((x - mu) ** 2).mean(-1, keepdims=True)
            return (x - mu) * jax.lax.rsqrt(var + LN_EPS) * g + b

        def _self_attention(x, wq, bq, wk, bk, wv, bv, wo, bo):
            b, s, d = x.shape
            q = ((x @ wq + bq) * HEAD_DIM ** (-0.5)).reshape(b, s, N_HEADS, HEAD_DIM)
            k = (x @ wk + bk).reshape(b, s, N_HEADS, HEAD_DIM)
            v = (x @ wv + bv).reshape(b, s, N_HEADS, HEAD_DIM)
            scores = jnp.einsum('bqhd,bkhd->bhqk', q, k)
            p = jax.nn.softmax(scores, axis=-1)
            o = jnp.einsum('bhqk,bkhd->bqhd', p, v).reshape(b, s, d)
            return o @ wo + bo

        def _moe_ffn(x, wr, w1, b1, w2, b2):
            T, D = x.shape
            C = int(np.ceil(CAP_FRAC * T))
            logits = x @ wr
            probs = jax.nn.softmax(logits, axis=-1)
            top1 = jnp.argmax(probs, axis=-1)
            m1 = jax.nn.one_hot(top1, N_EXPERTS, dtype=x.dtype)
            top2 = jnp.argmax(jnp.where(m1 > 0, -jnp.inf, logits), axis=-1)
            m2 = jax.nn.one_hot(top2, N_EXPERTS, dtype=x.dtype)
            loc1 = jnp.cumsum(m1, axis=0) - 1.0
            loc2 = jnp.cumsum(m2, axis=0) - 1.0 + m1.sum(0, keepdims=True)
            m1 = m1 * (loc1 < C)
            m2 = m2 * (loc2 < C)
            t1 = (probs * m1).sum(-1)
            t2 = (probs * m2).sum(-1)
            denom = jnp.maximum(t1 + t2, jnp.finfo(x.dtype).eps)
            t1, t2 = (t1 / denom, t2 / denom)
            tok = jnp.arange(T)
            s1 = loc1[tok, top1].astype(jnp.int32)
            s2 = loc2[tok, top2].astype(jnp.int32)
            v1 = m1[tok, top1] > 0
            v2 = m2[tok, top2] > 0
            s1 = jnp.where(v1, s1, C)
            s2 = jnp.where(v2, s2, C)
            buf = jnp.zeros((N_EXPERTS, C, D), x.dtype)
            buf = buf.at[top1, s1].set(x, mode='drop')
            buf = buf.at[top2, s2].set(x, mode='drop')
            h = jax.nn.relu(jnp.einsum('ecd,edf->ecf', buf, w1) + b1[:, None, :])
            y = (jnp.einsum('ecf,efd->ecd', h, w2) + b2[:, None, :]) * (1.0 - MOE_TOKEN_DROPOUT)
            y1 = y[top1, jnp.minimum(s1, C - 1)]
            y2 = y[top2, jnp.minimum(s2, C - 1)]
            g1 = t1 * v1
            g2 = t2 * v2
            return g1[:, None] * y1 + g2[:, None] * y2
        key = jax.random.key(seed)
        ks = jax.random.split(key, 20)

        def w(k, shape, scale=0.02):
            return jax.random.normal(k, shape, jnp.float32) * scale
        return {'x': jax.random.normal(ks[0], (B, S, D_MODEL), jnp.float32), 'wq': w(ks[1], (D_MODEL, D_MODEL)), 'bq': w(ks[2], (D_MODEL,)), 'wk': w(ks[3], (D_MODEL, D_MODEL)), 'bk': w(ks[4], (D_MODEL,)), 'wv': w(ks[5], (D_MODEL, D_MODEL)), 'bv': w(ks[6], (D_MODEL,)), 'wo': w(ks[7], (D_MODEL, D_MODEL)), 'bo': w(ks[8], (D_MODEL,)), 'ln1_g': 1.0 + w(ks[9], (D_MODEL,)), 'ln1_b': w(ks[10], (D_MODEL,)), 'ln2_g': 1.0 + w(ks[11], (D_MODEL,)), 'ln2_b': w(ks[12], (D_MODEL,)), 'wr': w(ks[13], (D_MODEL, N_EXPERTS)), 'w1': w(ks[14], (N_EXPERTS, D_MODEL, FFN_DIM)), 'b1': w(ks[15], (N_EXPERTS, FFN_DIM)), 'w2': w(ks[16], (N_EXPERTS, FFN_DIM, D_MODEL)), 'b2': w(ks[17], (N_EXPERTS, D_MODEL))}
    _L0_ffn_all = _L0_ffn_setup()
    _L0_ffn_in = {k: v for k, v in _L0_ffn_all.items() if k in ('wq', 'bq', 'wk', 'bk', 'wv', 'bv', 'wo', 'bo', 'ln1_g', 'ln1_b', 'ln2_g', 'ln2_b', 'wr', 'w1', 'b1', 'w2', 'b2')}
    del _L0_ffn_all
    return {'x': x, 'ctx_1024': ctx_1024, 'mask_BxS_bf1': mask_BxS_bf1, 'L0_xattn_attn_norm_w': _L0_xattn_in['attn_norm_w'], 'L0_xattn_Wq': _L0_xattn_in['Wq'], 'L0_xattn_Wk': _L0_xattn_in['Wk'], 'L0_xattn_Wv': _L0_xattn_in['Wv'], 'L0_xattn_Wo': _L0_xattn_in['Wo'], 'L0_xattn_bo': _L0_xattn_in['bo'], 'L0_xattn_cross_norm_w': _L0_xattn_in['cross_norm_w'], 'L0_xattn_cWq': _L0_xattn_in['cWq'], 'L0_xattn_cWk': _L0_xattn_in['cWk'], 'L0_xattn_cWv': _L0_xattn_in['cWv'], 'L0_xattn_cWo': _L0_xattn_in['cWo'], 'L0_xattn_cbo': _L0_xattn_in['cbo'], 'L0_xattn_ff_norm_w': _L0_xattn_in['ff_norm_w'], 'L0_xattn_ff_w1': _L0_xattn_in['ff_w1'], 'L0_xattn_ff_b1': _L0_xattn_in['ff_b1'], 'L0_xattn_ff_w2': _L0_xattn_in['ff_w2'], 'L0_xattn_ff_b2': _L0_xattn_in['ff_b2'], 'L0_xattn_norm_out_w': _L0_xattn_in['norm_out_w'], 'L0_xattn_proj_w': _L0_xattn_in['proj_w'], 'L0_xattn_proj_b': _L0_xattn_in['proj_b'], 'L0_attn_Wq': _L0_attn_in['Wq'], 'L0_attn_Wk': _L0_attn_in['Wk'], 'L0_attn_Wv': _L0_attn_in['Wv'], 'L0_attn_Wo': _L0_attn_in['Wo'], 'L0_ffn_wq': _L0_ffn_in['wq'], 'L0_ffn_bq': _L0_ffn_in['bq'], 'L0_ffn_wk': _L0_ffn_in['wk'], 'L0_ffn_bk': _L0_ffn_in['bk'], 'L0_ffn_wv': _L0_ffn_in['wv'], 'L0_ffn_bv': _L0_ffn_in['bv'], 'L0_ffn_wo': _L0_ffn_in['wo'], 'L0_ffn_bo': _L0_ffn_in['bo'], 'L0_ffn_ln1_g': _L0_ffn_in['ln1_g'], 'L0_ffn_ln1_b': _L0_ffn_in['ln1_b'], 'L0_ffn_ln2_g': _L0_ffn_in['ln2_g'], 'L0_ffn_ln2_b': _L0_ffn_in['ln2_b'], 'L0_ffn_wr': _L0_ffn_in['wr'], 'L0_ffn_w1': _L0_ffn_in['w1'], 'L0_ffn_b1': _L0_ffn_in['b1'], 'L0_ffn_w2': _L0_ffn_in['w2'], 'L0_ffn_b2': _L0_ffn_in['b2']}

def reference(x, ctx_1024, mask_BxS_bf1, L0_xattn_attn_norm_w, L0_xattn_Wq, L0_xattn_Wk, L0_xattn_Wv, L0_xattn_Wo, L0_xattn_bo, L0_xattn_cross_norm_w, L0_xattn_cWq, L0_xattn_cWk, L0_xattn_cWv, L0_xattn_cWo, L0_xattn_cbo, L0_xattn_ff_norm_w, L0_xattn_ff_w1, L0_xattn_ff_b1, L0_xattn_ff_w2, L0_xattn_ff_b2, L0_xattn_norm_out_w, L0_xattn_proj_w, L0_xattn_proj_b, L0_attn_Wq, L0_attn_Wk, L0_attn_Wv, L0_attn_Wo, L0_ffn_wq, L0_ffn_bq, L0_ffn_wk, L0_ffn_bk, L0_ffn_wv, L0_ffn_bv, L0_ffn_wo, L0_ffn_bo, L0_ffn_ln1_g, L0_ffn_ln1_b, L0_ffn_ln2_g, L0_ffn_ln2_b, L0_ffn_wr, L0_ffn_w1, L0_ffn_b1, L0_ffn_w2, L0_ffn_b2):
    import jax
    import jax.numpy as jnp

    def _L0_xattn_ref(x, chunked_seq, mask, attn_norm_w, Wq, Wk, Wv, Wo, bo, cross_norm_w, cWq, cWk, cWv, cWo, cbo, ff_norm_w, ff_w1, ff_b1, ff_w2, ff_b2, norm_out_w, proj_w, proj_b):
        import jax, jax.numpy as jnp
        import numpy as np
        L = 2
        D = 128
        HS = 128
        NH = 16
        DH = 64
        FF = 512
        ROT = 32
        B, SQ, SK = (64, 128, 64)
        EPS = 1e-08

        def rmsnorm(x, w):
            norm = jnp.sqrt(jnp.sum(x * x, axis=-1, keepdims=True)) * x.shape[-1] ** (-0.5)
            return x / jnp.maximum(norm, EPS) * w

        def rope_freqs(n):
            inv_freq = 1.0 / 10000.0 ** (jnp.arange(0, ROT, 2, dtype=jnp.float32) / ROT)
            f = jnp.arange(n, dtype=jnp.float32)[:, None] * inv_freq[None, :]
            return jnp.concatenate([f, f], axis=-1)[None, None]

        def apply_rope(t, freqs):
            rd = freqs.shape[-1]
            t1, tp = (t[..., :rd], t[..., rd:])
            half = rd // 2
            a, b = (t1[..., :half], t1[..., half:])
            rot = jnp.concatenate([-b, a], axis=-1)
            t1 = t1 * jnp.cos(freqs) + rot * jnp.sin(freqs)
            return jnp.concatenate([t1, tp], axis=-1)

        def attention(x, ctx, Wq, Wk, Wv, Wo, bo, pe_q, pe_k, mask):
            b, n, _ = x.shape
            m = ctx.shape[1]
            q = (x @ Wq).reshape(b, n, NH, DH).transpose(0, 2, 1, 3) * DH ** (-0.5)
            k = (ctx @ Wk).reshape(b, m, NH, DH).transpose(0, 2, 1, 3)
            v = (ctx @ Wv).reshape(b, m, NH, DH).transpose(0, 2, 1, 3)
            q = apply_rope(q, pe_q)
            k = apply_rope(k, pe_k)
            sim = jnp.einsum('bhid,bhjd->bhij', q, k)
            if mask is not None:
                sim = jnp.where(mask[:, None, None, :], sim, -jnp.finfo(sim.dtype).max)
            attn = jax.nn.softmax(sim, axis=-1)
            out = jnp.einsum('bhij,bhjd->bhid', attn, v)
            out = out.transpose(0, 2, 1, 3).reshape(b, n, NH * DH)
            return out @ Wo + bo
        pe_q = rope_freqs(x.shape[-2])
        pe_k = rope_freqs(chunked_seq.shape[-2])
        for l in range(L):
            h = rmsnorm(x, attn_norm_w[l])
            x = attention(h, h, Wq[l], Wk[l], Wv[l], Wo[l], bo[l], pe_q, pe_q, mask) + x
            h = rmsnorm(x, cross_norm_w[l])
            x = attention(h, chunked_seq, cWq[l], cWk[l], cWv[l], cWo[l], cbo[l], pe_q, pe_k, None) + x
            h = rmsnorm(x, ff_norm_w[l])
            x = jax.nn.gelu(h @ ff_w1[l] + ff_b1[l], approximate=False) @ ff_w2[l] + ff_b2[l] + x
        x = rmsnorm(x, norm_out_w)
        return x @ proj_w + proj_b

    def _L0_attn_ref(hidden_states, Wq, Wk, Wv, Wo):
        import jax, jax.numpy as jnp
        import numpy as np
        H_DIM = 128
        N_HEADS = 16
        HEAD_DIM = H_DIM // N_HEADS
        MAX_POS = 256
        BASE = 10000.0
        SCALING_FACTOR = 1.0

        def rotate_half(x):
            return jnp.concatenate([-x[..., 1::2], x[..., ::2]], axis=-1)

        def rope_cos_sin(seq_len, dtype):
            base = BASE
            if seq_len > MAX_POS:
                base = BASE * (SCALING_FACTOR * seq_len / MAX_POS - (SCALING_FACTOR - 1.0)) ** (HEAD_DIM / (HEAD_DIM - 2))
            inv_freq = 1.0 / base ** (jnp.arange(0, HEAD_DIM, 2, dtype=jnp.float32) / HEAD_DIM)
            t = jnp.arange(seq_len, dtype=jnp.float32)
            freqs = jnp.einsum('i,j->ij', t, inv_freq)
            emb = jnp.concatenate([freqs, freqs], axis=-1)
            return (emb.astype(dtype), jnp.cos(emb).astype(dtype), jnp.sin(emb).astype(dtype))
        B, S, H = hidden_states.shape

        def proj(x, W):
            y = jnp.einsum('bsh,oh->bso', x, W)
            return y.reshape(B, S, N_HEADS, HEAD_DIM).transpose(0, 2, 1, 3)
        q = proj(hidden_states, Wq)
        k = proj(hidden_states, Wk)
        v = proj(hidden_states, Wv)
        _, cos, sin = rope_cos_sin(S, hidden_states.dtype)
        cos = cos[None, None, :, :]
        sin = sin[None, None, :, :]
        q = q * cos + rotate_half(q) * sin
        k = k * cos + rotate_half(k) * sin
        scale = HEAD_DIM ** (-0.5)
        attn = jnp.einsum('bhsd,bhtd->bhst', q, k) / scale
        attn = jax.nn.softmax(attn, axis=-1)
        out = jnp.einsum('bhst,bhtd->bhsd', attn, v)
        out = out.transpose(0, 2, 1, 3).reshape(B, S, H)
        return jnp.einsum('bsh,oh->bso', out, Wo)

    def _L0_ffn_ref(x, wq, bq, wk, bk, wv, bv, wo, bo, ln1_g, ln1_b, ln2_g, ln2_b, wr, w1, b1, w2, b2):
        import jax, jax.numpy as jnp
        import numpy as np
        D_MODEL = 128
        N_HEADS = 16
        HEAD_DIM = D_MODEL // N_HEADS
        FFN_DIM = 512
        N_EXPERTS = 8
        CAP_FRAC = 0.25
        MOE_TOKEN_DROPOUT = 0.2
        LN_EPS = 1e-05
        B, S = (4, 64)

        def _layer_norm(x, g, b):
            mu = x.mean(-1, keepdims=True)
            var = ((x - mu) ** 2).mean(-1, keepdims=True)
            return (x - mu) * jax.lax.rsqrt(var + LN_EPS) * g + b

        def _self_attention(x, wq, bq, wk, bk, wv, bv, wo, bo):
            b, s, d = x.shape
            q = ((x @ wq + bq) * HEAD_DIM ** (-0.5)).reshape(b, s, N_HEADS, HEAD_DIM)
            k = (x @ wk + bk).reshape(b, s, N_HEADS, HEAD_DIM)
            v = (x @ wv + bv).reshape(b, s, N_HEADS, HEAD_DIM)
            scores = jnp.einsum('bqhd,bkhd->bhqk', q, k)
            p = jax.nn.softmax(scores, axis=-1)
            o = jnp.einsum('bhqk,bkhd->bqhd', p, v).reshape(b, s, d)
            return o @ wo + bo

        def _moe_ffn(x, wr, w1, b1, w2, b2):
            T, D = x.shape
            C = int(np.ceil(CAP_FRAC * T))
            logits = x @ wr
            probs = jax.nn.softmax(logits, axis=-1)
            top1 = jnp.argmax(probs, axis=-1)
            m1 = jax.nn.one_hot(top1, N_EXPERTS, dtype=x.dtype)
            top2 = jnp.argmax(jnp.where(m1 > 0, -jnp.inf, logits), axis=-1)
            m2 = jax.nn.one_hot(top2, N_EXPERTS, dtype=x.dtype)
            loc1 = jnp.cumsum(m1, axis=0) - 1.0
            loc2 = jnp.cumsum(m2, axis=0) - 1.0 + m1.sum(0, keepdims=True)
            m1 = m1 * (loc1 < C)
            m2 = m2 * (loc2 < C)
            t1 = (probs * m1).sum(-1)
            t2 = (probs * m2).sum(-1)
            denom = jnp.maximum(t1 + t2, jnp.finfo(x.dtype).eps)
            t1, t2 = (t1 / denom, t2 / denom)
            tok = jnp.arange(T)
            s1 = loc1[tok, top1].astype(jnp.int32)
            s2 = loc2[tok, top2].astype(jnp.int32)
            v1 = m1[tok, top1] > 0
            v2 = m2[tok, top2] > 0
            s1 = jnp.where(v1, s1, C)
            s2 = jnp.where(v2, s2, C)
            buf = jnp.zeros((N_EXPERTS, C, D), x.dtype)
            buf = buf.at[top1, s1].set(x, mode='drop')
            buf = buf.at[top2, s2].set(x, mode='drop')
            h = jax.nn.relu(jnp.einsum('ecd,edf->ecf', buf, w1) + b1[:, None, :])
            y = (jnp.einsum('ecf,efd->ecd', h, w2) + b2[:, None, :]) * (1.0 - MOE_TOKEN_DROPOUT)
            y1 = y[top1, jnp.minimum(s1, C - 1)]
            y2 = y[top2, jnp.minimum(s2, C - 1)]
            g1 = t1 * v1
            g2 = t2 * v2
            return g1[:, None] * y1 + g2[:, None] * y2
        h = _layer_norm(x, ln1_g, ln1_b)
        h = _self_attention(h, wq, bq, wk, bk, wv, bv, wo, bo)
        x = x + h
        h = _layer_norm(x, ln2_g, ln2_b)
        b, s, d = h.shape
        moe = _moe_ffn(h.reshape(b * s, d), wr, w1, b1, w2, b2).reshape(b, s, d)
        return x + moe
    x = x + _L0_xattn_ref(_layernorm(x, axis=-1), ctx_1024, mask_BxS_bf1, L0_xattn_attn_norm_w, L0_xattn_Wq, L0_xattn_Wk, L0_xattn_Wv, L0_xattn_Wo, L0_xattn_bo, L0_xattn_cross_norm_w, L0_xattn_cWq, L0_xattn_cWk, L0_xattn_cWv, L0_xattn_cWo, L0_xattn_cbo, L0_xattn_ff_norm_w, L0_xattn_ff_w1, L0_xattn_ff_b1, L0_xattn_ff_w2, L0_xattn_ff_b2, L0_xattn_norm_out_w, L0_xattn_proj_w, L0_xattn_proj_b)
    x = x + _L0_attn_ref(_layernorm(x, axis=-1), L0_attn_Wq, L0_attn_Wk, L0_attn_Wv, L0_attn_Wo)
    x = x + _L0_ffn_ref(_layernorm(x, axis=-1), L0_ffn_wq, L0_ffn_bq, L0_ffn_wk, L0_ffn_bk, L0_ffn_wv, L0_ffn_bv, L0_ffn_wo, L0_ffn_bo, L0_ffn_ln1_g, L0_ffn_ln1_b, L0_ffn_ln2_g, L0_ffn_ln2_b, L0_ffn_wr, L0_ffn_w1, L0_ffn_b1, L0_ffn_w2, L0_ffn_b2)
    return x

_drawn_inputs = setup_inputs


def setup_inputs(seed=0):
    import zlib

    import numpy as np

    out = dict(_drawn_inputs(seed))
    spreads = {'L0_xattn_attn_norm_w': (1.0, 0.6),
     'L0_xattn_bo': (0.0, 0.268),
     'L0_xattn_cross_norm_w': (1.0, 0.6),
     'L0_xattn_cbo': (0.0, 0.1),
     'L0_xattn_ff_norm_w': (1.0, 0.6),
     'L0_xattn_ff_b1': (0.0, 0.8),
     'L0_xattn_ff_b2': (0.0, 0.1),
     'L0_xattn_norm_out_w': (1.0, 0.2),
     'L0_xattn_proj_b': (0.0, 0.1)}
    factors = {'ctx_1024': 2.809,
     'L0_xattn_Wq': 8.0,
     'L0_xattn_Wk': 8.0,
     'L0_xattn_Wv': 5.184,
     'L0_xattn_Wo': 5.278,
     'L0_xattn_cWq': 8.0,
     'L0_xattn_cWk': 8.0,
     'L0_xattn_ff_w1': 3.296,
     'L0_xattn_ff_w2': 3.04,
     'L0_attn_Wq': 8.0,
     'L0_attn_Wk': 8.0,
     'L0_attn_Wv': 4.867,
     'L0_attn_Wo': 4.97,
     'L0_ffn_wq': 8.0,
     'L0_ffn_bq': 8.0,
     'L0_ffn_wk': 8.0,
     'L0_ffn_bk': 200.0,
     'L0_ffn_wv': 8.0,
     'L0_ffn_bv': 32.6,
     'L0_ffn_wo': 8.0,
     'L0_ffn_bo': 41.848,
     'L0_ffn_ln1_g': 8.0,
     'L0_ffn_ln1_b': 8.0,
     'L0_ffn_ln2_g': 64.0,
     'L0_ffn_ln2_b': 64.0,
     'L0_ffn_wr': 2.854,
     'L0_ffn_w1': 3.203,
     'L0_ffn_b1': 200.0,
     'L0_ffn_b2': 64.0}
    for name, (base, spread) in spreads.items():
        noise = np.random.default_rng([zlib.crc32(name.encode()), seed]).standard_normal(out[name].shape)
        drawn = base * np.exp(spread * noise) if base else spread * noise
        out[name] = jnp.asarray(drawn.astype(out[name].dtype))
    for name, factor in factors.items():
        out[name] = (out[name] * factor).astype(out[name].dtype)
    return out
```

```python
from contextlib import ExitStack, contextmanager

import numpy as np
import concourse.bass as bass
from concourse import mybir

F32 = mybir.dt.float32
U8 = mybir.dt.uint8
ALU = mybir.AluOpType
ACT = mybir.ActivationFunctionType
AX = mybir.AxisListType

P = 128
B, S, D = 128, 32, 128
BT = P // S
NT = B // BT
LAYERS = 2
NH, DH, ROT = 16, 64, 32
NG = 4
HG = NH // NG
SK = 257
FF = 512
FC = FF // P
NE, CAP = 8, 1024
HD8 = 8
BIG = float(np.finfo(np.float32).max)
SWAP_HALVES = [(i + 16) % 32 for i in range(32)]
SWAP_PAIRS = [8 * (i // 8) + (2 * (i % 8) + 1 if i % 8 < 4 else 2 * (i % 8 - 4)) for i in range(32)]


class Steps:

    def __init__(self, eng, sem, base):
        self.eng, self.sem, self.base, self.n = eng, sem, base, 0

    def go(self, ins):
        self.n += 1
        ins.then_inc(self.sem, 1)

    def __call__(self, ins):
        self.go(ins)
        self.eng.wait_ge(self.sem, self.base + self.n)


class Core:

    def __init__(self, nc, dram, stack):
        self.nc, self.dram, self.stack = nc, dram, stack
        self.PS = stack.enter_context(nc.psum_tensor("PS", [P, 8, 512], F32))
        self.X = self.buffer(stack, "X", [P, NT, D])
        self.ident = self.buffer(stack, "ident", [P, P])
        self.moments = self.buffer(stack, "moments", [P, NT, 6])
        self.mean_var = self.buffer(stack, "mean_var", [P, NT, 1])
        self.root = self.buffer(stack, "root", [P, NT])
        self.rstd = self.buffer(stack, "rstd", [P, NT, 1])
        self.x_tiles = dram["x"].rearrange("(t b) s d -> (b s) t d", b=BT)

    def sem(self, name):
        self.sems.append(self.nc.alloc_semaphore(name=name))
        return self.sems[-1]

    def clear_sems(self):
        for sem in self.sems:
            self.nc.gpsimd.sem_clear(sem)
        self.nc.all_engine_barrier()

    @contextmanager
    def stage(self):
        self.sems = []
        with ExitStack() as st:
            yield st
        self.nc.clear_and_free_semaphores(self.sems)
        self.nc.all_engine_barrier()

    def buffer(self, stack, name, shape, dt=F32):
        return stack.enter_context(self.nc.sbuf_tensor(name, shape, dt))


class Statistics:

    def __init__(self, core, name):
        self.core = core
        self.moments_done, self.steps = core.sem(name + "_moments_done"), core.sem(name + "_steps")
        self.square_ready, self.root_ready = core.sem(name + "_square_ready"), core.sem(name + "_root_ready")

    def run(self, src, rms):
        nc, c = self.core.nc, self.core
        with nc.Block() as block:
            @block.vector
            def _(dve):
                with dve.Fori(0, NT) as t:
                    nc.vector.bn_stats(c.moments[:, t, :], src[:, t, :]).then_inc(self.moments_done, 1)
                dve.wait_ge(self.moments_done, NT)
                mean0, m2_0, mean1, m2_1 = (c.moments[:, :, i] for i in (1, 2, 4, 5))
                mean = c.mean_var[:, :, 0]
                step = Steps(dve, self.steps, 0)
                step(nc.vector.tensor_tensor(mean, mean0, mean1, ALU.add))
                step(nc.vector.tensor_scalar(mean, mean, 0.5, None, ALU.mult))
                step(nc.vector.tensor_tensor(mean0, mean0, mean1, ALU.subtract))
                step(nc.vector.scalar_tensor_tensor(mean0, mean0, 0.25, mean0, ALU.mult, ALU.mult))
                step(nc.vector.tensor_tensor(m2_0, m2_0, m2_1, ALU.add))
                step(nc.vector.scalar_tensor_tensor(c.root[:], m2_0, 1.0 / D, mean0, ALU.mult, ALU.add))
                if rms:
                    step(nc.vector.tensor_tensor(mean, mean, mean, ALU.mult))
                    nc.vector.tensor_tensor(c.root[:], c.root[:], mean, ALU.add).then_inc(self.square_ready, 1)
                else:
                    nc.vector.tensor_scalar(c.root[:], c.root[:], 1e-5, None, ALU.add).then_inc(self.square_ready, 1)
                dve.wait_ge(self.root_ready, 1)
                if rms:
                    step(nc.vector.tensor_scalar(c.root[:], c.root[:], 1e-8, None, ALU.max))
                step(nc.vector.reciprocal(c.rstd[:, :, 0], c.root[:]))

            @block.scalar
            def _(act):
                act.wait_ge(self.square_ready, 1)
                nc.scalar.activation(c.root[:], c.root[:], ACT.Sqrt).then_inc(self.root_ready, 1)


def build(nc, dram):
    with ExitStack() as top:
        core = Core(nc, dram, top)
        with core.stage():
            loaded = core.sem("start_loaded")
            with nc.Block() as block:
                @block.sync
                def _(sp):
                    sp.dma_start(core.X[:], core.x_tiles).then_inc(loaded, 16)
                    sp.dma_start(core.ident[:], dram["ident"]).then_inc(loaded, 16)
                    sp.wait_ge(loaded, 32)

            Statistics(core, "ln_x").run(core.X, False)
            normalise(core, core.X, core.X, "x_normed")
        with core.stage() as st:
            perceiver(core, st)
        HB = core.buffer(top, "HB", [P, NT, D])
        with core.stage() as st:
            project(core, st, HB)
        with core.stage() as st:
            small = SmallAttention(core, st)
            Statistics(core, "ln_b").run(core.X, False)
            small.run(core.X, rotary=True)
            Statistics(core, "ln_c").run(core.X, False)
            normalise(core, HB, core.X, "c_normed")
            Statistics(core, "ln_c1").run(HB, False)
            small.run(HB, rotary=False)
        with core.stage() as st:
            Statistics(core, "ln_c2").run(HB, False)
            experts(core, st, HB)


def normalise(core, dst, src, name):
    nc, done = core.nc, core.sem(name)
    with nc.Block() as block:
        @block.vector
        def _(dve):
            with dve.Fori(0, NT) as t:
                nc.vector.tensor_scalar(dst[:, t, :], src[:, t, :], core.mean_var[:, t, 0:1],
                                        core.rstd[:, t, :], ALU.subtract, ALU.mult).then_inc(done, 1)
            dve.wait_ge(done, NT)


def heads(width, g):
    per = P // width
    first = g % per + 4 * per * (g // per)
    return range(first, first + 4 * per, per)


def perceiver(core, st):
    nc, dram = core.nc, core.dram
    def buf(name, shape, dt=F32):
        return core.buffer(st, name, shape, dt)

    tables = {n: buf(n, [P, SK if n[-1] == "k" else S]) for n in ("cos_k", "sin_k", "cos_q", "sin_q")}
    mask_bytes = buf("mask_bytes", [P, NT, BT * S], U8)
    last_rows_T = buf("last_rows_T", [P, NT, BT])
    W = {n: buf("w_" + n, [P, NH * ROT]) for n in ("sqR", "skR", "sqN", "skN", "cqR", "ckR")}
    VO = {a: buf("VO_" + a, [P, NH, D]) for a in "sc"}
    QK = buf("QK", [P, NH, D])
    W1, W2 = buf("W1", [P, FF]), buf("W2", [P, FC, D])
    b1 = buf("b1", [P, FC])
    rows = {n: buf("row_" + n, [P, D]) for n in ("sw", "cw", "fw", "sbo", "cbo", "fb2")}

    tables_loaded, last_turned, last_kept = (core.sem(n) for n in ("tables_loaded", "last_turned", "last_kept"))
    with ExitStack() as tmp, nc.Block() as block:
        last_rows = core.buffer(tmp, "last_rows", [B, D])

        @block.sync
        def _(sp):
            for n in tables:
                sp.dma_start(tables[n][:], dram[n]).then_inc(tables_loaded, 16)
            sp.dma_start(mask_bytes[:], dram["mask"].partition_broadcast(P)).then_inc(tables_loaded, 16)
            sp.dma_start(last_rows[:], dram["ctx"][:, SK - 1, :]).then_inc(tables_loaded, 16)

        @block.tensor
        def _(pe):
            pe.wait_ge(tables_loaded, 96)
            nc.tensor.transpose(core.PS[:, 0, 0:B], last_rows[:], core.ident[:]).then_inc(last_turned, 1)

        @block.vector
        def _(dve):
            dve.wait_ge(last_turned, 1)
            nc.vector.tensor_copy(last_rows_T[:], core.PS[:, 0, 0:B]).then_inc(last_kept, 1)
            dve.wait_ge(last_kept, 1)

    loaded, product_ready, product_kept = (core.sem(n) for n in
                                           ("weights_loaded", "product_ready", "product_kept"))
    stats = [Statistics(core, n) for n in ("rms_self", "rms_cross", "rms_ffn")]
    self_attention, cross_attention, feed_forward = SelfAttention(core), CrossAttention(core), FeedForward(core)

    with nc.Fori(0, LAYERS) as l:
        with ExitStack() as tmp:
            WvT = {a: core.buffer(tmp, "WvT_" + a, [P, NH // 2, D]) for a in "sc"}
            Wo = {a: core.buffer(tmp, "Wo_" + a, [P, NH // 2, D]) for a in "sc"}
            WqNT, WkNT = core.buffer(tmp, "WqNT", [P, NG, D]), core.buffer(tmp, "WkNT", [P, NG, D])
            chunks = lambda a: a.rearrange("(c p) d -> p c d", p=P)
            loads = [(W[n][:], dram[n][l]) for n in W]
            loads += [(WvT[a][:], chunks(dram[a + "WvT"][l])) for a in "sc"]
            loads += [(Wo[a][:], chunks(dram[a + "Wo"][l])) for a in "sc"]
            loads += [(WqNT[:], chunks(dram["cqNT"][l])), (WkNT[:], chunks(dram["ckNT"][l])),
                      (W1[:], dram["w1"][l]), (W2[:], chunks(dram["w2"][l])), (b1[:], dram["b1T"][l])]
            loads += [(rows[n][:], dram["row_" + n][l].partition_broadcast(P)) for n in rows]
            total = 16 * len(loads)
            products = [(VO["s"], WvT["s"], Wo["s"], DH), (VO["c"], WvT["c"], Wo["c"], DH),
                        (QK, WqNT, WkNT, ROT)]
            turns = [(p, g) for p in products for g in range(NG)]

            with nc.Block() as block:
                @block.sync
                def _(sp):
                    for dst, src in loads:
                        sp.dma_start(dst, src).then_inc(loaded, 16)
                    sp.wait_ge(loaded, total)

                @block.tensor
                def _(pe):
                    pe.wait_ge(loaded, total)
                    for k, ((_, left, right, width), g) in enumerate(turns):
                        if k >= 8:
                            pe.wait_ge(product_kept, k - 7)
                        for h, head in enumerate(heads(width, g)):
                            chunk, r = divmod(head * width, P)
                            ins = nc.tensor.matmul(core.PS[:, k % 8, h * D:(h + 1) * D],
                                                   left[r:r + width, chunk, :], right[r:r + width, chunk, :],
                                                   start=True, stop=True)
                        ins.then_inc(product_ready, 1)

                @block.vector
                def _(dve):
                    for k, ((dst, _, _, width), g) in enumerate(turns):
                        dve.wait_ge(product_ready, k + 1)
                        of = heads(width, g)
                        nc.vector.tensor_copy(dst[:, of.start:of[-1] + 1:of.step, :],
                                              core.PS[:, k % 8, :].rearrange("p (h d) -> p h d", h=HG)).then_inc(product_kept, 1)
                    dve.wait_ge(product_kept, len(turns))

        stats[0].run(core.X, True)
        self_attention.run(W, VO["s"], rows["sw"], rows["sbo"], tables, mask_bytes)
        stats[1].run(core.X, True)
        cross_attention.run(W, VO["c"], QK, rows["cw"], rows["cbo"], tables, last_rows_T)
        stats[2].run(core.X, True)
        feed_forward.run(W1, W2, b1, rows["fw"], rows["fb2"])
        core.clear_sems()


class Rope:

    def __init__(self, nc, step, raw, keep, cos, sin, out, swap):
        self.nc, self.step, self.raw, self.keep, self.cos, self.sin, self.out, self.swap = (
            nc, step, raw, keep, cos, sin, out, swap)

    def first(self):
        self.step.go(self.nc.vector.tensor_tensor(self.keep, self.raw, self.cos, ALU.mult))
        self.step(self.nc.vector.stream_shuffle(self.raw, self.raw, self.swap))

    def second(self):
        self.step(self.nc.vector.tensor_tensor(self.raw, self.raw, self.sin, ALU.mult))
        return self.nc.vector.tensor_tensor(self.out, self.raw, self.keep, ALU.add)


class SelfAttention:
    def __init__(self, core):
        self.core = core
        names = ("h_ready", "hT_ready", "hT_kept", "rot_ready", "plain_ready", "q_turned", "k_turned",
                  "q_rot_spread", "q_plain_spread", "k_plain_kept", "mask_ready", "scores_ready", "shifted",
                  "exp_done", "probs_ready", "pT_ready", "pT_kept", "uT_ready", "uT_kept_act", "uT_kept_dve",
                  "out_ready", "dve_steps", "pool_steps", "zeroed", "held")
        self.sems = {n: core.sem("self_" + n) for n in names}

    def run(self, W, VO, norm_row, bias_row, tables, mask_bytes):
        core, nc, PS, X, s = self.core, self.core.nc, self.core.PS, self.core.X, self.sems
        with ExitStack() as st:
            def buf(name, shape):
                return core.buffer(st, "self_" + name, shape)

            H, HT = buf("H", [P, D]), buf("HT", [P, P])
            keep = buf("keep", [P, NG, P])
            QR, KR, KN = buf("QR", [P, NG, P]), buf("KR", [P, NG, P]), buf("KN", [P, NG, P])
            QRd, QNd = buf("QRd", [P, NG, BT, HG, S]), buf("QNd", [P, NG, BT, HG, S])
            allow, forbid = buf("allow", [P, 1, P]), buf("forbid", [P, 1, P])
            top, total, inverse = buf("top", [P, NG * BT]), buf("total", [P, NG * BT]), buf("inverse", [P, NG * BT])
            PR, PT = buf("PR", [P, NG, P]), buf("PT", [P, NG, P])
            UT = buf("UT", [P, NH, BT, S])
            STEPS = 13
            SC = PS[:, 5, :]
            SC3 = SC.rearrange("p (g n) -> p g n", g=NG)
            SCj = SC.rearrange("p (m j) -> p m j", j=S)

            def per_row(v):
                return v[:].unsqueeze(2).to_broadcast([P, NG * BT, S])

            with nc.Block() as block:
                @block.gpsimd
                def _(pool):
                    nc.gpsimd.memset(QRd[:], 0.0).then_inc(s["zeroed"], 1)
                    nc.gpsimd.memset(QNd[:], 0.0).then_inc(s["zeroed"], 1)
                    with pool.Fori(0, NT) as t:
                        n = t
                        pool.wait_ge(s["h_ready"], n + 1)
                        nc.gpsimd.tensor_copy(allow[:, 0, :], mask_bytes[:, t, :]).then_inc(s["pool_steps"], 1)
                        pool.wait_ge(s["pool_steps"], n + 1)
                        pool.sem_inc(s["held"], 1)
                        nc.gpsimd.tensor_scalar(forbid[:], allow[:], -1.0, BIG, ALU.add,
                                                ALU.mult).then_inc(s["mask_ready"], 1)

                @block.vector
                def _(dve):
                    with dve.Fori(0, NT) as t:
                        n = t
                        step = Steps(dve, s["dve_steps"], n * STEPS)
                        nc.vector.scalar_tensor_tensor(H[:], X[:, t, :], core.rstd[:, t, :], norm_row[:],
                                                       ALU.mult, ALU.mult).then_inc(s["h_ready"], 1)
                        for k, (out, done, c, i) in enumerate(((QR, s["q_turned"], "cos_q", "sin_q"),
                                                               (KR, s["k_turned"], "cos_k", "sin_k"))):
                            dve.wait_ge(s["rot_ready"], 2 * n + k + 1)
                            if k == 1:
                                dve.wait_ge(s["q_turned"], n + 1)
                            view = lambda a: a.rearrange("p (m i) -> p m i", i=S)
                            bc = lambda a: tables[a][:, 0:S].unsqueeze(1).to_broadcast([P, NG * BT, S])
                            rope = Rope(nc, step, view(PS[:, 1 + k, :]), view(keep[:].rearrange("p g n -> p (g n)")),
                                        bc(c), bc(i), view(out[:].rearrange("p g n -> p (g n)")), SWAP_HALVES)
                            rope.first()
                            rope.second().then_inc(done, 1)
                        dve.wait_ge(s["scores_ready"], n + 1)
                        dve.wait_ge(s["mask_ready"], n + 1)
                        step(nc.vector.tensor_tensor(SC3, SC3, allow[:].to_broadcast([P, NG, P]), ALU.mult))
                        step(nc.vector.tensor_tensor(SC3, SC3, forbid[:].to_broadcast([P, NG, P]), ALU.add))
                        step(nc.vector.tensor_reduce(top[:], SCj, AX.X, ALU.max))
                        nc.vector.tensor_tensor(SCj, SCj, per_row(top), ALU.subtract).then_inc(s["shifted"], 1)
                        dve.wait_ge(s["exp_done"], n + 1)
                        step(nc.vector.tensor_reduce(total[:], SCj, AX.X, ALU.add))
                        step(nc.vector.reciprocal(inverse[:], total[:]))
                        nc.vector.tensor_tensor(PR[:].rearrange("p g (b j) -> p (g b) j", j=S), SCj,
                                                per_row(inverse), ALU.mult).then_inc(s["probs_ready"], 1)
                        for k, b in enumerate((1, 3)):
                            dve.wait_ge(s["uT_ready"], 4 * n + b + 1)
                            nc.vector.tensor_copy(UT[:, :, b, :], PS[:, 1 + b, :].rearrange("p (h i) -> p h i", i=S))\
                              .then_inc(s["uT_kept_dve"], 1)
                        dve.wait_ge(s["out_ready"], n + 1)
                        step(nc.vector.tensor_tensor(X[:, t, :], X[:, t, :], PS[:, 7, 0:D], ALU.add))
                        step(nc.vector.tensor_tensor(X[:, t, :], X[:, t, :], bias_row[:], ALU.add))
                        assert step.n == STEPS

                @block.scalar
                def _(act):
                    act.wait_ge(s["zeroed"], 2)
                    with act.Fori(0, NT) as t:
                        n = t
                        act.wait_ge(s["hT_ready"], n + 1)
                        nc.scalar.activation(HT[:], PS[:, 0, 0:P], ACT.Copy).then_inc(s["hT_kept"], 1)
                        act.wait_ge(s["plain_ready"], 2 * n + 1)
                        for h in range(HG):
                            r = slice(32 * h, 32 * h + 32)
                            nc.scalar.activation(QNd[r, :, :, h, :], PS[r, 3, :].rearrange(
                                "p (g b i) -> p g b i", g=NG, b=BT), ACT.Copy, scale=DH ** -0.5)\
                              .then_inc(s["q_plain_spread"], 1)
                        act.wait_ge(s["plain_ready"], 2 * n + 2)
                        nc.scalar.activation(KN[:].rearrange("p g n -> p (g n)"), PS[:, 4, :],
                                             ACT.Copy).then_inc(s["k_plain_kept"], 1)
                        act.wait_ge(s["q_turned"], n + 1)
                        for h in range(HG):
                            r = slice(32 * h, 32 * h + 32)
                            nc.scalar.activation(QRd[r, :, :, h, :], QR[r].rearrange(
                                "p g (b i) -> p g b i", b=BT), ACT.Copy).then_inc(s["q_rot_spread"], 1)
                        act.wait_ge(s["shifted"], n + 1)
                        nc.scalar.activation(SC, SC, ACT.Exp).then_inc(s["exp_done"], 1)
                        act.wait_ge(s["pT_ready"], n + 1)
                        nc.scalar.activation(PT[:].rearrange("p g n -> p (g n)"), PS[:, 6, :],
                                             ACT.Copy).then_inc(s["pT_kept"], 1)
                        for b in (0, 2):
                            act.wait_ge(s["uT_ready"], 4 * n + b + 1)
                            nc.scalar.activation(UT[:, :, b, :], PS[:, 1 + b, :].rearrange("p (h i) -> p h i", i=S),
                                                 ACT.Copy).then_inc(s["uT_kept_act"], 1)

                @block.tensor
                def _(pe):
                    pe.wait_ge(s["zeroed"], 2)
                    with pe.Fori(0, NT) as t:
                        n = t
                        pe.wait_ge(s["h_ready"], n + 1)
                        nc.tensor.transpose(PS[:, 0, 0:P], H[:], core.ident[:]).then_inc(s["hT_ready"], 1)
                        pe.wait_ge(s["hT_kept"], n + 1)
                        for i, (w, done) in enumerate((("sqR", s["rot_ready"]), ("skR", s["rot_ready"]),
                                                       ("sqN", s["plain_ready"]), ("skN", s["plain_ready"]))):
                            for g in range(NG):
                                ins = nc.tensor.matmul(PS[:, 1 + i, g * P:(g + 1) * P], W[w][:, g * P:(g + 1) * P],
                                                       HT[:], start=True, stop=True)
                            ins.then_inc(done, 1)
                        pe.wait_ge(s["q_plain_spread"], 4 * n + 4)
                        pe.wait_ge(s["k_plain_kept"], n + 1)
                        pe.wait_ge(s["q_rot_spread"], 4 * n + 4)
                        pe.wait_ge(s["k_turned"], n + 1)
                        for g in range(NG):
                            for b in range(BT):
                                out = PS[:, 5, g * P + b * S:g * P + (b + 1) * S]
                                nc.tensor.matmul(out, QNd[:, g, b].rearrange("p h i -> p (h i)"),
                                                 KN[:, g, b * S:(b + 1) * S], start=True, stop=False)
                                ins = nc.tensor.matmul(out, QRd[:, g, b].rearrange("p h i -> p (h i)"),
                                                       KR[:, g, b * S:(b + 1) * S], start=False, stop=True)
                        ins.then_inc(s["scores_ready"], 1)
                        pe.wait_ge(s["probs_ready"], n + 1)
                        for g in range(NG):
                            ins = nc.tensor.transpose(PS[:, 6, g * P:(g + 1) * P], PR[:, g, :], core.ident[:])
                        ins.then_inc(s["pT_ready"], 1)
                        pe.wait_ge(s["pT_kept"], n + 1)
                        for b in range(BT):
                            r = slice(b * S, (b + 1) * S)
                            nc.tensor.matmul(PS[:, 1 + b, :], H[r, :], PT[r].rearrange("p g n -> p (g n)"),
                                             start=True, stop=True).then_inc(s["uT_ready"], 1)
                        pe.wait_ge(s["uT_kept_act"], 2 * n + 2)
                        pe.wait_ge(s["uT_kept_dve"], 2 * n + 2)
                        for h in range(NH):
                            ins = nc.tensor.matmul(PS[:, 7, 0:D], UT[:, h].rearrange("p b i -> p (b i)"), VO[:, h, :],
                                                   start=(h == 0), stop=(h == NH - 1))
                        ins.then_inc(s["out_ready"], 1)


class CrossAttention:
    def __init__(self, core):
        self.core = core
        names = ("h_ready", "hT_ready", "hT_kept", "rot_ready", "q_turned", "q_rot_spread", "q_plain_ready",
                  "q_plain_kept", "ctxT_ready", "ctxT_kept", "last_kept", "k_ready", "k_turned", "scores_ready",
                  "top_ready", "exp_done", "inverse_ready", "pT_ready", "pT_kept", "u_ready", "last_part_ready",
                  "u_normed", "uT_ready", "uT_kept", "out_ready", "dve_steps", "zeroed", "held")
        self.sems = {n: core.sem("cross_" + n) for n in names}
        self.sems["ctx_loaded"] = [core.sem(f"cross_ctx_loaded{b}") for b in range(BT)]

    def run(self, W, VO, QK, norm_row, bias_row, tables, last_rows_T):
        core, nc, PS, X, s = self.core, self.core.nc, self.core.PS, self.core.X, self.sems
        NS = BT * NG
        STEPS = 3 * (2 * BT + 1) + 2
        ctx = core.dram["ctx"]
        with ExitStack() as st:
            def buf(name, shape):
                return core.buffer(st, "cross_" + name, shape)

            H, HT = buf("H", [P, D]), buf("HT", [P, P])
            C = [buf(f"C{b}", [P, 2, D]) for b in range(BT)]
            last_bc = [buf(f"last_bc{b}", [P, D]) for b in range(BT)]
            ctxT = buf("ctxT", [P, BT, SK])
            KR = [buf(f"KR{i}", [P, NG, SK]) for i in range(2)]
            keep = buf("keep", [P, 2, SK])
            QR = buf("QR", [P, NG, P])
            QRd = buf("QRd", [P, NG, BT, HG, S])
            QN = buf("QN", [P, NG, BT, HG, S])
            PR = [buf(f"PR{i}", [P, SK]) for i in range(3)]
            PT = [buf(f"PT{i}", [P, 2, P]) for i in range(2)]
            last_part = [buf(f"last_part{i}", [P, D]) for i in range(2)]
            U = [buf(f"U{i}", [P, D]) for i in range(2)]
            UT = buf("UT", [P, NH, BT, S])
            minus_top, total, inverse = buf("minus_top", [P, NS]), buf("total", [P, NS]), buf("inverse", [P, NS])

            def pair(src):
                return tables[src][:].unsqueeze(1).to_broadcast([P, 2, SK])

            with nc.Block() as block:
                @block.sync
                def _(sp):
                    def load(t, b):
                        row = BT * t + b
                        sp.dma_start(C[b][:], ctx[row, 0:2 * P, :].rearrange("(c p) d -> p c d", p=P))\
                          .then_inc(s["ctx_loaded"][b], 16)
                        sp.dma_start(last_bc[b][:], ctx[row, SK - 1, :].partition_broadcast(P))\
                          .then_inc(s["ctx_loaded"][b], 16)
                    for b in range(BT):
                        load(0, b)
                    with sp.Fori(0, NT - 1) as t:
                        for b in range(BT):
                            sp.wait_ge(s["u_normed"], t * NS + NG * (b + 1))
                            load(t + 1, b)

                @block.gpsimd
                def _(pool):
                    nc.gpsimd.memset(QRd[:], 0.0).then_inc(s["zeroed"], 1)
                    with pool.Fori(0, NT) as t:
                        n = t
                        pool.wait_ge(s["h_ready"], n + 1)
                        nc.gpsimd.tensor_copy(ctxT[:, :, SK - 1], last_rows_T[:, t, :]).then_inc(s["last_kept"], 1)
                        for q in range(NS):
                            b = q // NG
                            if q % NG == 0:
                                pool.wait_ge(s["ctx_loaded"][b], 32 * n + 32)
                            pool.wait_ge(s["inverse_ready"], NS * n + q + 1)
                            if q >= 2:
                                pool.wait_ge(s["u_normed"], NS * n + q - 1)
                            pool.sem_inc(s["held"], 1)
                            nc.gpsimd.tensor_scalar(last_part[q % 2][:], last_bc[b][:], PR[q % 3][:, SK - 1:SK],
                                                    inverse[:, q:q + 1], ALU.mult, ALU.mult)\
                              .then_inc(s["last_part_ready"], 1)

                @block.vector
                def _(dve):
                    with dve.Fori(0, NT) as t:
                        n = t
                        step = Steps(dve, s["dve_steps"], n * STEPS)
                        nc.vector.scalar_tensor_tensor(H[:], X[:, t, :], core.rstd[:, t, :], norm_row[:],
                                                       ALU.mult, ALU.mult).then_inc(s["h_ready"], 1)

                        def key_rope(b, half):
                            return Rope(nc, step, PS[:, 0:2, 0:SK], keep[:], pair("cos_k"), pair("sin_k"),
                                        KR[b % 2][:, 2 * half:2 * half + 2, :], SWAP_HALVES)

                        def rope_first(b, half):
                            dve.wait_ge(s["k_ready"], 2 * BT * n + 2 * b + half + 1)
                            if b or half:
                                dve.wait_ge(s["k_turned"], 2 * BT * n + 2 * b + half)
                            key_rope(b, half).first()

                        def rope_second(b, half):
                            key_rope(b, half).second().then_inc(s["k_turned"], 1)

                        rope_first(0, 0)
                        rope_second(0, 0)
                        dve.wait_ge(s["rot_ready"], n + 1)
                        dve.wait_ge(s["k_turned"], 2 * BT * n + 1)
                        view = lambda a: a.rearrange("p (m i) -> p m i", i=S)
                        bc = lambda a: tables[a][:].unsqueeze(1).to_broadcast([P, NG * BT, S])
                        q_keep = keep[:].rearrange("p g n -> p (g n)")[:, 0:NG * P]
                        q_rope = Rope(nc, step, view(PS[:, 5, :]), view(q_keep), bc("cos_q"), bc("sin_q"),
                                      view(QR[:].rearrange("p g n -> p (g n)")), SWAP_HALVES)
                        q_rope.first()
                        q_rope.second().then_inc(s["q_turned"], 1)
                        dve.wait_ge(s["q_turned"], n + 1)
                        rope_first(0, 1)
                        rope_second(0, 1)
                        for q in range(NS + 2):
                            b, g = divmod(q, NG)
                            if q < NS:
                                dve.wait_ge(s["scores_ready"], NS * n + q + 1)
                                nc.vector.tensor_reduce(minus_top[:, q:q + 1], PS[:, 2 + q % 2, 0:SK], AX.X, ALU.max,
                                                        negate=True).then_inc(s["top_ready"], 1)
                                if b + 1 < BT:
                                    (rope_first, rope_second)[g % 2](b + 1, g // 2)
                            if 1 <= q <= NS:
                                dve.wait_ge(s["exp_done"], NS * n + q)
                                nc.vector.reciprocal(inverse[:, q - 1:q], total[:, q - 1:q]).then_inc(s["inverse_ready"], 1)
                            if q >= 2:
                                dve.wait_ge(s["u_ready"], NS * n + q - 1)
                                dve.wait_ge(s["last_part_ready"], NS * n + q - 1)
                                dve.wait_ge(s["inverse_ready"], NS * n + q - 1)
                                if q >= 4:
                                    dve.wait_ge(s["uT_ready"], NS * n + q - 3)
                                nc.vector.scalar_tensor_tensor(U[q % 2][:], PS[:, 5, 0:D],
                                                               inverse[:, q - 2:q - 1], last_part[q % 2][:],
                                                               ALU.mult, ALU.add).then_inc(s["u_normed"], 1)
                        dve.wait_ge(s["out_ready"], n + 1)
                        step(nc.vector.tensor_tensor(X[:, t, :], X[:, t, :], PS[:, 5, 0:D], ALU.add))
                        step(nc.vector.tensor_tensor(X[:, t, :], X[:, t, :], bias_row[:], ALU.add))
                        assert step.n == STEPS

                @block.scalar
                def _(act):
                    act.wait_ge(s["zeroed"], 1)
                    with act.Fori(0, NT) as t:
                        n = t

                        def keep_ctxT(b):
                            act.wait_ge(s["ctxT_ready"], BT * n + b + 1)
                            nc.scalar.activation(ctxT[:, b, 0:2 * P], PS[:, 6, 0:2 * P],
                                                 ACT.Copy).then_inc(s["ctxT_kept"], 1)

                        keep_ctxT(0)
                        act.wait_ge(s["hT_ready"], n + 1)
                        nc.scalar.activation(HT[:], PS[:, 7, 0:P], ACT.Copy).then_inc(s["hT_kept"], 1)
                        for g in range(NG):
                            act.wait_ge(s["q_plain_ready"], NG * n + g + 1)
                            nc.scalar.activation(QN[:, g].rearrange("p b h i -> p h b i"),
                                                 PS[:, (2, 3, 4, 7)[g], :].rearrange("p (h b i) -> p h b i", h=HG, b=BT),
                                                 ACT.Copy, scale=DH ** -0.5).then_inc(s["q_plain_kept"], 1)
                        act.wait_ge(s["q_turned"], n + 1)
                        for h in range(HG):
                            r = slice(32 * h, 32 * h + 32)
                            nc.scalar.activation(QRd[r, :, :, h, :], QR[r].rearrange(
                                "p g (b i) -> p g b i", b=BT), ACT.Copy).then_inc(s["q_rot_spread"], 1)
                        keep_ctxT(1)
                        for q in range(NS + 3):
                            b, g = divmod(q, NG)
                            if q < NS:
                                act.wait_ge(s["top_ready"], NS * n + q + 1)
                                if q >= 3:
                                    act.wait_ge(s["pT_ready"], NS * n + q - 2)
                                    act.wait_ge(s["last_part_ready"], NS * n + q - 2)
                                nc.scalar.activation(PR[q % 3][:], PS[:, 2 + q % 2, 0:SK], ACT.Exp,
                                                     bias=minus_top[:, q:q + 1],
                                                     accum_out=total[:, q:q + 1]).then_inc(s["exp_done"], 1)
                                if g == 1 and b + 2 < BT:
                                    keep_ctxT(b + 2)
                            if 1 <= q <= NS:
                                act.wait_ge(s["pT_ready"], NS * n + q)
                                if q >= 3:
                                    act.wait_ge(s["u_ready"], NS * n + q - 2)
                                nc.scalar.activation(PT[(q - 1) % 2][:].rearrange("p c n -> p (c n)"),
                                                     PS[:, 4, 0:2 * P],
                                                     ACT.Copy).then_inc(s["pT_kept"], 1)
                            if q >= 3:
                                act.wait_ge(s["uT_ready"], NS * n + q - 2)
                                pb, pg = divmod(q - 3, NG)
                                nc.scalar.activation(UT[:, pg * HG:(pg + 1) * HG, pb, :],
                                                     PS[:, 7, 0:P].rearrange("p (h i) -> p h i", i=S),
                                                     ACT.Copy).then_inc(s["uT_kept"], 1)

                @block.tensor
                def _(pe):
                    pe.wait_ge(s["zeroed"], 1)
                    with pe.Fori(0, NT) as t:
                        n = t

                        def turn_ctx(b):
                            pe.wait_ge(s["ctx_loaded"][b], 32 * n + 32)
                            if b:
                                pe.wait_ge(s["ctxT_kept"], BT * n + b)
                            for c in range(2):
                                ins = nc.tensor.transpose(PS[:, 6, c * P:(c + 1) * P], C[b][:, c, :], core.ident[:])
                            ins.then_inc(s["ctxT_ready"], 1)

                        def keys(b, half):
                            pe.wait_ge(s["ctxT_kept"], BT * n + b + 1)
                            if b == 0:
                                pe.wait_ge(s["last_kept"], n + 1)
                            if b or half:
                                pe.wait_ge(s["k_turned"], 2 * BT * n + 2 * b + half)
                            for g in range(2):
                                gg = 2 * half + g
                                ins = nc.tensor.matmul(PS[:, g, 0:SK], W["ckR"][:, gg * P:(gg + 1) * P],
                                                       ctxT[:, b, :], start=True, stop=True)
                            ins.then_inc(s["k_ready"], 1)

                        turn_ctx(0)
                        pe.wait_ge(s["h_ready"], n + 1)
                        nc.tensor.transpose(PS[:, 7, 0:P], H[:], core.ident[:]).then_inc(s["hT_ready"], 1)
                        keys(0, 0)
                        pe.wait_ge(s["hT_kept"], n + 1)
                        for g in range(NG):
                            ins = nc.tensor.matmul(PS[:, 5, g * P:(g + 1) * P], W["cqR"][:, g * P:(g + 1) * P], HT[:],
                                                   start=True, stop=True)
                        ins.then_inc(s["rot_ready"], 1)
                        for g in range(NG):
                            for h in range(HG):
                                ins = nc.tensor.matmul(PS[:, (2, 3, 4, 7)[g], h * P:(h + 1) * P], QK[:, g * HG + h, :],
                                                       HT[:], start=True, stop=True)
                            ins.then_inc(s["q_plain_ready"], 1)
                        keys(0, 1)
                        turn_ctx(1)
                        for q in range(NS + 3):
                            b, g = divmod(q, NG)
                            if q < NS:
                                if q == 0:
                                    pe.wait_ge(s["q_plain_kept"], NG * n + NG)
                                    pe.wait_ge(s["q_rot_spread"], HG * n + HG)
                                if g % 2 == 0:
                                    pe.wait_ge(s["k_turned"], 2 * BT * n + 2 * b + g // 2 + 1)
                                if q >= 2:
                                    pe.wait_ge(s["exp_done"], NS * n + q - 1)
                                out = PS[:, 2 + q % 2, 0:SK]
                                nc.tensor.matmul(out, QN[:, g, b].rearrange("p h i -> p (h i)"), ctxT[:, b, :],
                                                 start=True, stop=False)
                                nc.tensor.matmul(out, QRd[:, g, b].rearrange("p h i -> p (h i)"), KR[b % 2][:, g, :],
                                                 start=False, stop=True).then_inc(s["scores_ready"], 1)
                                if b + 1 < BT and g % 2 == 0:
                                    keys(b + 1, g // 2)
                                if b + 2 < BT and g == 1:
                                    turn_ctx(b + 2)
                            if 1 <= q <= NS:
                                pe.wait_ge(s["exp_done"], NS * n + q)
                                if q >= 2:
                                    pe.wait_ge(s["pT_kept"], NS * n + q - 1)
                                for c in range(2):
                                    ins = nc.tensor.transpose(PS[:, 4, c * P:(c + 1) * P],
                                                              PR[(q - 1) % 3][:, c * P:(c + 1) * P], core.ident[:])
                                ins.then_inc(s["pT_ready"], 1)
                            if 2 <= q <= NS + 1:
                                pe.wait_ge(s["pT_kept"], NS * n + q - 1)
                                if q >= 3:
                                    pe.wait_ge(s["u_normed"], NS * n + q - 2)
                                for c in range(2):
                                    ins = nc.tensor.matmul(PS[:, 5, 0:D], PT[q % 2][:, c, :],
                                                           C[(q - 2) // NG][:, c, :], start=(c == 0), stop=(c == 1))
                                ins.then_inc(s["u_ready"], 1)
                            if q >= 3:
                                pe.wait_ge(s["u_normed"], NS * n + q - 2)
                                if q >= 4:
                                    pe.wait_ge(s["uT_kept"], NS * n + q - 3)
                                nc.tensor.transpose(PS[:, 7, 0:P], U[(q - 3) % 2][:], core.ident[:])\
                                  .then_inc(s["uT_ready"], 1)
                        pe.wait_ge(s["uT_kept"], NS * n + NS)
                        for h in range(NH):
                            ins = nc.tensor.matmul(PS[:, 5, 0:D], UT[:, h].rearrange("p b i -> p (b i)"),
                                                   VO[:, h, :], start=(h == 0), stop=(h == NH - 1))
                        ins.then_inc(s["out_ready"], 1)


class FeedForward:
    def __init__(self, core):
        self.core = core
        names = ("h_ready", "hT_ready", "hT_kept", "hidden_ready", "gelu_done", "out_ready", "added", "done")
        self.sems = {n: core.sem("ffn_" + n) for n in names}

    def run(self, W1, W2, b1, norm_row, bias_row):
        core, nc, PS, s = self.core, self.core.nc, self.core.PS, self.sems
        NU = NT // 4
        X4 = core.X[:].rearrange("p (u j) d -> p u j d", j=4)
        R4 = core.rstd[:].rearrange("p (u j) o -> p u j o", j=4)
        with ExitStack() as st:
            H = core.buffer(st, "ffn_H", [P, 4, D])
            HT = core.buffer(st, "ffn_HT", [P, 4 * P])
            G = core.buffer(st, "ffn_G", [P, FC, 4 * P])
            with nc.Block() as block:
                @block.vector
                def _(dve):
                    with dve.Fori(0, NU) as u:
                        n = u
                        for j in range(4):
                            nc.vector.scalar_tensor_tensor(H[:, j, :], X4[:, u, j, :], R4[:, u, j, :], norm_row[:],
                                                           ALU.mult, ALU.mult).then_inc(s["h_ready"], 1)
                        dve.wait_ge(s["out_ready"], n + 1)
                        nc.vector.tensor_tensor(X4[:, u], X4[:, u], PS[:, 5, :].rearrange("p (j d) -> p j d", j=4),
                                                ALU.add).then_inc(s["added"], 1)
                        dve.wait_ge(s["added"], n + 1)
                        nc.vector.tensor_tensor(X4[:, u], X4[:, u], bias_row[:].unsqueeze(1).to_broadcast([P, 4, D]),
                                                ALU.add).then_inc(s["done"], 1)
                        dve.wait_ge(s["done"], n + 1)

                @block.scalar
                def _(act):
                    with act.Fori(0, NU) as u:
                        n = u
                        act.wait_ge(s["hT_ready"], n + 1)
                        nc.scalar.activation(HT[:], PS[:, 0, :], ACT.Copy).then_inc(s["hT_kept"], 1)
                        for c in range(FC):
                            act.wait_ge(s["hidden_ready"], FC * n + c + 1)
                            nc.scalar.activation(G[:, c, :], PS[:, 1 + c, :], ACT.Gelu,
                                                 bias=b1[:, c:c + 1]).then_inc(s["gelu_done"], 1)

                @block.tensor
                def _(pe):
                    with pe.Fori(0, NU) as u:
                        n = u
                        pe.wait_ge(s["h_ready"], 4 * n + 4)
                        for j in range(4):
                            ins = nc.tensor.transpose(PS[:, 0, j * P:(j + 1) * P], H[:, j, :], core.ident[:])
                        ins.then_inc(s["hT_ready"], 1)
                        pe.wait_ge(s["hT_kept"], n + 1)
                        for c in range(FC):
                            nc.tensor.matmul(PS[:, 1 + c, :], W1[:, c * P:(c + 1) * P], HT[:],
                                             start=True, stop=True).then_inc(s["hidden_ready"], 1)
                        pe.wait_ge(s["gelu_done"], FC * n + FC)
                        for j in range(4):
                            for c in range(FC):
                                ins = nc.tensor.matmul(PS[:, 5, j * D:(j + 1) * D], G[:, c, j * P:(j + 1) * P],
                                                       W2[:, c, :], start=(c == 0), stop=(c == FC - 1))
                        ins.then_inc(s["out_ready"], 1)


def project(core, st, HB):
    nc, PS, dram = core.nc, core.PS, core.dram
    NU = NT // 4
    Statistics(core, "rms_out").run(core.X, True)
    X4 = core.X[:].rearrange("p (u j) d -> p u j d", j=4)
    B4 = HB[:].rearrange("p (u j) d -> p u j d", j=4)
    R4 = core.rstd[:].rearrange("p (u j) o -> p u j o", j=4)
    loaded, h_ready, hT_ready, hT_kept, out_ready, added, done = (
        core.sem("proj_" + n) for n in ("loaded", "h_ready", "hT_ready", "hT_kept", "out_ready", "added", "done"))
    H = core.buffer(st, "proj_H", [P, 4, D])
    HT = core.buffer(st, "proj_HT", [P, 4 * P])
    Wp = core.buffer(st, "proj_W", [P, D])
    norm_row, bias_row = core.buffer(st, "proj_norm", [P, D]), core.buffer(st, "proj_bias", [P, D])
    with nc.Block() as block:
        @block.sync
        def _(sp):
            for dst, src in ((norm_row[:], dram["norm_out_w"].partition_broadcast(P)), (Wp[:], dram["proj_w"]),
                             (bias_row[:], dram["proj_b"].partition_broadcast(P)), (HB[:], core.x_tiles)):
                sp.dma_start(dst, src).then_inc(loaded, 16)
            sp.wait_ge(loaded, 64)

        @block.vector
        def _(dve):
            dve.wait_ge(loaded, 64)
            with dve.Fori(0, NU) as u:
                for j in range(4):
                    nc.vector.scalar_tensor_tensor(H[:, j, :], X4[:, u, j, :], R4[:, u, j, :], norm_row[:],
                                                   ALU.mult, ALU.mult).then_inc(h_ready, 1)
                dve.wait_ge(h_ready, 4 * u + 4)
                dve.wait_ge(out_ready, u + 1)
                nc.vector.tensor_tensor(X4[:, u], B4[:, u], PS[:, 1, :].rearrange("p (j d) -> p j d", j=4),
                                        ALU.add).then_inc(added, 1)
                dve.wait_ge(added, u + 1)
                nc.vector.tensor_tensor(X4[:, u], X4[:, u], bias_row[:].unsqueeze(1).to_broadcast([P, 4, D]),
                                        ALU.add).then_inc(done, 1)
                dve.wait_ge(done, u + 1)

        @block.scalar
        def _(act):
            with act.Fori(0, NU) as u:
                act.wait_ge(hT_ready, u + 1)
                nc.scalar.activation(HT[:], PS[:, 0, :], ACT.Copy).then_inc(hT_kept, 1)

        @block.tensor
        def _(pe):
            pe.wait_ge(loaded, 64)
            with pe.Fori(0, NU) as u:
                pe.wait_ge(h_ready, 4 * u + 4)
                for j in range(4):
                    ins = nc.tensor.transpose(PS[:, 0, j * P:(j + 1) * P], H[:, j, :], core.ident[:])
                ins.then_inc(hT_ready, 1)
                pe.wait_ge(hT_kept, u + 1)
                for j in range(4):
                    ins = nc.tensor.matmul(PS[:, 1, j * D:(j + 1) * D], HT[:, j * P:(j + 1) * P], Wp[:],
                                           start=True, stop=True)
                ins.then_inc(out_ready, 1)


class SmallAttention:

    def __init__(self, core, st):
        self.core = core
        buf = lambda name, shape: core.buffer(st, "small_" + name, shape)
        self.W = {n: buf("W" + n, [P, D]) for n in "qkvo"}
        self.rows = {n: buf("row_" + n, [P, D]) for n in ("bv", "bo", "g", "b")}
        self.cols = buf("cols", [P, 2])
        self.tables = {n: buf(n, [P, S]) for n in ("cos8_q", "sin8_q", "cos8_k", "sin8_k")}
        self.pick = buf("pick", [P, HG])
        self.H, self.HT = buf("H", [P, D]), buf("HT", [P, P])
        self.Q, self.K, self.V, self.keep = (buf(n, [P, P]) for n in ("Q", "K", "V", "keep"))
        self.Qd = buf("Qd", [P, BT, HG, S])
        self.top, self.total, self.inverse = (buf(n, [P, NG, BT]) for n in ("top", "total", "inverse"))
        self.PR, self.PT = buf("PR", [P, NG, P]), buf("PT", [P, NG, P])
        self.picked, self.OT = buf("picked", [P, BT, HG, S]), buf("OT", [P, BT, S])

    def run(self, X, rotary):
        core, nc, PS, dram = self.core, self.core.nc, self.core.PS, self.core.dram
        name = "b_" if rotary else "c_"
        (loaded, h_ready, hT_ready, hT_kept, qkv_ready, q_spread, k_ready, v_kept, scores_ready, shifted, exp_done,
         probs_ready, pT_ready, pT_kept, o_ready, o_picked, out_ready, steps, held) = (core.sem(name + n) for n in (
             "loaded", "h_ready", "hT_ready", "hT_kept", "qkv_ready", "q_spread", "k_ready", "v_kept", "scores_ready",
             "shifted", "exp_done", "probs_ready", "pT_ready", "pT_kept", "o_ready", "o_picked", "out_ready", "steps", "held"))
        W, rows, tables, H, HT = self.W, self.rows, self.tables, self.H, self.HT
        loads = [(W[n][:], dram[name + "W" + n]) for n in "qkvo"]
        if rotary:
            loads += [(tables[n][:], dram[n]) for n in tables] + [(self.pick[:], dram["pick"])]
        else:
            loads += [(rows[n][:], dram["c_row_" + n].partition_broadcast(P)) for n in rows]
            loads += [(self.cols[:], dram["c_cols"])]
        need = 16 * len(loads)
        SC = PS[:, 0:4, 0:P].rearrange("p g (b j) -> p g b j", j=S)
        STEPS = 12 if rotary else 9

        def per_row(v):
            return v[:].unsqueeze(3).to_broadcast([P, NG, BT, S])

        with nc.Block() as block:
            @block.sync
            def _(sp):
                for dst, src in loads:
                    sp.dma_start(dst, src).then_inc(loaded, 16)

            @block.vector
            def _(dve):
                dve.wait_ge(loaded, need)
                with dve.Fori(0, NT) as t:
                    step = Steps(dve, steps, t * STEPS)
                    norm = nc.vector.tensor_scalar(H[:], X[:, t, :], core.mean_var[:, t, 0:1], core.rstd[:, t, :],
                                                   ALU.subtract, ALU.mult)
                    if rotary:
                        norm.then_inc(h_ready, 1)
                    else:
                        step(norm)
                        step(nc.vector.tensor_tensor(H[:], H[:], rows["g"][:], ALU.mult))
                        nc.vector.tensor_tensor(H[:], H[:], rows["b"][:], ALU.add).then_inc(h_ready, 1)
                    view = lambda a: a.rearrange("p (b i) -> p b i", i=S)
                    for k, (raw, out) in enumerate(((PS[:, 5, 0:P], self.Q), (PS[:, 6, 0:P], self.K))):
                        dve.wait_ge(qkv_ready, 3 * t + k + 1)
                        if rotary:
                            bc = lambda a: tables[a][:].unsqueeze(1).to_broadcast([P, BT, S])
                            kind = "qk"[k]
                            rope = Rope(nc, step, view(raw), view(self.keep[:]), bc("cos8_" + kind),
                                        bc("sin8_" + kind), view(out[:]), SWAP_PAIRS)
                            rope.first()
                            last = rope.second()
                        else:
                            last = nc.vector.tensor_scalar(out[:], raw, self.cols[:, k:k + 1],
                                                           HD8 ** -0.5 if k == 0 else 1.0, ALU.add, ALU.mult)
                        if k == 0:
                            step(last)
                            for h in range(HG):
                                nc.vector.tensor_scalar(self.Qd[:, :, h, :], view(self.Q[:]), self.pick[:, h:h + 1],
                                                        None, ALU.mult).then_inc(q_spread, 1)
                        else:
                            last.then_inc(k_ready, 1)
                    dve.wait_ge(qkv_ready, 3 * t + 3)
                    if rotary:
                        nc.vector.tensor_copy(self.V[:], PS[:, 7, 0:P]).then_inc(v_kept, 1)
                    else:
                        nc.vector.tensor_tensor(self.V[:], PS[:, 7, 0:P], rows["bv"][:], ALU.add).then_inc(v_kept, 1)
                    dve.wait_ge(scores_ready, t + 1)
                    step(nc.vector.tensor_reduce(self.top[:], SC, AX.X, ALU.max))
                    nc.vector.tensor_tensor(SC, SC, per_row(self.top), ALU.subtract).then_inc(shifted, 1)
                    dve.wait_ge(exp_done, t + 1)
                    step(nc.vector.tensor_reduce(self.total[:], SC, AX.X, ALU.add))
                    step(nc.vector.reciprocal(self.inverse[:], self.total[:]))
                    nc.vector.tensor_tensor(self.PR[:].rearrange("p g (b j) -> p g b j", j=S), SC,
                                            per_row(self.inverse), ALU.mult).then_inc(probs_ready, 1)
                    dve.wait_ge(o_ready, t + 1)
                    for b in range(BT):
                        ins = nc.vector.tensor_tensor(self.picked[:, b], PS[:, b, 0:P].rearrange("p (h i) -> p h i", i=S),
                                                      self.pick[:].unsqueeze(2).to_broadcast([P, HG, S]), ALU.mult)
                        if b == BT - 1:
                            step(ins)
                    nc.vector.tensor_reduce(self.OT[:], self.picked[:].rearrange("p b h i -> p b i h"), AX.X,
                                            ALU.add).then_inc(o_picked, 1)
                    dve.wait_ge(out_ready, t + 1)
                    step(nc.vector.tensor_tensor(X[:, t, :], X[:, t, :], PS[:, 4, 0:D], ALU.add))
                    if not rotary:
                        step(nc.vector.tensor_tensor(X[:, t, :], X[:, t, :], rows["bo"][:], ALU.add))
                    assert step.n == STEPS, step.n

            @block.scalar
            def _(act):
                with act.Fori(0, NT) as t:
                    act.wait_ge(hT_ready, t + 1)
                    nc.scalar.activation(HT[:], PS[:, 4, 0:P], ACT.Copy).then_inc(hT_kept, 1)
                    act.wait_ge(shifted, t + 1)
                    nc.scalar.activation(SC, SC, ACT.Exp).then_inc(exp_done, 1)
                    act.wait_ge(pT_ready, t + 1)
                    nc.scalar.activation(self.PT[:].rearrange("p g n -> p (g n)"), PS[:, 5, :],
                                         ACT.Copy).then_inc(pT_kept, 1)

            @block.tensor
            def _(pe):
                pe.wait_ge(loaded, need)
                with pe.Fori(0, NT) as t:
                    pe.wait_ge(h_ready, t + 1)
                    nc.tensor.transpose(PS[:, 4, 0:P], H[:], core.ident[:]).then_inc(hT_ready, 1)
                    pe.wait_ge(hT_kept, t + 1)
                    nc.tensor.matmul(PS[:, 5, 0:P], W["q"][:], HT[:], start=True, stop=True).then_inc(qkv_ready, 1)
                    nc.tensor.matmul(PS[:, 6, 0:P], W["k"][:], HT[:], start=True, stop=True).then_inc(qkv_ready, 1)
                    nc.tensor.matmul(PS[:, 7, 0:P], HT[:], W["v"][:], start=True, stop=True).then_inc(qkv_ready, 1)
                    pe.wait_ge(q_spread, 4 * t + 4)
                    pe.wait_ge(k_ready, t + 1)
                    for b in range(BT):
                        for g in range(NG):
                            r = slice(32 * g, 32 * g + 32)
                            ins = nc.tensor.matmul(PS[:, g, b * S:(b + 1) * S],
                                                   self.Qd[r, b].rearrange("p h i -> p (h i)"),
                                                   self.K[r, b * S:(b + 1) * S], start=True, stop=True)
                    ins.then_inc(scores_ready, 1)
                    pe.wait_ge(probs_ready, t + 1)
                    for g in range(NG):
                        ins = nc.tensor.transpose(PS[:, 5, g * P:(g + 1) * P], self.PR[:, g, :], core.ident[:])
                    ins.then_inc(pT_ready, 1)
                    pe.wait_ge(pT_kept, t + 1)
                    pe.wait_ge(v_kept, t + 1)
                    pe.sem_inc(held, 1)
                    for g in range(NG):
                        for b in range(BT):
                            r, c = slice(32 * b, 32 * b + 32), slice(32 * g, 32 * g + 32)
                            ins = nc.tensor.matmul(PS[c, b, 0:P], self.V[r, c], self.PT[r, g, :],
                                                   start=True, stop=True)
                    ins.then_inc(o_ready, 1)
                    pe.wait_ge(o_picked, t + 1)
                    nc.tensor.matmul(PS[:, 4, 0:D], self.OT[:].rearrange("p b i -> p (b i)"), W["o"][:],
                                     start=True, stop=True).then_inc(out_ready, 1)


def experts(core, st, HB):
    nc, PS, dram, X = core.nc, core.PS, core.dram, core.X
    buf = lambda name, shape: core.buffer(st, "moe_" + name, shape)
    H2T = buf("H2T", [P, NT, P])
    W1, W2 = buf("W1", [P, NE, FF]), buf("W2", [P, NE, FC, D])
    b1, b2 = buf("b1", [P, NE, FC]), buf("b2", [NE, D])
    Wr = buf("Wr", [P, NE])
    g_row, b_row = buf("g_row", [P, D]), buf("b_row", [P, D])
    upto, ones = buf("upto", [P, P]), buf("ones", [P, P])
    order = buf("order", [P, NE])
    H, HT = buf("H", [P, D]), buf("HT", [P, P])
    L, E, PRB, EQ, M1, M2, C1, C2, A, A2, V1 = (buf(n, [P, NT, NE]) for n in (
        "logits", "exps", "probs", "equal", "first", "second", "place1", "place2", "scan_a", "scan_b", "kept"))
    GATE = buf("gate", [P, NT, NE])
    row, row2, row3 = buf("row", [P, NT]), buf("row2", [P, NT]), buf("row3", [P, NT])
    sems = {n: core.sem("moe_" + n) for n in (
        "loaded", "normed", "h_ready", "hT_ready", "hT_kept", "hT_kept_all", "logits_ready", "logits_kept",
        "shifted", "exp_done", "steps", "masks_ready", "counts_ready", "gates_ready",
        "gT_ready", "gT_kept", "base_ready", "base_added", "base_all", "hidden_ready", "relu_act", "relu_dve",
        "y_ready", "y_added", "stored")}
    S_ = lambda n: sems[n]
    loads = [(W1[:], dram["e_w1"].rearrange("e d f -> d e f")),
             (W2[:], dram["e_w2"].rearrange("e (c p) d -> p e c d", p=P)),
             (b1[:], dram["e_b1T"]), (b2[:], dram["e_b2"]), (Wr[:], dram["wr"]),
             (g_row[:], dram["ln2_g"].partition_broadcast(P)), (b_row[:], dram["ln2_b"].partition_broadcast(P)),
             (upto[:], dram["upto"]), (ones[:], dram["ones"]), (order[:], dram["order"])]

    with nc.Block() as block:
        @block.sync
        def _(sp):
            for dst, src in loads[2:] + loads[:2]:
                sp.dma_start(dst, src).then_inc(S_("loaded"), 16)
            sp.wait_ge(S_("loaded"), 16 * len(loads))

        @block.vector
        def _(dve):
            dve.wait_ge(S_("loaded"), 16 * len(loads))
            with dve.Fori(0, NT) as t:
                step = Steps(dve, S_("steps"), 2 * t)
                step(nc.vector.tensor_scalar(H[:], HB[:, t, :], core.mean_var[:, t, 0:1], core.rstd[:, t, :],
                                             ALU.subtract, ALU.mult))
                step(nc.vector.tensor_tensor(H[:], H[:], g_row[:], ALU.mult))
                nc.vector.tensor_tensor(H[:], H[:], b_row[:], ALU.add).then_inc(S_("h_ready"), 1)
                dve.wait_ge(S_("hT_kept"), t + 1)
                nc.vector.tensor_copy(H2T[:, t, :], HT[:]).then_inc(S_("hT_kept_all"), 1)
                dve.wait_ge(S_("logits_ready"), t + 1)
                nc.vector.tensor_copy(L[:, t, :], PS[:, 1, 0:NE]).then_inc(S_("logits_kept"), 1)
            dve.wait_ge(S_("logits_kept"), NT)

        @block.scalar
        def _(act):
            with act.Fori(0, NT) as t:
                act.wait_ge(S_("hT_ready"), t + 1)
                nc.scalar.activation(HT[:], PS[:, 0, 0:P], ACT.Copy).then_inc(S_("hT_kept"), 1)

        @block.tensor
        def _(pe):
            pe.wait_ge(S_("loaded"), 16 * len(loads))
            with pe.Fori(0, NT) as t:
                pe.wait_ge(S_("h_ready"), t + 1)
                nc.tensor.transpose(PS[:, 0, 0:P], H[:], core.ident[:]).then_inc(S_("hT_ready"), 1)
                pe.wait_ge(S_("hT_kept"), t + 1)
                nc.tensor.matmul(PS[:, 1, 0:NE], HT[:], Wr[:], start=True, stop=True).then_inc(S_("logits_ready"), 1)
                pe.wait_ge(S_("hT_kept_all"), t + 1)

    def each(v):
        return v[:].unsqueeze(2).to_broadcast([P, NT, NE])

    with nc.Block() as block:
        @block.vector
        def _(dve):
            step = Steps(dve, S_("steps"), 2 * NT)
            tt = lambda o, a, b, op: step(nc.vector.tensor_tensor(o, a, b, op))
            orders = order[:].unsqueeze(1).to_broadcast([P, NT, NE])

            def one_hot(dst, values):
                step(nc.vector.tensor_reduce(row[:], values, AX.X, ALU.max))
                tt(EQ[:], values, each(row), ALU.is_equal)
                tt(EQ[:], EQ[:], orders, ALU.mult)
                step(nc.vector.tensor_reduce(row[:], EQ[:], AX.X, ALU.max))
                tt(dst, EQ[:], each(row), ALU.is_equal)

            step(nc.vector.tensor_reduce(row[:], L[:], AX.X, ALU.max))
            nc.vector.tensor_tensor(E[:], L[:], each(row), ALU.subtract).then_inc(S_("shifted"), 1)
            dve.wait_ge(S_("exp_done"), 1)
            step(nc.vector.tensor_reduce(row[:], E[:], AX.X, ALU.add))
            step(nc.vector.reciprocal(row2[:], row[:]))
            tt(PRB[:], E[:], each(row2), ALU.mult)
            one_hot(M1[:], PRB[:])
            step(nc.vector.tensor_scalar(EQ[:], M1[:], -3.0e38, None, ALU.mult))
            tt(L[:], L[:], EQ[:], ALU.add)
            one_hot(M2[:], L[:])
            dve.wait_ge(S_("steps"), 2 * NT + step.n)
            nc.vector.tensor_copy(V1[:], M2[:]).then_inc(S_("masks_ready"), 1)
            dve.wait_ge(S_("counts_ready"), 1)

            def places(dst, k):
                step(nc.vector.tensor_copy(A[:], PS[:, 2 * k + 1, 0:NT * NE]))
                a, b = A, A2
                shift = 1
                while shift < NT:
                    step(nc.vector.tensor_copy(b[:, 0:shift, :], a[:, 0:shift, :]))
                    tt(b[:, shift:NT, :], a[:, shift:NT, :], a[:, 0:NT - shift, :], ALU.add)
                    a, b = b, a
                    shift *= 2
                tt(dst, a[:], PS[:, 2 * k + 1, 0:NT * NE].rearrange("p (t e) -> p t e", e=NE), ALU.subtract)
                tt(dst, dst, PS[:, 2 * k, 0:NT * NE].rearrange("p (t e) -> p t e", e=NE), ALU.add)
                return a

            a = places(C1[:], 0)
            step(nc.vector.tensor_copy(V1[:, 0, :], a[:, NT - 1, :]))
            places(C2[:], 1)
            tt(C2[:], C2[:], V1[:, 0:1, :].to_broadcast([P, NT, NE]), ALU.add)
            for m, c in ((M1, C1), (M2, C2)):
                step(nc.vector.tensor_scalar(c[:], c[:], float(CAP), None, ALU.is_le))
                tt(m[:], m[:], c[:], ALU.mult)
            for m, r in ((M1, row2), (M2, row3)):
                tt(EQ[:], PRB[:], m[:], ALU.mult)
                step(nc.vector.tensor_reduce(r[:], EQ[:], AX.X, ALU.add))
            tt(row[:], row2[:], row3[:], ALU.add)
            step(nc.vector.tensor_scalar(row[:], row[:], float(np.finfo(np.float32).eps), None, ALU.max))
            step(nc.vector.reciprocal(row[:], row[:]))
            for m, r in ((M1, row2), (M2, row3)):
                tt(r[:], r[:], row[:], ALU.mult)
                tt(m[:], m[:], each(r), ALU.mult)
            tt(GATE[:], M1[:], M2[:], ALU.add)
            step(nc.vector.tensor_scalar(GATE[:], GATE[:], 1.0 - 0.2, None, ALU.mult))

        @block.scalar
        def _(act):
            act.wait_ge(S_("shifted"), 1)
            nc.scalar.activation(E[:], E[:], ACT.Exp).then_inc(S_("exp_done"), 1)

        @block.tensor
        def _(pe):
            pe.wait_ge(S_("masks_ready"), 1)
            for k, m in enumerate((M1, M2)):
                flat = m[:].rearrange("p t e -> p (t e)")
                nc.tensor.matmul(PS[:, 2 * k, 0:NT * NE], upto[:], flat, start=True, stop=True)
                ins = nc.tensor.matmul(PS[:, 2 * k + 1, 0:NT * NE], ones[:], flat, start=True, stop=True)
            ins.then_inc(S_("counts_ready"), 1)

    GT = buf("gT", [NE, P])
    G8 = buf("g8", [P, NE])
    with nc.Block() as block:
        @block.vector
        def _(dve):
            with dve.Fori(0, NT) as t:
                nc.vector.tensor_copy(G8[:], GATE[:, t, :]).then_inc(S_("gates_ready"), 1)
                nc.vector.tensor_tensor(X[:, t, :], X[:, t, :], HB[:, t, :], ALU.add).then_inc(S_("base_added"), 1)
                dve.wait_ge(S_("base_added"), t + 1)
                dve.wait_ge(S_("base_ready"), t + 1)
                nc.vector.tensor_tensor(X[:, t, :], X[:, t, :], PS[:, 1, 0:D], ALU.add).then_inc(S_("base_all"), 1)
            dve.wait_ge(S_("base_all"), NT)

        @block.scalar
        def _(act):
            with act.Fori(0, NT) as t:
                act.wait_ge(S_("gT_ready"), t + 1)
                nc.scalar.activation(GT[:], PS[0:NE, 0, 0:P], ACT.Copy).then_inc(S_("gT_kept"), 1)

        @block.tensor
        def _(pe):
            with pe.Fori(0, NT) as t:
                pe.wait_ge(S_("gates_ready"), t + 1)
                nc.tensor.transpose(PS[0:NE, 0, 0:P], G8[:], core.ident[:]).then_inc(S_("gT_ready"), 1)
                pe.wait_ge(S_("gT_kept"), t + 1)
                nc.tensor.matmul(PS[:, 1, 0:D], GT[:], b2[:], start=True, stop=True).then_inc(S_("base_ready"), 1)

    NU = NT // 4
    HT4 = H2T[:].rearrange("p (u j) n -> p u (j n)", j=4)
    X4 = X[:].rearrange("p (u j) d -> p u j d", j=4)
    G4 = GATE[:].rearrange("p (u j) e -> p u j e", j=4)
    out4 = dram["out"].rearrange("(u j b) s d -> u (b s) j d", j=4, b=BT)
    G = [buf(f"hidden{i}", [P, FC, 4 * P]) for i in range(2)]
    with nc.Block() as block:
        @block.tensor
        def _(pe):
            with pe.Fori(0, NU) as u:
                def up(e):
                    for c in range(FC):
                        if e >= 1:
                            pe.wait_ge(S_(("relu_act", "relu_dve")[c % 2]), 2 * NE * u + 2 * (e - 1) + c // 2 + 1)
                        nc.tensor.matmul(PS[:, 2 + c, :], W1[:, e, c * P:(c + 1) * P], HT4[:, u, :],
                                         start=True, stop=True).then_inc(S_("hidden_ready"), 1)
                up(0)
                for e in range(NE):
                    if e + 1 < NE:
                        up(e + 1)
                    pe.wait_ge(S_("relu_act"), 2 * NE * u + 2 * e + 2)
                    pe.wait_ge(S_("relu_dve"), 2 * NE * u + 2 * e + 2)
                    if e >= 2:
                        pe.wait_ge(S_("y_added"), 4 * (NE * u + e - 1))
                    for j in range(4):
                        for c in range(FC):
                            ins = nc.tensor.matmul(PS[:, 6 + e % 2, j * D:(j + 1) * D],
                                                   G[e % 2][:, c, j * P:(j + 1) * P], W2[:, e, c, :],
                                                   start=(c == 0), stop=(c == FC - 1))
                    ins.then_inc(S_("y_ready"), 1)
                pe.wait_ge(S_("y_added"), 4 * NE * (u + 1))

        @block.scalar
        def _(act):
            with act.Fori(0, NU) as u:
                for e in range(NE):
                    for c in (0, 2):
                        act.wait_ge(S_("hidden_ready"), FC * (NE * u + e) + c + 1)
                        if e >= 2:
                            act.wait_ge(S_("y_ready"), NE * u + e - 1)
                        nc.scalar.activation(G[e % 2][:, c, :], PS[:, 2 + c, :], ACT.Relu,
                                             bias=b1[:, e, c:c + 1]).then_inc(S_("relu_act"), 1)

        @block.vector
        def _(dve):
            with dve.Fori(0, NU) as u:
                for e in range(NE + 1):
                    for c in (1, 3):
                        if e < NE:
                            dve.wait_ge(S_("hidden_ready"), FC * (NE * u + e) + c + 1)
                            if e >= 2:
                                dve.wait_ge(S_("y_ready"), NE * u + e - 1)
                            nc.vector.tensor_scalar(G[e % 2][:, c, :], PS[:, 2 + c, :], b1[:, e, c:c + 1], 0.0,
                                                    ALU.add, ALU.max).then_inc(S_("relu_dve"), 1)
                    if e:
                        dve.wait_ge(S_("y_ready"), NE * u + e)
                        if e >= 2:
                            dve.wait_ge(S_("y_added"), 4 * (NE * u + e - 1))
                        for j in range(4):
                            nc.vector.scalar_tensor_tensor(X4[:, u, j, :], PS[:, 6 + (e - 1) % 2, j * D:(j + 1) * D],
                                                           G4[:, u, j, e - 1:e], X4[:, u, j, :], ALU.mult,
                                                           ALU.add).then_inc(S_("y_added"), 1)

        @block.sync
        def _(sp):
            with sp.Fori(0, NU) as u:
                sp.wait_ge(S_("y_added"), 4 * NE * (u + 1))
                sp.dma_start(out4[u], X4[:, u]).then_inc(S_("stored"), 16)
            sp.wait_ge(S_("stored"), 16 * NU)


def tables():
    f32 = np.float32
    t = {"ident": np.eye(P, dtype=f32), "ones": np.ones((P, P), f32),
         "upto": np.triu(np.ones((P, P), f32)),
         "order": np.tile(np.arange(NE, 0, -1, dtype=f32), (P, 1))}
    lanes = np.arange(P)
    c = lanes % 32
    inv = (1.0 / f32(10000.0) ** (np.arange(0, ROT, 2, dtype=f32) / f32(ROT))).astype(f32)
    angle = (np.arange(SK, dtype=f32)[:, None] * inv[None, :]).astype(f32)[:, c % 16].T
    sign = np.where(c < 16, -1.0, 1.0).astype(f32)[:, None]
    t["cos_k"], t["sin_k"] = np.cos(angle).astype(f32), (np.sin(angle) * sign).astype(f32)
    t["cos_q"] = (t["cos_k"][:, :S] * f32(DH ** -0.5)).astype(f32)
    t["sin_q"] = (t["sin_k"][:, :S] * f32(DH ** -0.5)).astype(f32)
    c = lanes % HD8
    inv = (1.0 / f32(10000.0) ** (np.arange(0, HD8, 2, dtype=f32) / f32(HD8))).astype(f32)
    angle = (np.arange(S, dtype=f32)[:, None] * inv[None, :]).astype(f32)[:, c % 4].T
    sign = np.where(c < 4, -1.0, 1.0).astype(f32)[:, None]
    t["cos8_k"], t["sin8_k"] = np.cos(angle).astype(f32), (np.sin(angle) * sign).astype(f32)
    t["cos8_q"] = (t["cos8_k"] / f32(HD8 ** -0.5)).astype(f32)
    t["sin8_q"] = (t["sin8_k"] / f32(HD8 ** -0.5)).astype(f32)
    t["pick"] = (lanes[:, None] % 32 // HD8 == np.arange(HG)[None, :]).astype(f32)
    return t


def lay_out(i):
    def heads(w, rotated):
        w = w.reshape(LAYERS, D, NH, DH)
        return (w[..., :ROT] if rotated else w[..., ROT:]).reshape(LAYERS, D, NH * ROT)

    x = "L0_xattn_"
    a = {"x": i["x"], "ctx": i["ctx_1024"], "mask": i["mask_BxS_bf1"].view(np.uint8).reshape(-1)}
    a["sqR"], a["skR"] = heads(i[x + "Wq"], True), heads(i[x + "Wk"], True)
    a["sqN"], a["skN"] = heads(i[x + "Wq"], False), heads(i[x + "Wk"], False)
    a["cqR"], a["ckR"] = heads(i[x + "cWq"], True), heads(i[x + "cWk"], True)
    a["cqNT"] = heads(i[x + "cWq"], False).transpose(0, 2, 1)
    a["ckNT"] = heads(i[x + "cWk"], False).transpose(0, 2, 1)
    a["sWvT"], a["cWvT"] = i[x + "Wv"].transpose(0, 2, 1), i[x + "cWv"].transpose(0, 2, 1)
    a["sWo"], a["cWo"] = i[x + "Wo"], i[x + "cWo"]
    a["w1"], a["w2"] = i[x + "ff_w1"], i[x + "ff_w2"]
    a["b1T"] = i[x + "ff_b1"].reshape(LAYERS, FC, P).transpose(0, 2, 1)
    for n, src in (("sw", "attn_norm_w"), ("cw", "cross_norm_w"), ("fw", "ff_norm_w"), ("sbo", "bo"),
                   ("cbo", "cbo"), ("fb2", "ff_b2")):
        a["row_" + n] = i[x + src]
    for n in ("norm_out_w", "proj_w", "proj_b"):
        a[n] = i[x + n]
    for n in "qkvo":
        a["b_W" + n] = i["L0_attn_W" + n].T
        a["c_W" + n] = i["L0_ffn_w" + n]
    for n, src in (("bv", "bv"), ("bo", "bo"), ("g", "ln1_g"), ("b", "ln1_b")):
        a["c_row_" + n] = i["L0_ffn_" + src]
    a["c_cols"] = np.stack([i["L0_ffn_bq"], i["L0_ffn_bk"]], axis=1)
    a["e_w1"], a["e_w2"], a["e_b2"], a["wr"] = (i["L0_ffn_" + n] for n in ("w1", "w2", "b2", "wr"))
    a["e_b1T"] = i["L0_ffn_b1"].reshape(NE, FC, P).transpose(2, 0, 1)
    a["ln2_g"], a["ln2_b"] = i["L0_ffn_ln2_g"], i["L0_ffn_ln2_b"]
    return a


def kernel(**inputs):
    import concourse.bacc as bacc
    from concourse.bass_utils import run_bass_kernel_spmd

    nc = bacc.Bacc("TRN2", target_bir_lowering=False, num_devices=1)
    arrays = {n: np.ascontiguousarray(a) for n, a in lay_out({k: np.asarray(v) for k, v in inputs.items()}).items()}
    arrays.update({n: np.ascontiguousarray(a) for n, a in tables().items()})
    dram = {n: nc.dram_tensor("in_" + n, a.shape, mybir.dt.from_np(a.dtype), kind="ExternalInput").ap()
            for n, a in arrays.items()}
    dram["out"] = nc.dram_tensor("out", (B, S, D), F32, kind="ExternalOutput").ap()
    build(nc, dram)
    r = run_bass_kernel_spmd(nc, [{"in_" + n: a for n, a in arrays.items()}], core_ids=[0])
    return r.results[0]["out"]
```

```python
from contextlib import ExitStack, contextmanager

import numpy as np
import concourse.bass as bass
from concourse import mybir

F32 = mybir.dt.float32
U8 = mybir.dt.uint8
ALU = mybir.AluOpType
ACT = mybir.ActivationFunctionType
AX = mybir.AxisListType

P = 128
B, S, D = 128, 32, 128
BT = P // S
NT = B // BT
LAYERS = 2
NH, DH, ROT = 16, 64, 32
NG = 4
HG = NH // NG
SK = 257
FF = 512
FC = FF // P
NE, CAP = 8, 1024
HD8 = 8
BIG = float(np.finfo(np.float32).max)
PLAIN_AT = (11, 12, 13, 15)
SWAP_HALVES = [(i + 16) % 32 for i in range(32)]
SWAP_PAIRS = [8 * (i // 8) + (2 * (i % 8) + 1 if i % 8 < 4 else 2 * (i % 8 - 4)) for i in range(32)]


def in_eights(eng, body):
    with eng.Fori(0, NT // 8) as u:
        for j in range(8):
            body(8 * u + j)


def in_pairs(eng, count, tile):
    with eng.Fori(0, count // 2 - 1) as u:
        tile(2 * u, 0, False)
        tile(2 * u + 1, 1, False)
    tile(count - 2, 0, False)
    tile(count - 1, 1, True)


class Steps:

    def __init__(self, eng, sem, base):
        self.eng, self.sem, self.base, self.n = eng, sem, base, 0

    def go(self, ins):
        self.n += 1
        ins.then_inc(self.sem, 1)

    def __call__(self, ins):
        self.go(ins)
        self.eng.wait_ge(self.sem, self.base + self.n)


class Core:

    def __init__(self, nc, dram, stack):
        self.nc, self.dram, self.stack = nc, dram, stack
        self.PS = stack.enter_context(nc.psum_tensor("PS", [P, 8, 512], F32))
        self.X = self.buffer(stack, "X", [P, NT, D])
        self.ident = self.buffer(stack, "ident", [P, P])
        self.moments = self.buffer(stack, "moments", [P, NT, 6])
        self.mean_var = self.buffer(stack, "mean_var", [P, NT, 1])
        self.root = self.buffer(stack, "root", [P, NT])
        self.rstd = self.buffer(stack, "rstd", [P, NT, 1])
        self.x_tiles = dram["x"].rearrange("(t b) s d -> (b s) t d", b=BT)

    def sem(self, name):
        self.sems.append(self.nc.alloc_semaphore(name=name))
        return self.sems[-1]

    def clear_sems(self):
        for sem in self.sems:
            self.nc.gpsimd.sem_clear(sem)
        self.nc.all_engine_barrier()

    @contextmanager
    def stage(self):
        self.sems = []
        with ExitStack() as st:
            yield st
        self.nc.clear_and_free_semaphores(self.sems)
        self.nc.all_engine_barrier()

    def buffer(self, stack, name, shape, dt=F32):
        return stack.enter_context(self.nc.sbuf_tensor(name, shape, dt))


class Statistics:

    def __init__(self, core, name):
        self.core = core
        self.moments_done, self.steps = core.sem(name + "_moments_done"), core.sem(name + "_steps")
        self.square_ready, self.root_ready = core.sem(name + "_square_ready"), core.sem(name + "_root_ready")

    def run(self, src, rms):
        nc, c = self.core.nc, self.core
        with nc.Block() as block:
            @block.vector
            def _(dve):
                in_eights(dve, lambda t: nc.vector.bn_stats(c.moments[:, t, :], src[:, t, :])
                          .then_inc(self.moments_done, 1))
                dve.wait_ge(self.moments_done, NT)
                mean0, m2_0, mean1, m2_1 = (c.moments[:, :, i] for i in (1, 2, 4, 5))
                mean = c.mean_var[:, :, 0]
                step = Steps(dve, self.steps, 0)
                step(nc.vector.tensor_tensor(mean, mean0, mean1, ALU.add))
                step(nc.vector.tensor_scalar(mean, mean, 0.5, None, ALU.mult))
                step(nc.vector.tensor_tensor(mean0, mean0, mean1, ALU.subtract))
                step(nc.vector.scalar_tensor_tensor(mean0, mean0, 0.25, mean0, ALU.mult, ALU.mult))
                step(nc.vector.tensor_tensor(m2_0, m2_0, m2_1, ALU.add))
                step(nc.vector.scalar_tensor_tensor(c.root[:], m2_0, 1.0 / D, mean0, ALU.mult, ALU.add))
                if rms:
                    step(nc.vector.tensor_tensor(mean, mean, mean, ALU.mult))
                    nc.vector.tensor_tensor(c.root[:], c.root[:], mean, ALU.add).then_inc(self.square_ready, 1)
                else:
                    nc.vector.tensor_scalar(c.root[:], c.root[:], 1e-5, None, ALU.add).then_inc(self.square_ready, 1)
                dve.wait_ge(self.root_ready, 1)
                if rms:
                    step(nc.vector.tensor_scalar(c.root[:], c.root[:], 1e-8, None, ALU.max))
                step(nc.vector.reciprocal(c.rstd[:, :, 0], c.root[:]))

            @block.scalar
            def _(act):
                act.wait_ge(self.square_ready, 1)
                nc.scalar.activation(c.root[:], c.root[:], ACT.Sqrt).then_inc(self.root_ready, 1)


def build(nc, dram):
    with ExitStack() as top:
        core = Core(nc, dram, top)
        with core.stage():
            loaded = core.sem("start_loaded")
            with nc.Block() as block:
                @block.sync
                def _(sp):
                    sp.dma_start(core.X[:], core.x_tiles).then_inc(loaded, 16)
                    sp.dma_start(core.ident[:], dram["ident"]).then_inc(loaded, 16)
                    sp.wait_ge(loaded, 32)

            Statistics(core, "ln_x").run(core.X, False)
            normalise(core, core.X, core.X, "x_normed")
        with core.stage() as st:
            perceiver(core, st)
        HB = core.buffer(top, "HB", [P, NT, D])
        with core.stage() as st:
            project(core, st, HB)
        with core.stage() as st:
            small = SmallAttention(core, st)
            Statistics(core, "ln_b").run(core.X, False)
            small.run(core.X, rotary=True)
            Statistics(core, "ln_c").run(core.X, False)
            normalise(core, HB, core.X, "c_normed")
            Statistics(core, "ln_c1").run(HB, False)
            small.run(HB, rotary=False)
        with core.stage() as st:
            Statistics(core, "ln_c2").run(HB, False)
            experts(core, st, HB)


def normalise(core, dst, src, name):
    nc, done = core.nc, core.sem(name)
    with nc.Block() as block:
        @block.vector
        def _(dve):
            in_eights(dve, lambda t: nc.vector.tensor_scalar(
                dst[:, t, :], src[:, t, :], core.mean_var[:, t, 0:1], core.rstd[:, t, :],
                ALU.subtract, ALU.mult).then_inc(done, 1))
            dve.wait_ge(done, NT)


def heads(width, g):
    per = P // width
    first = g % per + 4 * per * (g // per)
    return range(first, first + 4 * per, per)


def perceiver(core, st):
    nc, dram = core.nc, core.dram
    def buf(name, shape, dt=F32):
        return core.buffer(st, name, shape, dt)

    tables = {n: buf(n, [P, SK if n[-1] == "k" else S]) for n in ("cos_k", "sin_k", "cos_q", "sin_q")}
    mask_bytes = buf("mask_bytes", [P, NT, BT * S], U8)
    last_rows_T = buf("last_rows_T", [P, NT, BT])
    W = {n: buf("w_" + n, [P, NH * ROT]) for n in ("sqR", "skR", "sqN", "skN", "cqR", "ckR")}
    VO = {a: buf("VO_" + a, [P, NH, D]) for a in "sc"}
    QK = buf("QK", [P, NH, D])
    W1, W2 = buf("W1", [P, FF]), buf("W2", [P, FC, D])
    b1 = buf("b1", [P, FC])
    rows = {n: buf("row_" + n, [P, D]) for n in ("sw", "cw", "fw", "sbo", "cbo", "fb2")}

    tables_loaded, last_turned, last_kept = (core.sem(n) for n in ("tables_loaded", "last_turned", "last_kept"))
    with ExitStack() as tmp, nc.Block() as block:
        last_rows = core.buffer(tmp, "last_rows", [B, D])

        @block.sync
        def _(sp):
            for n in tables:
                sp.dma_start(tables[n][:], dram[n]).then_inc(tables_loaded, 16)
            sp.dma_start(mask_bytes[:], dram["mask"].partition_broadcast(P)).then_inc(tables_loaded, 16)
            sp.dma_start(last_rows[:], dram["ctx"][:, SK - 1, :]).then_inc(tables_loaded, 16)

        @block.tensor
        def _(pe):
            pe.wait_ge(tables_loaded, 96)
            nc.tensor.transpose(core.PS[:, 0, 0:B], last_rows[:], core.ident[:]).then_inc(last_turned, 1)

        @block.vector
        def _(dve):
            dve.wait_ge(last_turned, 1)
            nc.vector.tensor_copy(last_rows_T[:], core.PS[:, 0, 0:B]).then_inc(last_kept, 1)
            dve.wait_ge(last_kept, 1)

    loaded, product_ready, product_kept = (core.sem(n) for n in
                                           ("weights_loaded", "product_ready", "product_kept"))
    stats = [Statistics(core, n) for n in ("rms_self", "rms_cross", "rms_ffn")]
    self_attention, cross_attention, feed_forward = SelfAttention(core), CrossAttention(core), FeedForward(core)

    with nc.Fori(0, LAYERS) as l:
        with ExitStack() as tmp:
            WvT = {a: core.buffer(tmp, "WvT_" + a, [P, NH // 2, D]) for a in "sc"}
            Wo = {a: core.buffer(tmp, "Wo_" + a, [P, NH // 2, D]) for a in "sc"}
            WqNT, WkNT = core.buffer(tmp, "WqNT", [P, NG, D]), core.buffer(tmp, "WkNT", [P, NG, D])
            chunks = lambda a: a.rearrange("(c p) d -> p c d", p=P)
            loads = [(W[n][:], dram[n][l]) for n in W]
            loads += [(WvT[a][:], chunks(dram[a + "WvT"][l])) for a in "sc"]
            loads += [(Wo[a][:], chunks(dram[a + "Wo"][l])) for a in "sc"]
            loads += [(WqNT[:], chunks(dram["cqNT"][l])), (WkNT[:], chunks(dram["ckNT"][l])),
                      (W1[:], dram["w1"][l]), (W2[:], chunks(dram["w2"][l])), (b1[:], dram["b1T"][l])]
            loads += [(rows[n][:], dram["row_" + n][l].partition_broadcast(P)) for n in rows]
            total = 16 * len(loads)
            products = [(VO["s"], WvT["s"], Wo["s"], DH), (VO["c"], WvT["c"], Wo["c"], DH),
                        (QK, WqNT, WkNT, ROT)]
            turns = [(p, g) for p in products for g in range(NG)]

            with nc.Block() as block:
                @block.sync
                def _(sp):
                    for dst, src in loads:
                        sp.dma_start(dst, src).then_inc(loaded, 16)
                    sp.wait_ge(loaded, total)

                @block.tensor
                def _(pe):
                    pe.wait_ge(loaded, total)
                    for k, ((_, left, right, width), g) in enumerate(turns):
                        if k >= 8:
                            pe.wait_ge(product_kept, k - 7)
                        for h, head in enumerate(heads(width, g)):
                            chunk, r = divmod(head * width, P)
                            ins = nc.tensor.matmul(core.PS[:, k % 8, h * D:(h + 1) * D],
                                                   left[r:r + width, chunk, :], right[r:r + width, chunk, :],
                                                   start=True, stop=True)
                        ins.then_inc(product_ready, 1)

                @block.vector
                def _(dve):
                    for k, ((dst, _, _, width), g) in enumerate(turns):
                        dve.wait_ge(product_ready, k + 1)
                        of = heads(width, g)
                        nc.vector.tensor_copy(dst[:, of.start:of[-1] + 1:of.step, :],
                                              core.PS[:, k % 8, :].rearrange("p (h d) -> p h d", h=HG)).then_inc(product_kept, 1)
                    dve.wait_ge(product_kept, len(turns))

        stats[0].run(core.X, True)
        self_attention.run(W, VO["s"], rows["sw"], rows["sbo"], tables, mask_bytes)
        stats[1].run(core.X, True)
        cross_attention.run(W, VO["c"], QK, rows["cw"], rows["cbo"], tables, last_rows_T)
        stats[2].run(core.X, True)
        feed_forward.run(W1, W2, b1, rows["fw"], rows["fb2"])
        core.clear_sems()


class Rope:

    def __init__(self, nc, step, raw, keep, cos, sin, out, swap):
        self.nc, self.step, self.raw, self.keep, self.cos, self.sin, self.out, self.swap = (
            nc, step, raw, keep, cos, sin, out, swap)

    def first(self):
        self.step.go(self.nc.vector.tensor_tensor(self.keep, self.raw, self.cos, ALU.mult))
        self.step(self.nc.vector.stream_shuffle(self.raw, self.raw, self.swap))

    def second(self):
        self.step(self.nc.vector.tensor_tensor(self.raw, self.raw, self.sin, ALU.mult))
        return self.nc.vector.tensor_tensor(self.out, self.raw, self.keep, ALU.add)


class SelfAttention:

    def __init__(self, core):
        self.core = core
        names = ("h_ready", "hT_ready", "hT_kept", "rot_ready", "plain_ready", "q_turned", "k_turned",
                 "q_rot_spread", "q_plain_spread", "k_plain_kept", "mask_ready", "scores_ready", "shifted",
                 "exp_done", "probs_ready", "pT_ready", "pT_kept", "uT_ready", "uT_kept", "out_ready", "dve_steps",
                 "pool_steps", "zeroed", "held")
        self.sems = {n: core.sem("self_" + n) for n in names}

    def run(self, W, VO, norm_row, bias_row, tables, mask_bytes):
        core, nc, PS, X, s = self.core, self.core.nc, self.core.PS, self.core.X, self.sems
        FRONT_STEPS, BACK_STEPS = 6, 7
        with ExitStack() as st:
            def buf(name, shape):
                return core.buffer(st, "self_" + name, shape)

            H = [buf(f"H{i}", [P, D]) for i in range(2)]
            HT = buf("HT", [P, P])
            keep = buf("keep", [P, NG * P])
            QR = buf("QR", [P, NG, P])
            QD, K = buf("QD", [P, NG, 2, BT, 2, S]), buf("K", [P, NG, 2, P])
            allow, forbid = buf("allow", [P, 1, P]), buf("forbid", [P, 1, P])
            top, total, inverse = buf("top", [P, NG * BT]), buf("total", [P, NG * BT]), buf("inverse", [P, NG * BT])
            PR, PT = buf("PR", [P, NG, P]), buf("PT", [P, NG, P])
            UT = buf("UT", [P, NH, BT, S])
            SC = PS[:, 4, :]
            SC3 = SC.rearrange("p (g n) -> p g n", g=NG)
            SCj = SC.rearrange("p (m j) -> p m j", j=S)
            flat = lambda a: a[:].rearrange("p g n -> p (g n)")

            def per_row(v):
                return v[:].unsqueeze(2).to_broadcast([P, NG * BT, S])

            with nc.Block() as block:
                @block.gpsimd
                def _(pool):
                    nc.gpsimd.memset(QD[:], 0.0).then_inc(s["zeroed"], 1)
                    with pool.Fori(0, NT) as n:
                        pool.wait_ge(s["k_turned"], 2 * n + 2)
                        nc.gpsimd.tensor_copy(allow[:, 0, :], mask_bytes[:, n, :]).then_inc(s["pool_steps"], 1)
                        pool.wait_ge(s["pool_steps"], n + 1)
                        pool.sem_inc(s["held"], 1)
                        nc.gpsimd.tensor_scalar(forbid[:], allow[:], -1.0, BIG, ALU.add,
                                                ALU.mult).then_inc(s["mask_ready"], 1)

                @block.vector
                def _(dve):
                    def hidden(n, parity):
                        nc.vector.scalar_tensor_tensor(H[parity][:], X[:, n, :], core.rstd[:, n, :], norm_row[:],
                                                       ALU.mult, ALU.mult).then_inc(s["h_ready"], 1)

                    def turn(step, n):
                        view = lambda a: a.rearrange("p (m i) -> p m i", i=S)
                        for k, (c, i) in enumerate((("cos_q", "sin_q"), ("cos_k", "sin_k"))):
                            dve.wait_ge(s["rot_ready"], 2 * n + k + 1)
                            if k == 1:
                                dve.wait_ge(s["q_turned"], n + 1)
                            bc = lambda a: tables[a][:, 0:S].unsqueeze(1).to_broadcast([P, NG * BT, S])
                            rope = Rope(nc, step, view(PS[:, k, :]), view(keep[:]), bc(c), bc(i), view(flat(QR)),
                                        SWAP_HALVES)
                            rope.first()
                            if k == 0:
                                rope.second().then_inc(s["q_turned"], 1)
                                continue
                            step(nc.vector.tensor_tensor(rope.raw, rope.raw, rope.sin, ALU.mult))
                            for pair in range(2):
                                r = slice(64 * pair, 64 * pair + 64)
                                nc.vector.tensor_tensor(K[r, :, pair, :],
                                                        PS[r, 1, :].rearrange("p (g n) -> p g n", g=NG),
                                                        keep[r].rearrange("p (g n) -> p g n", g=NG),
                                                        ALU.add).then_inc(s["k_turned"], 1)

                    def tile(n, parity, last):
                        if not last:
                            hidden(n + 1, 1 - parity)
                        step = Steps(dve, s["dve_steps"], FRONT_STEPS + n * (FRONT_STEPS + BACK_STEPS))
                        dve.wait_ge(s["scores_ready"], n + 1)
                        dve.wait_ge(s["mask_ready"], n + 1)
                        step(nc.vector.tensor_tensor(SC3, SC3, allow[:].to_broadcast([P, NG, P]), ALU.mult))
                        step(nc.vector.tensor_tensor(SC3, SC3, forbid[:].to_broadcast([P, NG, P]), ALU.add))
                        step(nc.vector.tensor_reduce(top[:], SCj, AX.X, ALU.max))
                        nc.vector.tensor_tensor(SCj, SCj, per_row(top), ALU.subtract).then_inc(s["shifted"], 1)
                        dve.wait_ge(s["exp_done"], n + 1)
                        step(nc.vector.tensor_reduce(total[:], SCj, AX.X, ALU.add))
                        step(nc.vector.reciprocal(inverse[:], total[:]))
                        nc.vector.tensor_tensor(PR[:].rearrange("p g (b j) -> p (g b) j", j=S), SCj,
                                                per_row(inverse), ALU.mult).then_inc(s["probs_ready"], 1)
                        if not last:
                            turn(step, n + 1)
                        dve.wait_ge(s["out_ready"], n + 1)
                        step(nc.vector.tensor_tensor(X[:, n, :], X[:, n, :], PS[:, 5, 0:D], ALU.add))
                        step(nc.vector.tensor_tensor(X[:, n, :], X[:, n, :], bias_row[:], ALU.add))
                        assert step.n == BACK_STEPS + (0 if last else FRONT_STEPS)

                    hidden(0, 0)
                    turn(Steps(dve, s["dve_steps"], 0), 0)
                    in_pairs(dve, NT, tile)

                @block.scalar
                def _(act):
                    def keep_hT(n):
                        act.wait_ge(s["hT_ready"], n + 1)
                        nc.scalar.activation(HT[:], PS[:, 5, 0:P], ACT.Copy).then_inc(s["hT_kept"], 1)

                    def plain(n):
                        act.wait_ge(s["plain_ready"], 2 * n + 1)
                        for x in range(HG):
                            r = slice(32 * x, 32 * x + 32)
                            nc.scalar.activation(QD[r, :, (x // 2 + 1) % 2, :, x % 2, :], PS[r, 2, :].rearrange(
                                "p (g b i) -> p g b i", g=NG, b=BT), ACT.Copy, scale=DH ** -0.5)\
                              .then_inc(s["q_plain_spread"], 1)
                        act.wait_ge(s["plain_ready"], 2 * n + 2)
                        for pair in range(2):
                            r = slice(64 * (1 - pair), 64 * (1 - pair) + 64)
                            nc.scalar.activation(K[r, :, pair, :], PS[r, 3, :].rearrange("p (g n) -> p g n", g=NG),
                                                 ACT.Copy).then_inc(s["k_plain_kept"], 1)

                    def rotated(n):
                        act.wait_ge(s["q_turned"], n + 1)
                        for h in range(HG):
                            r = slice(32 * h, 32 * h + 32)
                            nc.scalar.activation(QD[r, :, h // 2, :, h % 2, :], QR[r].rearrange(
                                "p g (b i) -> p g b i", b=BT), ACT.Copy).then_inc(s["q_rot_spread"], 1)

                    def tile(n, parity, last):
                        if not last:
                            keep_hT(n + 1)
                        act.wait_ge(s["shifted"], n + 1)
                        nc.scalar.activation(SC, SC, ACT.Exp).then_inc(s["exp_done"], 1)
                        if not last:
                            plain(n + 1)
                        act.wait_ge(s["pT_ready"], n + 1)
                        nc.scalar.activation(flat(PT), PS[:, 5, :], ACT.Copy).then_inc(s["pT_kept"], 1)
                        for b in range(BT):
                            act.wait_ge(s["uT_ready"], BT * n + b + 1)
                            nc.scalar.activation(UT[:, :, b, :], PS[:, 6 + b % 2, :].rearrange("p (h i) -> p h i", i=S),
                                                 ACT.Copy).then_inc(s["uT_kept"], 1)
                        if not last:
                            rotated(n + 1)

                    act.wait_ge(s["zeroed"], 1)
                    keep_hT(0)
                    plain(0)
                    rotated(0)
                    in_pairs(act, NT, tile)

                @block.tensor
                def _(pe):
                    def front(n, parity):
                        pe.wait_ge(s["h_ready"], n + 1)
                        nc.tensor.transpose(PS[:, 5, 0:P], H[parity][:], core.ident[:]).then_inc(s["hT_ready"], 1)
                        pe.wait_ge(s["hT_kept"], n + 1)
                        project(2, "sqN", "plain_ready")
                        project(3, "skN", "plain_ready")
                        project(0, "sqR", "rot_ready")

                    def project(bank, w, done):
                        for g in range(NG):
                            ins = nc.tensor.matmul(PS[:, bank, g * P:(g + 1) * P], W[w][:, g * P:(g + 1) * P],
                                                   HT[:], start=True, stop=True)
                        ins.then_inc(s[done], 1)

                    def tile(n, parity, last):
                        pe.wait_ge(s["q_plain_spread"], HG * n + HG)
                        pe.wait_ge(s["k_plain_kept"], 2 * n + 2)
                        pe.wait_ge(s["q_rot_spread"], HG * n + HG)
                        pe.wait_ge(s["k_turned"], 2 * n + 2)
                        for g in range(NG):
                            for pair in range(2):
                                for b in range(BT):
                                    ins = nc.tensor.matmul(
                                        PS[64 * pair:64 * pair + 64, 4, g * P + b * S:g * P + (b + 1) * S],
                                        QD[:, g, pair, b].rearrange("p h i -> p (h i)"),
                                        K[:, g, pair, b * S:(b + 1) * S], start=True, stop=True)
                        ins.then_inc(s["scores_ready"], 1)
                        if not last:
                            front(n + 1, 1 - parity)
                        pe.wait_ge(s["probs_ready"], n + 1)
                        for g in range(NG):
                            ins = nc.tensor.transpose(PS[:, 5, g * P:(g + 1) * P], PR[:, g, :], core.ident[:])
                        ins.then_inc(s["pT_ready"], 1)
                        if not last:
                            project(1, "skR", "rot_ready")
                        pe.wait_ge(s["pT_kept"], n + 1)
                        for b in range(BT):
                            if b >= 2:
                                pe.wait_ge(s["uT_kept"], BT * n + b - 1)
                            r = slice(b * S, (b + 1) * S)
                            nc.tensor.matmul(PS[:, 6 + b % 2, :], H[parity][r, :], flat(PT)[r],
                                             start=True, stop=True).then_inc(s["uT_ready"], 1)
                        pe.wait_ge(s["uT_kept"], BT * n + BT)
                        for h in range(NH):
                            ins = nc.tensor.matmul(PS[:, 5, 0:D], UT[:, h].rearrange("p b i -> p (b i)"), VO[:, h, :],
                                                   start=(h == 0), stop=(h == NH - 1))
                        ins.then_inc(s["out_ready"], 1)

                    pe.wait_ge(s["zeroed"], 1)
                    front(0, 0)
                    project(1, "skR", "rot_ready")
                    in_pairs(pe, NT, tile)


class CrossAttention:

    def __init__(self, core):
        self.core = core
        names = ("h_ready", "hT_ready", "hT_kept", "rot_ready", "q_turned", "q_rot_spread", "q_plain_ready",
                 "q_plain_kept", "ctxT_ready", "ctxT_kept", "last_kept", "k_ready", "k_turned", "scores_ready",
                 "top_ready", "exp_done", "inverse_ready", "pT_ready", "pT_kept", "u_ready", "last_part_ready",
                 "u_normed", "uT_ready", "uT_kept", "out_ready", "x_added", "dve_steps", "zeroed", "held")
        self.sems = {n: core.sem("cross_" + n) for n in names}
        self.sems["ctx_loaded"] = [core.sem(f"cross_ctx_loaded{b}") for b in range(BT)]

    def run(self, W, VO, QK, norm_row, bias_row, tables, last_rows_T):
        core, nc, PS, X, s = self.core, self.core.nc, self.core.PS, self.core.X, self.sems
        NS = BT * NG
        NK = 2 * BT
        KEEP_Q, KEEP_K, ADD = 3, 3, 1
        TILE_STEPS = NK * KEEP_K + KEEP_Q + ADD
        ctx = core.dram["ctx"]
        with ExitStack() as st:
            def buf(name, shape):
                return core.buffer(st, "cross_" + name, shape)

            H, HT = buf("H", [P, D]), buf("HT", [P, P])
            C = [buf(f"C{b}", [P, 2, D]) for b in range(BT)]
            last_bc = [buf(f"last_bc{b}", [P, D]) for b in range(BT)]
            ctxT = buf("ctxT", [P, BT, SK])
            KR = [buf(f"KR{i}", [P, NG, SK]) for i in range(2)]
            keep, keep_q = buf("keep", [P, 2, SK]), buf("keep_q", [P, NG * P])
            QR = buf("QR", [P, NG, P])
            QRd = [buf(f"QRd{i}", [P, NG, BT, HG, S]) for i in range(2)]
            QN = [buf(f"QN{i}", [P, NG, BT, HG, S]) for i in range(2)]
            PR = [buf(f"PR{i}", [P, SK]) for i in range(4)]
            PT = [buf(f"PT{i}", [P, 2, P]) for i in range(2)]
            last_part = [buf(f"last_part{i}", [P, D]) for i in range(2)]
            U = [buf(f"U{i}", [P, D]) for i in range(2)]
            UT = buf("UT", [P, NH, BT, S])
            minus_top, total, inverse = buf("minus_top", [P, NS]), buf("total", [P, NS]), buf("inverse", [P, NS])

            def pair(src):
                return tables[src][:].unsqueeze(1).to_broadcast([P, 2, SK])

            def wait(eng, name, value):
                if not (isinstance(value, int) and value <= 0):
                    eng.wait_ge(s[name], value)

            def all_tiles(eng, tile):
                tile(0, 0, True, False)
                with eng.Fori(0, NT // 2 - 1) as u:
                    tile(2 * u + 1, 1, False, False)
                    tile(2 * u + 2, 0, False, False)
                tile(NT - 1, 1, False, True)

            with nc.Block() as block:
                @block.sync
                def _(sp):
                    def load(t, b):
                        row = BT * t + b
                        sp.dma_start(C[b][:], ctx[row, 0:2 * P, :].rearrange("(c p) d -> p c d", p=P))\
                          .then_inc(s["ctx_loaded"][b], 16)
                        sp.dma_start(last_bc[b][:], ctx[row, SK - 1, :].partition_broadcast(P))\
                          .then_inc(s["ctx_loaded"][b], 16)
                    for b in range(BT):
                        load(0, b)
                    with sp.Fori(0, NT - 1) as t:
                        for b in range(BT):
                            sp.wait_ge(s["u_normed"], t * NS + NG * (b + 1))
                            load(t + 1, b)

                @block.gpsimd
                def _(pool):
                    for i in range(2):
                        nc.gpsimd.memset(QRd[i][:], 0.0).then_inc(s["zeroed"], 1)

                    def last_column(n, b):
                        pool.wait_ge(s["ctxT_ready"], BT * n + b + 1)
                        pool.sem_inc(s["held"], 1)
                        nc.gpsimd.tensor_copy(ctxT[:, b % BT, SK - 1:SK],
                                              last_rows_T[:, n + b // BT, b % BT:b % BT + 1]).then_inc(s["last_kept"], 1)

                    def tile(n, parity, first, last):
                        for q in range(NS):
                            b, g = divmod(q, NG)
                            if g == 0:
                                pool.wait_ge(s["ctx_loaded"][b], 32 * n + 32)
                            if g == 2 and not (last and b + 2 >= BT):
                                last_column(n, b + 2)
                            pool.wait_ge(s["inverse_ready"], NS * n + q + 1)
                            wait(pool, "u_normed", NS * n + q - 1)
                            pool.sem_inc(s["held"], 1)
                            nc.gpsimd.tensor_scalar(last_part[q % 2][:], last_bc[b][:], PR[q % 4][:, SK - 1:SK],
                                                    inverse[:, q:q + 1], ALU.mult, ALU.mult)\
                              .then_inc(s["last_part_ready"], 1)

                    last_column(0, 0)
                    last_column(0, 1)
                    all_tiles(pool, tile)

                @block.vector
                def _(dve):
                    def hidden(n):
                        nc.vector.scalar_tensor_tensor(H[:], X[:, n, :], core.rstd[:, n, :], norm_row[:],
                                                       ALU.mult, ALU.mult).then_inc(s["h_ready"], 1)

                    def key_rope(step, b, half):
                        return Rope(nc, step, PS[:, 0:2, 0:SK], keep[:], pair("cos_k"), pair("sin_k"),
                                    KR[b % 2][:, 2 * half:2 * half + 2, :], SWAP_HALVES)

                    def keys_first(step, n, b, half):
                        dve.wait_ge(s["k_ready"], NK * n + 2 * b + half + 1)
                        wait(dve, "k_turned", NK * n + 2 * b + half)
                        key_rope(step, b, half).first()

                    def keys_second(step, n, b, half):
                        key_rope(step, b, half).second().then_inc(s["k_turned"], 1)

                    def query_rope(step, bank):
                        view = lambda a: a.rearrange("p (m i) -> p m i", i=S)
                        bc = lambda a: tables[a][:].unsqueeze(1).to_broadcast([P, NG * BT, S])
                        return Rope(nc, step, view(PS[:, bank, :]), view(keep_q[:]), bc("cos_q"), bc("sin_q"),
                                    view(QR[:].rearrange("p g n -> p (g n)")), SWAP_HALVES)

                    def add_out(step, n):
                        dve.wait_ge(s["out_ready"], n + 1)
                        nc.vector.tensor_tensor(X[:, n, :], X[:, n, :], PS[:, 6, 0:D], ALU.add)\
                          .then_inc(s["x_added"], 1)
                        dve.wait_ge(s["x_added"], n + 1)
                        step.go(nc.vector.tensor_tensor(X[:, n, :], X[:, n, :], bias_row[:], ALU.add))

                    def tile(n, parity, first, last):
                        step = Steps(dve, s["dve_steps"], 2 * KEEP_K + KEEP_Q + n * TILE_STEPS - (0 if first else ADD))
                        for q in range(NS + 2 * last):
                            b, g = divmod(q, NG)
                            if q < NS:
                                dve.wait_ge(s["scores_ready"], NS * n + q + 1)
                                nc.vector.tensor_reduce(minus_top[:, q:q + 1], PS[:, 2 + q % 2, 0:SK], AX.X, ALU.max,
                                                        negate=True).then_inc(s["top_ready"], 1)
                                if not (last and b + 1 == BT):
                                    (keys_first, keys_second)[g % 2](step, n, b + 1, g // 2)
                            if (q >= 1 or not first) and q <= NS:
                                r = (q - 1) % NS
                                dve.wait_ge(s["exp_done"], NS * n + q)
                                nc.vector.reciprocal(inverse[:, r:r + 1], total[:, r:r + 1])\
                                  .then_inc(s["inverse_ready"], 1)
                            if q >= 2 or not first:
                                r = (q - 2) % NS
                                dve.wait_ge(s["u_ready"], NS * n + q - 1)
                                dve.wait_ge(s["last_part_ready"], NS * n + q - 1)
                                dve.wait_ge(s["inverse_ready"], NS * n + q - 1)
                                wait(dve, "uT_ready", NS * n + q - 3)
                                nc.vector.scalar_tensor_tensor(U[q % 2][:], PS[:, 5, 0:D], inverse[:, r:r + 1],
                                                               last_part[q % 2][:], ALU.mult,
                                                               ALU.add).then_inc(s["u_normed"], 1)
                            if q == 4 and not last:
                                hidden(n + 1)
                            if q == 4 and not first:
                                add_out(step, n - 1)
                            if q == 8 and not last:
                                dve.wait_ge(s["rot_ready"], n + 2)
                                query_rope(step, 6).first()
                            if q == 9 and not last:
                                query_rope(step, 6).second().then_inc(s["q_turned"], 1)
                        assert step.n == TILE_STEPS - ADD * first - (2 * KEEP_K + KEEP_Q) * last

                    step = Steps(dve, s["dve_steps"], 0)
                    hidden(0)
                    keys_first(step, 0, 0, 0)
                    keys_second(step, 0, 0, 0)
                    dve.wait_ge(s["rot_ready"], 1)
                    query_rope(step, 5).first()
                    query_rope(step, 5).second().then_inc(s["q_turned"], 1)
                    keys_first(step, 0, 0, 1)
                    keys_second(step, 0, 0, 1)
                    all_tiles(dve, tile)
                    add_out(step, NT - 1)

                @block.scalar
                def _(act):
                    def keep_ctxT(n, b):
                        act.wait_ge(s["ctxT_ready"], BT * n + b + 1)
                        nc.scalar.activation(ctxT[:, b % BT, 0:2 * P], PS[:, 6, 0:2 * P],
                                             ACT.Copy).then_inc(s["ctxT_kept"], 1)

                    def keep_hT(n, bank):
                        act.wait_ge(s["hT_ready"], n + 1)
                        nc.scalar.activation(HT[:], PS[:, bank, 0:P], ACT.Copy).then_inc(s["hT_kept"], 1)

                    def keep_plain(n, parity, g, bank):
                        act.wait_ge(s["q_plain_ready"], NG * n + g + 1)
                        nc.scalar.activation(QN[parity][:, g].rearrange("p b h i -> p h b i"),
                                             PS[:, bank, :].rearrange("p (h b i) -> p h b i", h=HG, b=BT),
                                             ACT.Copy, scale=DH ** -0.5).then_inc(s["q_plain_kept"], 1)

                    def spread(n, parity, h):
                        act.wait_ge(s["q_turned"], n + 1)
                        r = slice(32 * h, 32 * h + 32)
                        nc.scalar.activation(QRd[parity][r, :, :, h, :], QR[r].rearrange(
                            "p g (b i) -> p g b i", b=BT), ACT.Copy).then_inc(s["q_rot_spread"], 1)

                    def tile(n, parity, first, last):
                        for q in range(NS + 3 * last):
                            b, g = divmod(q, NG)
                            if q < NS:
                                act.wait_ge(s["top_ready"], NS * n + q + 1)
                                wait(act, "pT_ready", NS * n + q - 3)
                                wait(act, "last_part_ready", NS * n + q - 3)
                                nc.scalar.activation(PR[q % 4][:], PS[:, 2 + q % 2, 0:SK], ACT.Exp,
                                                     bias=minus_top[:, q:q + 1],
                                                     accum_out=total[:, q:q + 1]).then_inc(s["exp_done"], 1)
                            if (1 <= q or not first) and q <= NS:
                                act.wait_ge(s["pT_ready"], NS * n + q)
                                wait(act, "u_ready", NS * n + q - 2)
                                nc.scalar.activation(PT[(q - 1) % 2][:].rearrange("p c n -> p (c n)"),
                                                     PS[:, 4, 0:2 * P], ACT.Copy).then_inc(s["pT_kept"], 1)
                            if q >= 3 or not first:
                                act.wait_ge(s["uT_ready"], NS * n + q - 2)
                                pb, pg = divmod((q - 3) % NS, NG)
                                nc.scalar.activation(UT[:, pg * HG:(pg + 1) * HG, pb, :],
                                                     PS[:, 7, 0:P].rearrange("p (h i) -> p h i", i=S),
                                                     ACT.Copy).then_inc(s["uT_kept"], 1)
                            if g == 2 and b < BT and not (last and b + 2 >= BT):
                                keep_ctxT(n, b + 2)
                            if not last:
                                if q == 5:
                                    keep_hT(n + 1, 6)
                                if q in PLAIN_AT:
                                    keep_plain(n + 1, 1 - parity, PLAIN_AT.index(q), 6)
                                if 10 <= q < 10 + HG:
                                    spread(n + 1, 1 - parity, q - 10)

                    act.wait_ge(s["zeroed"], 2)
                    keep_ctxT(0, 0)
                    keep_hT(0, 7)
                    for g in range(NG):
                        keep_plain(0, 0, g, (2, 3, 4, 7)[g])
                    for h in range(HG):
                        spread(0, 0, h)
                    keep_ctxT(0, 1)
                    all_tiles(act, tile)

                @block.tensor
                def _(pe):
                    def turn_ctx(n, b):
                        pe.wait_ge(s["ctx_loaded"][b % BT], 32 * (n + b // BT) + 32)
                        for c in range(2):
                            ins = nc.tensor.transpose(PS[:, 6, c * P:(c + 1) * P], C[b % BT][:, c, :], core.ident[:])
                        ins.then_inc(s["ctxT_ready"], 1)

                    def keys(n, b, half):
                        pe.wait_ge(s["ctxT_kept"], BT * n + b + 1)
                        pe.wait_ge(s["last_kept"], BT * n + b + 1)
                        wait(pe, "k_turned", NK * n + 2 * b + half)
                        for i in range(2):
                            g = 2 * half + i
                            ins = nc.tensor.matmul(PS[:, i, 0:SK], W["ckR"][:, g * P:(g + 1) * P],
                                                   ctxT[:, b % BT, :], start=True, stop=True)
                        ins.then_inc(s["k_ready"], 1)

                    def turn_h(n, bank):
                        pe.wait_ge(s["h_ready"], n + 1)
                        nc.tensor.transpose(PS[:, bank, 0:P], H[:], core.ident[:]).then_inc(s["hT_ready"], 1)

                    def rotary_queries(bank):
                        for g in range(NG):
                            ins = nc.tensor.matmul(PS[:, bank, g * P:(g + 1) * P], W["cqR"][:, g * P:(g + 1) * P],
                                                   HT[:], start=True, stop=True)
                        ins.then_inc(s["rot_ready"], 1)

                    def plain_queries(g, bank):
                        for h in range(HG):
                            ins = nc.tensor.matmul(PS[:, bank, h * P:(h + 1) * P], QK[:, g * HG + h, :], HT[:],
                                                   start=True, stop=True)
                        ins.then_inc(s["q_plain_ready"], 1)

                    def out_tile(n):
                        pe.wait_ge(s["uT_kept"], NS * n + NS)
                        for h in range(NH):
                            ins = nc.tensor.matmul(PS[:, 6, 0:D], UT[:, h].rearrange("p b i -> p (b i)"),
                                                   VO[:, h, :], start=(h == 0), stop=(h == NH - 1))
                        ins.then_inc(s["out_ready"], 1)

                    def bank6(n, q, last):
                        if q == 2:
                            pe.wait_ge(s["q_plain_kept"], NG * n + NG)
                            turn_ctx(n, 2)
                        if q == 3 and not (isinstance(n, int) and n == 0):
                            pe.wait_ge(s["ctxT_kept"], BT * n + 3)
                            out_tile(n - 1)
                        if q == 5 and not last:
                            pe.wait_ge(s["ctxT_kept"], BT * n + 3)
                            wait(pe, "x_added", n)
                            turn_h(n + 1, 6)
                        if q == 6:
                            if last:
                                pe.wait_ge(s["x_added"], n)
                            else:
                                pe.wait_ge(s["hT_kept"], n + 2)
                            turn_ctx(n, 3)
                        if last:
                            return
                        if q == 7:
                            pe.wait_ge(s["ctxT_kept"], BT * n + 4)
                            rotary_queries(6)
                        if q == 10:
                            pe.wait_ge(s["q_turned"], n + 2)
                            turn_ctx(n, 4)
                        if q == 14:
                            pe.wait_ge(s["q_plain_kept"], NG * n + NG + 3)
                            turn_ctx(n, 5)
                        if q in PLAIN_AT:
                            g = PLAIN_AT.index(q)
                            if g in (0, 3):
                                pe.wait_ge(s["ctxT_kept"], BT * n + (5 if g == 0 else 6))
                            else:
                                pe.wait_ge(s["q_plain_kept"], NG * n + NG + g)
                            plain_queries(g, 6)

                    def tile(n, parity, first, last):
                        for q in range(NS + 3 * last):
                            b, g = divmod(q, NG)
                            if q < NS:
                                if q == 0:
                                    pe.wait_ge(s["q_rot_spread"], HG * n + HG)
                                if first and q == 0:
                                    pe.wait_ge(s["q_plain_kept"], NG)
                                elif b == 0:
                                    pe.wait_ge(s["q_plain_kept"], NG * n + g + 1)
                                if g % 2 == 0:
                                    pe.wait_ge(s["k_turned"], NK * n + 2 * b + g // 2 + 1)
                                wait(pe, "exp_done", NS * n + q - 1)
                                out = PS[:, 2 + q % 2, 0:SK]
                                nc.tensor.matmul(out, QN[parity][:, g, b].rearrange("p h i -> p (h i)"),
                                                 ctxT[:, b, :], start=True, stop=False)
                                nc.tensor.matmul(out, QRd[parity][:, g, b].rearrange("p h i -> p (h i)"),
                                                 KR[b % 2][:, g, :], start=False, stop=True)\
                                  .then_inc(s["scores_ready"], 1)
                                if g % 2 == 0 and not (last and b + 1 == BT):
                                    keys(n, b + 1, g // 2)
                                bank6(n, q, last)
                            if (1 <= q or not first) and q <= NS:
                                pe.wait_ge(s["exp_done"], NS * n + q)
                                wait(pe, "pT_kept", NS * n + q - 1)
                                for c in range(2):
                                    ins = nc.tensor.transpose(PS[:, 4, c * P:(c + 1) * P],
                                                              PR[(q - 1) % 4][:, c * P:(c + 1) * P], core.ident[:])
                                ins.then_inc(s["pT_ready"], 1)
                            if (2 <= q or not first) and q <= NS + 1:
                                pe.wait_ge(s["pT_kept"], NS * n + q - 1)
                                wait(pe, "u_normed", NS * n + q - 2)
                                for c in range(2):
                                    ins = nc.tensor.matmul(PS[:, 5, 0:D], PT[q % 2][:, c, :],
                                                           C[(q - 2) % NS // NG][:, c, :], start=(c == 0),
                                                           stop=(c == 1))
                                ins.then_inc(s["u_ready"], 1)
                            if q >= 3 or not first:
                                pe.wait_ge(s["u_normed"], NS * n + q - 2)
                                wait(pe, "uT_kept", NS * n + q - 3)
                                nc.tensor.transpose(PS[:, 7, 0:P], U[(q - 3) % 2][:], core.ident[:])\
                                  .then_inc(s["uT_ready"], 1)

                    pe.wait_ge(s["zeroed"], 2)
                    turn_ctx(0, 0)
                    turn_h(0, 7)
                    keys(0, 0, 0)
                    pe.wait_ge(s["hT_kept"], 1)
                    rotary_queries(5)
                    for g in range(NG):
                        plain_queries(g, (2, 3, 4, 7)[g])
                    turn_ctx(0, 1)
                    keys(0, 0, 1)
                    all_tiles(pe, tile)
                    pe.wait_ge(s["ctxT_kept"], BT * NT)
                    out_tile(NT - 1)


class FeedForward:

    def __init__(self, core):
        self.core = core
        names = ("h_ready", "hT_ready", "hT_kept", "hidden_ready", "gelu_done", "out_ready", "added", "done")
        self.sems = {n: core.sem("ffn_" + n) for n in names}

    def run(self, W1, W2, b1, norm_row, bias_row):
        core, nc, PS, s = self.core, self.core.nc, self.core.PS, self.sems
        NU = NT // 4
        X4 = core.X[:].rearrange("p (u j) d -> p u j d", j=4)
        R4 = core.rstd[:].rearrange("p (u j) o -> p u j o", j=4)
        with ExitStack() as st:
            H = core.buffer(st, "ffn_H", [P, 4, D])
            HT = core.buffer(st, "ffn_HT", [P, 4 * P])
            G = [core.buffer(st, f"ffn_G{i}", [P, FC, 4 * P]) for i in range(2)]
            with nc.Block() as block:
                @block.vector
                def _(dve):
                    def front(n):
                        for j in range(4):
                            nc.vector.scalar_tensor_tensor(H[:, j, :], X4[:, n, j, :], R4[:, n, j, :], norm_row[:],
                                                           ALU.mult, ALU.mult).then_inc(s["h_ready"], 1)
                        dve.wait_ge(s["hT_ready"], n + 1)
                        nc.vector.tensor_copy(HT[:], PS[:, 0, :]).then_inc(s["hT_kept"], 1)

                    def tile(n, parity, last):
                        if not last:
                            front(n + 1)
                        dve.wait_ge(s["out_ready"], n + 1)
                        nc.vector.tensor_tensor(X4[:, n], X4[:, n], PS[:, 5, :].rearrange("p (j d) -> p j d", j=4),
                                                ALU.add).then_inc(s["added"], 1)
                        dve.wait_ge(s["added"], n + 1)
                        nc.vector.tensor_tensor(X4[:, n], X4[:, n], bias_row[:].unsqueeze(1).to_broadcast([P, 4, D]),
                                                ALU.add).then_inc(s["done"], 1)

                    front(0)
                    in_pairs(dve, NU, tile)
                    dve.wait_ge(s["done"], NU)

                @block.scalar
                def _(act):
                    def tile(n, parity, last):
                        for c in range(FC):
                            act.wait_ge(s["hidden_ready"], FC * n + c + 1)
                            nc.scalar.activation(G[parity][:, c, :], PS[:, 1 + c, :], ACT.Gelu,
                                                 bias=b1[:, c:c + 1]).then_inc(s["gelu_done"], 1)

                    in_pairs(act, NU, tile)

                @block.tensor
                def _(pe):
                    def front(n, first):
                        pe.wait_ge(s["h_ready"], 4 * n + 4)
                        for j in range(4):
                            ins = nc.tensor.transpose(PS[:, 0, j * P:(j + 1) * P], H[:, j, :], core.ident[:])
                        ins.then_inc(s["hT_ready"], 1)
                        pe.wait_ge(s["hT_kept"], n + 1)
                        for c in range(FC):
                            if not first:
                                pe.wait_ge(s["gelu_done"], FC * (n - 1) + c + 1)
                            nc.tensor.matmul(PS[:, 1 + c, :], W1[:, c * P:(c + 1) * P], HT[:],
                                             start=True, stop=True).then_inc(s["hidden_ready"], 1)

                    def tile(n, parity, last):
                        if not last:
                            front(n + 1, False)
                        else:
                            pe.wait_ge(s["added"], n)
                        pe.wait_ge(s["gelu_done"], FC * n + FC)
                        for j in range(4):
                            for c in range(FC):
                                ins = nc.tensor.matmul(PS[:, 5, j * D:(j + 1) * D],
                                                       G[parity][:, c, j * P:(j + 1) * P],
                                                       W2[:, c, :], start=(c == 0), stop=(c == FC - 1))
                        ins.then_inc(s["out_ready"], 1)

                    front(0, True)
                    in_pairs(pe, NU, tile)


def project(core, st, HB):
    nc, PS, dram = core.nc, core.PS, core.dram
    NU = NT // 4
    Statistics(core, "rms_out").run(core.X, True)
    X4 = core.X[:].rearrange("p (u j) d -> p u j d", j=4)
    B4 = HB[:].rearrange("p (u j) d -> p u j d", j=4)
    R4 = core.rstd[:].rearrange("p (u j) o -> p u j o", j=4)
    loaded, h_ready, hT_ready, hT_kept, out_ready, added, done = (
        core.sem("proj_" + n) for n in ("loaded", "h_ready", "hT_ready", "hT_kept", "out_ready", "added", "done"))
    H = core.buffer(st, "proj_H", [P, 4, D])
    HT = core.buffer(st, "proj_HT", [P, 4 * P])
    Wp = core.buffer(st, "proj_W", [P, D])
    norm_row, bias_row = core.buffer(st, "proj_norm", [P, D]), core.buffer(st, "proj_bias", [P, D])
    with nc.Block() as block:
        @block.sync
        def _(sp):
            for dst, src in ((norm_row[:], dram["norm_out_w"].partition_broadcast(P)), (Wp[:], dram["proj_w"]),
                             (bias_row[:], dram["proj_b"].partition_broadcast(P)), (HB[:], core.x_tiles)):
                sp.dma_start(dst, src).then_inc(loaded, 16)
            sp.wait_ge(loaded, 64)

        @block.vector
        def _(dve):
            dve.wait_ge(loaded, 64)
            with dve.Fori(0, NU) as u:
                for j in range(4):
                    nc.vector.scalar_tensor_tensor(H[:, j, :], X4[:, u, j, :], R4[:, u, j, :], norm_row[:],
                                                   ALU.mult, ALU.mult).then_inc(h_ready, 1)
                dve.wait_ge(h_ready, 4 * u + 4)
                dve.wait_ge(out_ready, u + 1)
                nc.vector.tensor_tensor(X4[:, u], B4[:, u], PS[:, 1, :].rearrange("p (j d) -> p j d", j=4),
                                        ALU.add).then_inc(added, 1)
                dve.wait_ge(added, u + 1)
                nc.vector.tensor_tensor(X4[:, u], X4[:, u], bias_row[:].unsqueeze(1).to_broadcast([P, 4, D]),
                                        ALU.add).then_inc(done, 1)
                dve.wait_ge(done, u + 1)

        @block.scalar
        def _(act):
            with act.Fori(0, NU) as u:
                act.wait_ge(hT_ready, u + 1)
                nc.scalar.activation(HT[:], PS[:, 0, :], ACT.Copy).then_inc(hT_kept, 1)

        @block.tensor
        def _(pe):
            pe.wait_ge(loaded, 64)
            with pe.Fori(0, NU) as u:
                pe.wait_ge(h_ready, 4 * u + 4)
                for j in range(4):
                    ins = nc.tensor.transpose(PS[:, 0, j * P:(j + 1) * P], H[:, j, :], core.ident[:])
                ins.then_inc(hT_ready, 1)
                pe.wait_ge(hT_kept, u + 1)
                for j in range(4):
                    ins = nc.tensor.matmul(PS[:, 1, j * D:(j + 1) * D], HT[:, j * P:(j + 1) * P], Wp[:],
                                           start=True, stop=True)
                ins.then_inc(out_ready, 1)


class SmallAttention:

    def __init__(self, core, st):
        self.core = core
        buf = lambda name, shape: core.buffer(st, "small_" + name, shape)
        self.W = {n: buf("W" + n, [P, D]) for n in "qkvo"}
        self.rows = {n: buf("row_" + n, [P, D]) for n in ("bv", "bo", "g", "b")}
        self.cols = buf("cols", [P, 2])
        self.tables = {n: buf(n, [P, S]) for n in ("cos8_q", "sin8_q", "cos8_k", "sin8_k")}
        self.pick = buf("pick", [P, HG])
        self.H, self.HT = buf("H", [P, D]), buf("HT", [P, P])
        self.Q, self.K, self.V, self.keep = (buf(n, [P, P]) for n in ("Q", "K", "V", "keep"))
        self.Qd = buf("Qd", [P, BT, HG, S])
        self.top, self.total, self.inverse = (buf(n, [P, NG, BT]) for n in ("top", "total", "inverse"))
        self.PR, self.PT = buf("PR", [P, NG, P]), buf("PT", [P, NG, P])
        self.picked, self.OT = buf("picked", [P, BT, HG, S]), buf("OT", [P, BT, S])

    def run(self, X, rotary):
        core, nc, PS, dram = self.core, self.core.nc, self.core.PS, self.core.dram
        name = "b_" if rotary else "c_"
        (loaded, h_ready, hT_ready, hT_kept, qkv_ready, q_spread, k_ready, v_kept, scores_ready, shifted, exp_done,
         probs_ready, pT_ready, pT_kept, o_ready, o_picked, out_ready, steps, held) = (core.sem(name + n) for n in (
             "loaded", "h_ready", "hT_ready", "hT_kept", "qkv_ready", "q_spread", "k_ready", "v_kept", "scores_ready",
             "shifted", "exp_done", "probs_ready", "pT_ready", "pT_kept", "o_ready", "o_picked", "out_ready", "steps", "held"))
        W, rows, tables, H, HT = self.W, self.rows, self.tables, self.H, self.HT
        loads = [(W[n][:], dram[name + "W" + n]) for n in "qkvo"]
        if rotary:
            loads += [(tables[n][:], dram[n]) for n in tables] + [(self.pick[:], dram["pick"])]
        else:
            loads += [(rows[n][:], dram["c_row_" + n].partition_broadcast(P)) for n in rows]
            loads += [(self.cols[:], dram["c_cols"])]
        need = 16 * len(loads)
        SC = PS[:, 0:4, 0:P].rearrange("p g (b j) -> p g b j", j=S)
        FRONT_STEPS, BACK_STEPS = (7, 5) if rotary else (3, 6)

        def per_row(v):
            return v[:].unsqueeze(3).to_broadcast([P, NG, BT, S])

        def all_tiles(eng, tile):
            with eng.Fori(0, NT - 1) as n:
                tile(n, False)
            tile(NT - 1, True)

        with nc.Block() as block:
            @block.sync
            def _(sp):
                for dst, src in loads:
                    sp.dma_start(dst, src).then_inc(loaded, 16)

            @block.vector
            def _(dve):
                def hidden(step, n):
                    norm = nc.vector.tensor_scalar(H[:], X[:, n, :], core.mean_var[:, n, 0:1], core.rstd[:, n, :],
                                                   ALU.subtract, ALU.mult)
                    if rotary:
                        norm.then_inc(h_ready, 1)
                    else:
                        step(norm)
                        step(nc.vector.tensor_tensor(H[:], H[:], rows["g"][:], ALU.mult))
                        nc.vector.tensor_tensor(H[:], H[:], rows["b"][:], ALU.add).then_inc(h_ready, 1)

                def queries_keys(step, n):
                    view = lambda a: a.rearrange("p (b i) -> p b i", i=S)
                    dve.wait_ge(qkv_ready, n + 1)
                    for k, out in enumerate((self.Q, self.K)):
                        raw = PS[:, 6, k * P:(k + 1) * P]
                        if rotary:
                            bc = lambda a: tables[a][:].unsqueeze(1).to_broadcast([P, BT, S])
                            kind = "qk"[k]
                            rope = Rope(nc, step, view(raw), view(self.keep[:]), bc("cos8_" + kind),
                                        bc("sin8_" + kind), view(out[:]), SWAP_PAIRS)
                            rope.first()
                            done = rope.second()
                        else:
                            done = nc.vector.tensor_scalar(out[:], raw, self.cols[:, k:k + 1],
                                                           HD8 ** -0.5 if k == 0 else 1.0, ALU.add, ALU.mult)
                        if k == 0:
                            step(done)
                            for h in range(HG):
                                nc.vector.tensor_scalar(self.Qd[:, :, h, :], view(self.Q[:]), self.pick[:, h:h + 1],
                                                        None, ALU.mult).then_inc(q_spread, 1)
                        else:
                            done.then_inc(k_ready, 1)

                def values(n):
                    raw = PS[:, 6, 2 * P:3 * P]
                    if rotary:
                        nc.vector.tensor_copy(self.V[:], raw).then_inc(v_kept, 1)
                    else:
                        nc.vector.tensor_tensor(self.V[:], raw, rows["bv"][:], ALU.add).then_inc(v_kept, 1)

                def tile(n, last):
                    step = Steps(dve, steps, FRONT_STEPS + n * (FRONT_STEPS + BACK_STEPS))
                    if not last:
                        hidden(step, n + 1)
                    dve.wait_ge(scores_ready, n + 1)
                    step(nc.vector.tensor_reduce(self.top[:], SC, AX.X, ALU.max))
                    nc.vector.tensor_tensor(SC, SC, per_row(self.top), ALU.subtract).then_inc(shifted, 1)
                    dve.wait_ge(exp_done, n + 1)
                    step(nc.vector.tensor_reduce(self.total[:], SC, AX.X, ALU.add))
                    step(nc.vector.reciprocal(self.inverse[:], self.total[:]))
                    nc.vector.tensor_tensor(self.PR[:].rearrange("p g (b j) -> p g b j", j=S), SC,
                                            per_row(self.inverse), ALU.mult).then_inc(probs_ready, 1)
                    if not last:
                        queries_keys(step, n + 1)
                    dve.wait_ge(o_ready, n + 1)
                    step(nc.vector.tensor_tensor(self.picked[:], PS[:, 0:4, 0:P].rearrange("p b (h i) -> p b h i", i=S),
                                                 self.pick[:].unsqueeze(1).unsqueeze(3).to_broadcast([P, BT, HG, S]),
                                                 ALU.mult))
                    nc.vector.tensor_reduce(self.OT[:], self.picked[:].rearrange("p b h i -> p b i h"), AX.X,
                                            ALU.add).then_inc(o_picked, 1)
                    if not last:
                        values(n + 1)
                    dve.wait_ge(out_ready, n + 1)
                    step(nc.vector.tensor_tensor(X[:, n, :], X[:, n, :], PS[:, 7, 0:D], ALU.add))
                    if not rotary:
                        step(nc.vector.tensor_tensor(X[:, n, :], X[:, n, :], rows["bo"][:], ALU.add))
                    assert step.n == BACK_STEPS + (0 if last else FRONT_STEPS), step.n

                dve.wait_ge(loaded, need)
                step = Steps(dve, steps, 0)
                hidden(step, 0)
                queries_keys(step, 0)
                values(0)
                all_tiles(dve, tile)

            @block.scalar
            def _(act):
                def keep_hT(n):
                    act.wait_ge(hT_ready, n + 1)
                    nc.scalar.activation(HT[:], PS[:, 4, 0:P], ACT.Copy).then_inc(hT_kept, 1)

                def tile(n, last):
                    if not last:
                        keep_hT(n + 1)
                    act.wait_ge(shifted, n + 1)
                    nc.scalar.activation(SC, SC, ACT.Exp).then_inc(exp_done, 1)
                    act.wait_ge(pT_ready, n + 1)
                    nc.scalar.activation(self.PT[:].rearrange("p g n -> p (g n)"), PS[:, 5, :],
                                         ACT.Copy).then_inc(pT_kept, 1)

                keep_hT(0)
                all_tiles(act, tile)

            @block.tensor
            def _(pe):
                def front(n):
                    pe.wait_ge(h_ready, n + 1)
                    nc.tensor.transpose(PS[:, 4, 0:P], H[:], core.ident[:]).then_inc(hT_ready, 1)
                    pe.wait_ge(hT_kept, n + 1)
                    nc.tensor.matmul(PS[:, 6, 0:P], W["q"][:], HT[:], start=True, stop=True)
                    nc.tensor.matmul(PS[:, 6, P:2 * P], W["k"][:], HT[:], start=True, stop=True)
                    nc.tensor.matmul(PS[:, 6, 2 * P:3 * P], HT[:], W["v"][:], start=True,
                                     stop=True).then_inc(qkv_ready, 1)

                def tile(n, last):
                    pe.wait_ge(q_spread, HG * n + HG)
                    pe.wait_ge(k_ready, n + 1)
                    for b in range(BT):
                        for g in range(NG):
                            r = slice(32 * g, 32 * g + 32)
                            ins = nc.tensor.matmul(PS[:, g, b * S:(b + 1) * S],
                                                   self.Qd[r, b].rearrange("p h i -> p (h i)"),
                                                   self.K[r, b * S:(b + 1) * S], start=True, stop=True)
                    ins.then_inc(scores_ready, 1)
                    pe.wait_ge(v_kept, n + 1)
                    pe.sem_inc(held, 1)
                    if not last:
                        front(n + 1)
                    pe.wait_ge(probs_ready, n + 1)
                    for g in range(NG):
                        ins = nc.tensor.transpose(PS[:, 5, g * P:(g + 1) * P], self.PR[:, g, :], core.ident[:])
                    ins.then_inc(pT_ready, 1)
                    pe.wait_ge(pT_kept, n + 1)
                    pe.sem_inc(held, 1)
                    for g in range(NG):
                        for b in range(BT):
                            r, c = slice(32 * b, 32 * b + 32), slice(32 * g, 32 * g + 32)
                            ins = nc.tensor.matmul(PS[c, b, 0:P], self.V[r, c], self.PT[r, g, :],
                                                   start=True, stop=True)
                    ins.then_inc(o_ready, 1)
                    pe.wait_ge(o_picked, n + 1)
                    nc.tensor.matmul(PS[:, 7, 0:D], self.OT[:].rearrange("p b i -> p (b i)"), W["o"][:],
                                     start=True, stop=True).then_inc(out_ready, 1)

                pe.wait_ge(loaded, need)
                front(0)
                all_tiles(pe, tile)


def experts(core, st, HB):
    nc, PS, dram, X = core.nc, core.PS, core.dram, core.X
    buf = lambda name, shape: core.buffer(st, "moe_" + name, shape)
    H2T = buf("H2T", [P, NT, P])
    W1, W2 = buf("W1", [P, NE, FF]), buf("W2", [P, NE, FC, D])
    b1, b2 = buf("b1", [P, NE, FC]), buf("b2", [NE, D])
    Wr = buf("Wr", [P, NE])
    g_col, b_col = buf("g_col", [P, 1]), buf("b_col", [P, 1])
    upto, ones = buf("upto", [P, P]), buf("ones", [P, P])
    order = buf("order", [P, NE])
    H, HT = buf("H", [P, 4, D]), buf("HT", [P, 4 * P])
    L, E, PRB, EQ, M1, M2, C1, C2, A, A2, V1 = (buf(n, [P, NT, NE]) for n in (
        "logits", "exps", "probs", "equal", "first", "second", "place1", "place2", "scan_a", "scan_b", "kept"))
    GATE = buf("gate", [P, NT, NE])
    row, row2, row3 = buf("row", [P, NT]), buf("row2", [P, NT]), buf("row3", [P, NT])
    sems = {n: core.sem("moe_" + n) for n in (
        "loaded", "normed", "h_ready", "hT_ready", "hT_kept", "hT_kept_all", "logits_ready", "logits_kept",
        "shifted", "exp_done", "steps", "masks_ready", "counts_ready", "gates_ready",
        "gT_ready", "gT_kept", "base_ready", "base_added", "base_all", "hidden_ready", "relu_act", "relu_dve",
        "y_ready", "y_added", "stored")}
    S_ = lambda n: sems[n]
    loads = [(W1[:], dram["e_w1"].rearrange("e d f -> d e f")),
             (W2[:], dram["e_w2"].rearrange("e (c p) d -> p e c d", p=P)),
             (b1[:], dram["e_b1T"]), (b2[:], dram["e_b2"]), (Wr[:], dram["wr"]),
             (g_col[:], dram["ln2_g"]), (b_col[:], dram["ln2_b"]),
             (upto[:], dram["upto"]), (ones[:], dram["ones"]), (order[:], dram["order"])]

    NU = NT // 4
    HT4 = H2T[:].rearrange("p (u j) n -> p u (j n)", j=4)
    X4 = X[:].rearrange("p (u j) d -> p u j d", j=4)
    HB4 = HB[:].rearrange("p (u j) d -> p u j d", j=4)
    G4, L4 = (a[:].rearrange("p (u j) e -> p u j e", j=4) for a in (GATE, L))
    MV4, R4 = (a[:].rearrange("p (u j) o -> p u j o", j=4) for a in (core.mean_var, core.rstd))

    with nc.Block() as block:
        @block.sync
        def _(sp):
            for dst, src in loads[2:] + loads[:2]:
                sp.dma_start(dst, src).then_inc(S_("loaded"), 16)
            sp.wait_ge(S_("loaded"), 16 * len(loads))

        @block.vector
        def _(dve):
            dve.wait_ge(S_("loaded"), 16 * len(loads))
            with dve.Fori(0, NU) as u:
                for j in range(4):
                    nc.vector.tensor_scalar(H[:, j, :], HB4[:, u, j, :], MV4[:, u, j, :], R4[:, u, j, :],
                                            ALU.subtract, ALU.mult).then_inc(S_("h_ready"), 1)
                dve.wait_ge(S_("hT_ready"), u + 1)
                nc.vector.tensor_scalar(HT[:], PS[:, 0, :], g_col[:], b_col[:], ALU.mult,
                                        ALU.add).then_inc(S_("hT_kept"), 1)
                dve.wait_ge(S_("logits_ready"), u + 1)
                nc.vector.tensor_copy(L4[:, u], PS[:, 1, 0:4 * NE].rearrange("p (j e) -> p j e", j=4))\
                  .then_inc(S_("logits_kept"), 1)
                dve.wait_ge(S_("hT_kept_all"), u + 1)
                dve.wait_ge(S_("logits_kept"), u + 1)

        @block.scalar
        def _(act):
            with act.Fori(0, NU) as u:
                act.wait_ge(S_("hT_kept"), u + 1)
                nc.scalar.activation(HT4[:, u, :], HT[:], ACT.Copy).then_inc(S_("hT_kept_all"), 1)

        @block.tensor
        def _(pe):
            pe.wait_ge(S_("loaded"), 16 * len(loads))
            with pe.Fori(0, NU) as u:
                pe.wait_ge(S_("h_ready"), 4 * u + 4)
                for j in range(4):
                    ins = nc.tensor.transpose(PS[:, 0, j * P:(j + 1) * P], H[:, j, :], core.ident[:])
                ins.then_inc(S_("hT_ready"), 1)
                pe.wait_ge(S_("hT_kept"), u + 1)
                for j in range(4):
                    ins = nc.tensor.matmul(PS[:, 1, j * NE:(j + 1) * NE], HT[:, j * P:(j + 1) * P], Wr[:],
                                           start=True, stop=True)
                ins.then_inc(S_("logits_ready"), 1)

    def each(v):
        return v[:].unsqueeze(2).to_broadcast([P, NT, NE])

    with nc.Block() as block:
        @block.vector
        def _(dve):
            step = Steps(dve, S_("steps"), 0)
            tt = lambda o, a, b, op: step(nc.vector.tensor_tensor(o, a, b, op))
            orders = order[:].unsqueeze(1).to_broadcast([P, NT, NE])

            def one_hot(dst, values):
                step(nc.vector.tensor_reduce(row[:], values, AX.X, ALU.max))
                tt(EQ[:], values, each(row), ALU.is_equal)
                tt(EQ[:], EQ[:], orders, ALU.mult)
                step(nc.vector.tensor_reduce(row[:], EQ[:], AX.X, ALU.max))
                tt(dst, EQ[:], each(row), ALU.is_equal)

            step(nc.vector.tensor_reduce(row[:], L[:], AX.X, ALU.max))
            nc.vector.tensor_tensor(E[:], L[:], each(row), ALU.subtract).then_inc(S_("shifted"), 1)
            dve.wait_ge(S_("exp_done"), 1)
            step(nc.vector.tensor_reduce(row[:], E[:], AX.X, ALU.add))
            step(nc.vector.reciprocal(row2[:], row[:]))
            tt(PRB[:], E[:], each(row2), ALU.mult)
            one_hot(M1[:], PRB[:])
            step(nc.vector.tensor_scalar(EQ[:], M1[:], -3.0e38, None, ALU.mult))
            tt(L[:], L[:], EQ[:], ALU.add)
            one_hot(M2[:], L[:])
            dve.wait_ge(S_("steps"), step.n)
            nc.vector.tensor_copy(V1[:], M2[:]).then_inc(S_("masks_ready"), 1)
            dve.wait_ge(S_("counts_ready"), 1)

            def places(dst, k):
                step(nc.vector.tensor_copy(A[:], PS[:, 2 * k + 1, 0:NT * NE]))
                a, b = A, A2
                shift = 1
                while shift < NT:
                    step(nc.vector.tensor_copy(b[:, 0:shift, :], a[:, 0:shift, :]))
                    tt(b[:, shift:NT, :], a[:, shift:NT, :], a[:, 0:NT - shift, :], ALU.add)
                    a, b = b, a
                    shift *= 2
                tt(dst, a[:], PS[:, 2 * k + 1, 0:NT * NE].rearrange("p (t e) -> p t e", e=NE), ALU.subtract)
                tt(dst, dst, PS[:, 2 * k, 0:NT * NE].rearrange("p (t e) -> p t e", e=NE), ALU.add)
                return a

            a = places(C1[:], 0)
            step(nc.vector.tensor_copy(V1[:, 0, :], a[:, NT - 1, :]))
            places(C2[:], 1)
            tt(C2[:], C2[:], V1[:, 0:1, :].to_broadcast([P, NT, NE]), ALU.add)
            for m, c in ((M1, C1), (M2, C2)):
                step(nc.vector.tensor_scalar(c[:], c[:], float(CAP), None, ALU.is_le))
                tt(m[:], m[:], c[:], ALU.mult)
            for m, r in ((M1, row2), (M2, row3)):
                tt(EQ[:], PRB[:], m[:], ALU.mult)
                step(nc.vector.tensor_reduce(r[:], EQ[:], AX.X, ALU.add))
            tt(row[:], row2[:], row3[:], ALU.add)
            step(nc.vector.tensor_scalar(row[:], row[:], float(np.finfo(np.float32).eps), None, ALU.max))
            step(nc.vector.reciprocal(row[:], row[:]))
            for m, r in ((M1, row2), (M2, row3)):
                tt(r[:], r[:], row[:], ALU.mult)
                tt(m[:], m[:], each(r), ALU.mult)
            tt(GATE[:], M1[:], M2[:], ALU.add)
            step(nc.vector.tensor_scalar(GATE[:], GATE[:], 1.0 - 0.2, None, ALU.mult))

        @block.scalar
        def _(act):
            act.wait_ge(S_("shifted"), 1)
            nc.scalar.activation(E[:], E[:], ACT.Exp).then_inc(S_("exp_done"), 1)

        @block.tensor
        def _(pe):
            pe.wait_ge(S_("masks_ready"), 1)
            for k, m in enumerate((M1, M2)):
                flat = m[:].rearrange("p t e -> p (t e)")
                nc.tensor.matmul(PS[:, 2 * k, 0:NT * NE], upto[:], flat, start=True, stop=True)
                ins = nc.tensor.matmul(PS[:, 2 * k + 1, 0:NT * NE], ones[:], flat, start=True, stop=True)
            ins.then_inc(S_("counts_ready"), 1)

    GT = buf("gT", [NE, 4 * P])
    G8 = buf("g8", [P, 4, NE])
    with nc.Block() as block:
        @block.vector
        def _(dve):
            with dve.Fori(0, NU) as u:
                nc.vector.tensor_copy(G8[:], G4[:, u]).then_inc(S_("gates_ready"), 1)
                nc.vector.tensor_tensor(X4[:, u], X4[:, u], HB4[:, u], ALU.add).then_inc(S_("base_added"), 1)
                dve.wait_ge(S_("base_added"), u + 1)
                dve.wait_ge(S_("base_ready"), u + 1)
                nc.vector.tensor_tensor(X4[:, u], X4[:, u], PS[:, 1, :].rearrange("p (j d) -> p j d", j=4),
                                        ALU.add).then_inc(S_("base_all"), 1)
                dve.wait_ge(S_("base_all"), u + 1)

        @block.scalar
        def _(act):
            with act.Fori(0, NU) as u:
                act.wait_ge(S_("gT_ready"), u + 1)
                nc.scalar.activation(GT[:], PS[0:NE, 0, :], ACT.Copy).then_inc(S_("gT_kept"), 1)

        @block.tensor
        def _(pe):
            with pe.Fori(0, NU) as u:
                pe.wait_ge(S_("gates_ready"), u + 1)
                for j in range(4):
                    ins = nc.tensor.transpose(PS[0:NE, 0, j * P:(j + 1) * P], G8[:, j, :], core.ident[:])
                ins.then_inc(S_("gT_ready"), 1)
                pe.wait_ge(S_("gT_kept"), u + 1)
                for j in range(4):
                    ins = nc.tensor.matmul(PS[:, 1, j * D:(j + 1) * D], GT[:, j * P:(j + 1) * P], b2[:],
                                           start=True, stop=True)
                ins.then_inc(S_("base_ready"), 1)

    out4 = dram["out"].rearrange("(u j b) s d -> u (b s) j d", j=4, b=BT)
    G = [buf(f"hidden{i}", [P, FC, 4 * P]) for i in range(2)]
    with nc.Block() as block:
        @block.tensor
        def _(pe):
            with pe.Fori(0, NU) as u:
                def up(e):
                    for c in range(FC):
                        if e >= 1:
                            pe.wait_ge(S_(("relu_act", "relu_dve")[c % 2]), 2 * NE * u + 2 * (e - 1) + c // 2 + 1)
                        nc.tensor.matmul(PS[:, 2 + c, :], W1[:, e, c * P:(c + 1) * P], HT4[:, u, :],
                                         start=True, stop=True).then_inc(S_("hidden_ready"), 1)
                up(0)
                for e in range(NE):
                    if e + 1 < NE:
                        up(e + 1)
                    pe.wait_ge(S_("relu_act"), 2 * NE * u + 2 * e + 2)
                    pe.wait_ge(S_("relu_dve"), 2 * NE * u + 2 * e + 2)
                    if e >= 2:
                        pe.wait_ge(S_("y_added"), 4 * (NE * u + e - 1))
                    for j in range(4):
                        for c in range(FC):
                            ins = nc.tensor.matmul(PS[:, 6 + e % 2, j * D:(j + 1) * D],
                                                   G[e % 2][:, c, j * P:(j + 1) * P], W2[:, e, c, :],
                                                   start=(c == 0), stop=(c == FC - 1))
                    ins.then_inc(S_("y_ready"), 1)
                pe.wait_ge(S_("y_added"), 4 * NE * (u + 1))

        @block.scalar
        def _(act):
            with act.Fori(0, NU) as u:
                for e in range(NE):
                    for c in (0, 2):
                        act.wait_ge(S_("hidden_ready"), FC * (NE * u + e) + c + 1)
                        if e >= 2:
                            act.wait_ge(S_("y_ready"), NE * u + e - 1)
                        nc.scalar.activation(G[e % 2][:, c, :], PS[:, 2 + c, :], ACT.Relu,
                                             bias=b1[:, e, c:c + 1]).then_inc(S_("relu_act"), 1)

        @block.vector
        def _(dve):
            with dve.Fori(0, NU) as u:
                for e in range(NE + 1):
                    for c in (1, 3):
                        if e < NE:
                            dve.wait_ge(S_("hidden_ready"), FC * (NE * u + e) + c + 1)
                            if e >= 2:
                                dve.wait_ge(S_("y_ready"), NE * u + e - 1)
                            nc.vector.tensor_scalar(G[e % 2][:, c, :], PS[:, 2 + c, :], b1[:, e, c:c + 1], 0.0,
                                                    ALU.add, ALU.max).then_inc(S_("relu_dve"), 1)
                    if e:
                        dve.wait_ge(S_("y_ready"), NE * u + e)
                        if e >= 2:
                            dve.wait_ge(S_("y_added"), 4 * (NE * u + e - 1))
                        for j in range(4):
                            nc.vector.scalar_tensor_tensor(X4[:, u, j, :], PS[:, 6 + (e - 1) % 2, j * D:(j + 1) * D],
                                                           G4[:, u, j, e - 1:e], X4[:, u, j, :], ALU.mult,
                                                           ALU.add).then_inc(S_("y_added"), 1)

        @block.sync
        def _(sp):
            with sp.Fori(0, NU) as u:
                sp.wait_ge(S_("y_added"), 4 * NE * (u + 1))
                sp.dma_start(out4[u], X4[:, u]).then_inc(S_("stored"), 16)
            sp.wait_ge(S_("stored"), 16 * NU)


def tables():
    f32 = np.float32
    t = {"ident": np.eye(P, dtype=f32), "ones": np.ones((P, P), f32),
         "upto": np.triu(np.ones((P, P), f32)),
         "order": np.tile(np.arange(NE, 0, -1, dtype=f32), (P, 1))}
    lanes = np.arange(P)
    c = lanes % 32
    inv = (1.0 / f32(10000.0) ** (np.arange(0, ROT, 2, dtype=f32) / f32(ROT))).astype(f32)
    angle = (np.arange(SK, dtype=f32)[:, None] * inv[None, :]).astype(f32)[:, c % 16].T
    sign = np.where(c < 16, -1.0, 1.0).astype(f32)[:, None]
    t["cos_k"], t["sin_k"] = np.cos(angle).astype(f32), (np.sin(angle) * sign).astype(f32)
    t["cos_q"] = (t["cos_k"][:, :S] * f32(DH ** -0.5)).astype(f32)
    t["sin_q"] = (t["sin_k"][:, :S] * f32(DH ** -0.5)).astype(f32)
    c = lanes % HD8
    inv = (1.0 / f32(10000.0) ** (np.arange(0, HD8, 2, dtype=f32) / f32(HD8))).astype(f32)
    angle = (np.arange(S, dtype=f32)[:, None] * inv[None, :]).astype(f32)[:, c % 4].T
    sign = np.where(c < 4, -1.0, 1.0).astype(f32)[:, None]
    t["cos8_k"], t["sin8_k"] = np.cos(angle).astype(f32), (np.sin(angle) * sign).astype(f32)
    t["cos8_q"] = (t["cos8_k"] / f32(HD8 ** -0.5)).astype(f32)
    t["sin8_q"] = (t["sin8_k"] / f32(HD8 ** -0.5)).astype(f32)
    t["pick"] = (lanes[:, None] % 32 // HD8 == np.arange(HG)[None, :]).astype(f32)
    return t


def lay_out(i):
    def heads(w, rotated):
        w = w.reshape(LAYERS, D, NH, DH)
        return (w[..., :ROT] if rotated else w[..., ROT:]).reshape(LAYERS, D, NH * ROT)

    def pairs_swapped(w):
        w = w.reshape(LAYERS, D, NG, 2, 2 * ROT)
        return w[:, :, :, ::-1].reshape(LAYERS, D, NH * ROT)

    x = "L0_xattn_"
    a = {"x": i["x"], "ctx": i["ctx_1024"], "mask": i["mask_BxS_bf1"].view(np.uint8).reshape(-1)}
    a["sqR"], a["skR"] = heads(i[x + "Wq"], True), heads(i[x + "Wk"], True)
    a["sqN"], a["skN"] = (pairs_swapped(heads(i[x + n], False)) for n in ("Wq", "Wk"))
    a["cqR"], a["ckR"] = heads(i[x + "cWq"], True), heads(i[x + "cWk"], True)
    a["cqNT"] = heads(i[x + "cWq"], False).transpose(0, 2, 1)
    a["ckNT"] = heads(i[x + "cWk"], False).transpose(0, 2, 1)
    a["sWvT"], a["cWvT"] = i[x + "Wv"].transpose(0, 2, 1), i[x + "cWv"].transpose(0, 2, 1)
    a["sWo"], a["cWo"] = i[x + "Wo"], i[x + "cWo"]
    a["w1"], a["w2"] = i[x + "ff_w1"], i[x + "ff_w2"]
    a["b1T"] = i[x + "ff_b1"].reshape(LAYERS, FC, P).transpose(0, 2, 1)
    for n, src in (("sw", "attn_norm_w"), ("cw", "cross_norm_w"), ("fw", "ff_norm_w"), ("sbo", "bo"),
                   ("cbo", "cbo"), ("fb2", "ff_b2")):
        a["row_" + n] = i[x + src]
    for n in ("norm_out_w", "proj_w", "proj_b"):
        a[n] = i[x + n]
    for n in "qkvo":
        a["b_W" + n] = i["L0_attn_W" + n].T
        a["c_W" + n] = i["L0_ffn_w" + n]
    for n, src in (("bv", "bv"), ("bo", "bo"), ("g", "ln1_g"), ("b", "ln1_b")):
        a["c_row_" + n] = i["L0_ffn_" + src]
    a["c_cols"] = np.stack([i["L0_ffn_bq"], i["L0_ffn_bk"]], axis=1)
    a["e_w1"], a["e_w2"], a["e_b2"], a["wr"] = (i["L0_ffn_" + n] for n in ("w1", "w2", "b2", "wr"))
    a["e_b1T"] = i["L0_ffn_b1"].reshape(NE, FC, P).transpose(2, 0, 1)
    a["ln2_g"], a["ln2_b"] = i["L0_ffn_ln2_g"][:, None], i["L0_ffn_ln2_b"][:, None]
    return a


def kernel(**inputs):
    import concourse.bacc as bacc
    from concourse.bass_utils import run_bass_kernel_spmd

    nc = bacc.Bacc("TRN2", target_bir_lowering=False, num_devices=1)
    arrays = {n: np.ascontiguousarray(a) for n, a in lay_out({k: np.asarray(v) for k, v in inputs.items()}).items()}
    arrays.update({n: np.ascontiguousarray(a) for n, a in tables().items()})
    dram = {n: nc.dram_tensor("in_" + n, a.shape, mybir.dt.from_np(a.dtype), kind="ExternalInput").ap()
            for n, a in arrays.items()}
    dram["out"] = nc.dram_tensor("out", (B, S, D), F32, kind="ExternalOutput").ap()
    build(nc, dram)
    r = run_bass_kernel_spmd(nc, [{"in_" + n: a for n, a in arrays.items()}], core_ids=[0])
    return r.results[0]["out"]
```

```python
from contextlib import ExitStack, contextmanager

import numpy as np
import concourse.bass as bass
from concourse import mybir

F32 = mybir.dt.float32
U8 = mybir.dt.uint8
ALU = mybir.AluOpType
ACT = mybir.ActivationFunctionType
AX = mybir.AxisListType

P = 128
B, S, D = 128, 32, 128
BT = P // S
NT = B // BT
LAYERS = 2
NH, DH, ROT = 16, 64, 32
NG = 4
HG = NH // NG
SK = 257
FF = 512
FC = FF // P
NE, CAP = 8, 1024
HD8 = 8
BIG = float(np.finfo(np.float32).max)
PLAIN_AT, CTX_AT = (2, 5, 12, 13), (0, 4, 11, 14)
SWAP_HALVES = [(i + 16) % 32 for i in range(32)]
SWAP_PAIRS = [8 * (i // 8) + (2 * (i % 8) + 1 if i % 8 < 4 else 2 * (i % 8 - 4)) for i in range(32)]


def in_eights(eng, body):
    with eng.Fori(0, NT // 8) as u:
        for j in range(8):
            body(8 * u + j)


def in_pairs(eng, count, tile):
    with eng.Fori(0, count // 2 - 1) as u:
        tile(2 * u, 0, False)
        tile(2 * u + 1, 1, False)
    tile(count - 2, 0, False)
    tile(count - 1, 1, True)


def in_slots(eng, slot):
    slot(0, 0, True, False)
    with eng.Fori(0, NT // 2 - 1) as u:
        slot(2 * u + 1, 1, False, False)
        slot(2 * u + 2, 0, False, False)
    slot(NT - 1, 1, False, True)


class Steps:

    def __init__(self, eng, sem, base):
        self.eng, self.sem, self.base, self.n = eng, sem, base, 0

    def go(self, ins):
        self.n += 1
        ins.then_inc(self.sem, 1)

    def __call__(self, ins):
        self.go(ins)
        self.eng.wait_ge(self.sem, self.base + self.n)


class Core:

    def __init__(self, nc, dram, stack):
        self.nc, self.dram, self.stack = nc, dram, stack
        self.PS = stack.enter_context(nc.psum_tensor("PS", [P, 8, 512], F32))
        self.X = self.buffer(stack, "X", [P, NT, D])
        self.ident = self.buffer(stack, "ident", [P, P])
        self.moments = self.buffer(stack, "moments", [P, NT, 6])
        self.mean_var = self.buffer(stack, "mean_var", [P, NT, 1])
        self.root = self.buffer(stack, "root", [P, NT])
        self.rstd = self.buffer(stack, "rstd", [P, NT, 1])
        self.x_tiles = dram["x"].rearrange("(t b) s d -> (b s) t d", b=BT)

    def sem(self, name):
        self.sems.append(self.nc.alloc_semaphore(name=name))
        return self.sems[-1]

    def clear_sems(self):
        for sem in self.sems:
            self.nc.gpsimd.sem_clear(sem)
        self.nc.all_engine_barrier()

    @contextmanager
    def stage(self):
        self.sems = []
        with ExitStack() as st:
            yield st
        self.nc.clear_and_free_semaphores(self.sems)
        self.nc.all_engine_barrier()

    def buffer(self, stack, name, shape, dt=F32):
        return stack.enter_context(self.nc.sbuf_tensor(name, shape, dt))


class Statistics:

    def __init__(self, core, name):
        self.core = core
        self.moments_done, self.steps = core.sem(name + "_moments_done"), core.sem(name + "_steps")
        self.square_ready, self.root_ready = core.sem(name + "_square_ready"), core.sem(name + "_root_ready")

    def run(self, src, rms):
        nc, c = self.core.nc, self.core
        with nc.Block() as block:
            @block.vector
            def _(dve):
                in_eights(dve, lambda t: nc.vector.bn_stats(c.moments[:, t, :], src[:, t, :])
                          .then_inc(self.moments_done, 1))
                dve.wait_ge(self.moments_done, NT)
                mean0, m2_0, mean1, m2_1 = (c.moments[:, :, i] for i in (1, 2, 4, 5))
                mean = c.mean_var[:, :, 0]
                step = Steps(dve, self.steps, 0)
                step(nc.vector.tensor_tensor(mean, mean0, mean1, ALU.add))
                step(nc.vector.tensor_scalar(mean, mean, 0.5, None, ALU.mult))
                step(nc.vector.tensor_tensor(mean0, mean0, mean1, ALU.subtract))
                step(nc.vector.scalar_tensor_tensor(mean0, mean0, 0.25, mean0, ALU.mult, ALU.mult))
                step(nc.vector.tensor_tensor(m2_0, m2_0, m2_1, ALU.add))
                step(nc.vector.scalar_tensor_tensor(c.root[:], m2_0, 1.0 / D, mean0, ALU.mult, ALU.add))
                if rms:
                    step(nc.vector.tensor_tensor(mean, mean, mean, ALU.mult))
                    nc.vector.tensor_tensor(c.root[:], c.root[:], mean, ALU.add).then_inc(self.square_ready, 1)
                else:
                    nc.vector.tensor_scalar(c.root[:], c.root[:], 1e-5, None, ALU.add).then_inc(self.square_ready, 1)
                dve.wait_ge(self.root_ready, 1)
                if rms:
                    step(nc.vector.tensor_scalar(c.root[:], c.root[:], 1e-8, None, ALU.max))
                step(nc.vector.reciprocal(c.rstd[:, :, 0], c.root[:]))

            @block.scalar
            def _(act):
                act.wait_ge(self.square_ready, 1)
                nc.scalar.activation(c.root[:], c.root[:], ACT.Sqrt).then_inc(self.root_ready, 1)


def build(nc, dram):
    with ExitStack() as top:
        core = Core(nc, dram, top)
        with core.stage():
            loaded = core.sem("start_loaded")
            with nc.Block() as block:
                @block.sync
                def _(sp):
                    sp.dma_start(core.X[:], core.x_tiles).then_inc(loaded, 16)
                    sp.dma_start(core.ident[:], dram["ident"]).then_inc(loaded, 16)
                    sp.wait_ge(loaded, 32)

            Statistics(core, "ln_x").run(core.X, False)
            normalise(core, core.X, core.X, "x_normed")
        with core.stage() as st:
            perceiver(core, st)
        HB = core.buffer(top, "HB", [P, NT, D])
        with core.stage() as st:
            project(core, st, HB)
        with core.stage() as st:
            small = SmallAttention(core, st)
            Statistics(core, "ln_b").run(core.X, False)
            small.run(core.X, rotary=True)
            Statistics(core, "ln_c").run(core.X, False)
            normalise(core, HB, core.X, "c_normed")
            Statistics(core, "ln_c1").run(HB, False)
            small.run(HB, rotary=False)
        with core.stage() as st:
            Statistics(core, "ln_c2").run(HB, False)
            experts(core, st, HB)


def normalise(core, dst, src, name):
    nc, done = core.nc, core.sem(name)
    with nc.Block() as block:
        @block.vector
        def _(dve):
            in_eights(dve, lambda t: nc.vector.tensor_scalar(
                dst[:, t, :], src[:, t, :], core.mean_var[:, t, 0:1], core.rstd[:, t, :],
                ALU.subtract, ALU.mult).then_inc(done, 1))
            dve.wait_ge(done, NT)


def heads(width, g):
    per = P // width
    first = g % per + 4 * per * (g // per)
    return range(first, first + 4 * per, per)


def perceiver(core, st):
    nc, dram = core.nc, core.dram
    def buf(name, shape, dt=F32):
        return core.buffer(st, name, shape, dt)

    tables = {n: buf(n, [P, SK if n[-1] == "k" else S]) for n in ("cos_k", "sin_k", "cos_q", "sin_q")}
    mask_bytes = buf("mask_bytes", [P, NT, BT * S], U8)
    last_rows_T = buf("last_rows_T", [P, NT, BT])
    W = {n: buf("w_" + n, [P, NH * ROT]) for n in ("sqR", "skR", "sqN", "skN", "cqR", "ckR")}
    VO = {a: buf("VO_" + a, [P, NH, D]) for a in "sc"}
    QK = buf("QK", [P, NH, D])
    W1, W2 = buf("W1", [P, FF]), buf("W2", [P, FC, D])
    b1 = buf("b1", [P, FC])
    rows = {n: buf("row_" + n, [P, D]) for n in ("sw", "cw", "fw", "sbo", "cbo", "fb2")}

    tables_loaded, last_turned, last_kept = (core.sem(n) for n in ("tables_loaded", "last_turned", "last_kept"))
    with ExitStack() as tmp, nc.Block() as block:
        last_rows = core.buffer(tmp, "last_rows", [B, D])

        @block.sync
        def _(sp):
            for n in tables:
                sp.dma_start(tables[n][:], dram[n]).then_inc(tables_loaded, 16)
            sp.dma_start(mask_bytes[:], dram["mask"].partition_broadcast(P)).then_inc(tables_loaded, 16)
            sp.dma_start(last_rows[:], dram["ctx"][:, SK - 1, :]).then_inc(tables_loaded, 16)

        @block.tensor
        def _(pe):
            pe.wait_ge(tables_loaded, 96)
            nc.tensor.transpose(core.PS[:, 0, 0:B], last_rows[:], core.ident[:]).then_inc(last_turned, 1)

        @block.vector
        def _(dve):
            dve.wait_ge(last_turned, 1)
            nc.vector.tensor_copy(last_rows_T[:], core.PS[:, 0, 0:B]).then_inc(last_kept, 1)
            dve.wait_ge(last_kept, 1)

    factors_loaded, loaded, product_ready, product_kept = (
        core.sem(n) for n in ("factors_loaded", "weights_loaded", "product_ready", "product_kept"))
    stats = [Statistics(core, n) for n in ("rms_self", "rms_cross", "rms_ffn")]
    self_attention, cross_attention, feed_forward = SelfAttention(core), CrossAttention(core), FeedForward(core)

    with nc.Fori(0, LAYERS) as l:
        with ExitStack() as tmp:
            WvT = {a: core.buffer(tmp, "WvT_" + a, [P, NH // 2, D]) for a in "sc"}
            Wo = {a: core.buffer(tmp, "Wo_" + a, [P, NH // 2, D]) for a in "sc"}
            WqNT, WkNT = core.buffer(tmp, "WqNT", [P, NG, D]), core.buffer(tmp, "WkNT", [P, NG, D])
            chunks = lambda a: a.rearrange("(c p) d -> p c d", p=P)
            factors = [(WvT[a][:], chunks(dram[a + "WvT"][l])) for a in "sc"]
            factors += [(Wo[a][:], chunks(dram[a + "Wo"][l])) for a in "sc"]
            factors += [(WqNT[:], chunks(dram["cqNT"][l])), (WkNT[:], chunks(dram["ckNT"][l]))]
            loads = [(W[n][:], dram[n][l]) for n in W]
            loads += [(W1[:], dram["w1"][l]), (W2[:], chunks(dram["w2"][l])), (b1[:], dram["b1T"][l])]
            loads += [(rows[n][:], dram["row_" + n][l].partition_broadcast(P)) for n in rows]
            products = [(VO["s"], WvT["s"], Wo["s"], DH), (VO["c"], WvT["c"], Wo["c"], DH),
                        (QK, WqNT, WkNT, ROT)]
            turns = [(p, g) for p in products for g in range(NG)]

            with nc.Block() as block:
                @block.sync
                def _(sp):
                    for dst, src in factors:
                        sp.dma_start(dst, src).then_inc(factors_loaded, 16)
                    for dst, src in loads:
                        sp.dma_start(dst, src).then_inc(loaded, 16)
                    sp.wait_ge(loaded, 16 * len(loads))

                @block.tensor
                def _(pe):
                    pe.wait_ge(factors_loaded, 16 * len(factors))
                    for k, ((_, left, right, width), g) in enumerate(turns):
                        if k >= 8:
                            pe.wait_ge(product_kept, k - 7)
                        for h, head in enumerate(heads(width, g)):
                            chunk, r = divmod(head * width, P)
                            ins = nc.tensor.matmul(core.PS[:, k % 8, h * D:(h + 1) * D],
                                                   left[r:r + width, chunk, :], right[r:r + width, chunk, :],
                                                   start=True, stop=True)
                        ins.then_inc(product_ready, 1)

                @block.vector
                def _(dve):
                    for k, ((dst, _, _, width), g) in enumerate(turns):
                        dve.wait_ge(product_ready, k + 1)
                        of = heads(width, g)
                        nc.vector.tensor_copy(dst[:, of.start:of[-1] + 1:of.step, :],
                                              core.PS[:, k % 8, :].rearrange("p (h d) -> p h d", h=HG)).then_inc(product_kept, 1)
                    dve.wait_ge(product_kept, len(turns))

        stats[0].run(core.X, True)
        self_attention.run(W, VO["s"], rows["sw"], rows["sbo"], tables, mask_bytes)
        stats[1].run(core.X, True)
        cross_attention.run(W, VO["c"], QK, rows["cw"], rows["cbo"], tables, last_rows_T)
        stats[2].run(core.X, True)
        feed_forward.run(W1, W2, b1, rows["fw"], rows["fb2"])
        core.clear_sems()


class Rope:

    def __init__(self, nc, step, raw, keep, cos, sin, out, swap):
        self.nc, self.step, self.raw, self.keep, self.cos, self.sin, self.out, self.swap = (
            nc, step, raw, keep, cos, sin, out, swap)

    def product(self):
        self.step.go(self.nc.vector.tensor_tensor(self.keep, self.raw, self.cos, ALU.mult))

    def partner(self):
        self.step(self.nc.vector.stream_shuffle(self.raw, self.raw, self.swap))

    def partner_product(self):
        self.step(self.nc.vector.tensor_tensor(self.raw, self.raw, self.sin, ALU.mult))

    def sum(self):
        return self.nc.vector.tensor_tensor(self.out, self.raw, self.keep, ALU.add)

    def first(self):
        self.product()
        self.partner()

    def second(self):
        self.partner_product()
        return self.sum()


class SelfAttention:

    def __init__(self, core):
        self.core = core
        names = ("h_ready", "hv_ready", "x_added", "hT_ready", "hT_kept", "rot_ready", "plain_ready", "q_turned", "k_turned",
                 "q_rot_spread", "q_plain_spread", "k_plain_kept", "mask_ready", "scores_ready", "shifted",
                 "exp_done", "probs_ready", "pT_ready", "pT_kept", "uT_ready", "uT_kept", "out_ready", "dve_steps",
                 "pool_steps", "zeroed", "held")
        self.sems = {n: core.sem("self_" + n) for n in names}

    def run(self, W, VO, norm_row, bias_row, tables, mask_bytes):
        core, nc, PS, X, s = self.core, self.core.nc, self.core.PS, self.core.X, self.sems
        ROPE, SOFTMAX, ADD = 6, 5, 1
        with ExitStack() as st:
            def buf(name, shape):
                return core.buffer(st, "self_" + name, shape)

            H, HV = buf("H", [P, D]), buf("HV", [P, D])
            HT = buf("HT", [P, P])
            keep = buf("keep", [P, NG * P])
            QR = buf("QR", [P, NG, P])
            QD, K = buf("QD", [P, NG, 2, BT, 2, S]), buf("K", [P, NG, 2, P])
            allow, forbid = buf("allow", [P, 1, P]), buf("forbid", [P, 1, P])
            top, total, inverse = buf("top", [P, NG * BT]), buf("total", [P, NG * BT]), buf("inverse", [P, NG * BT])
            PR = [buf(f"PR{i}", [P, NG, P]) for i in range(2)]
            PT = buf("PT", [P, NG, P])
            UT = buf("UT", [P, NH, BT, S])
            SC = PS[:, 4, :]
            SC3 = SC.rearrange("p (g n) -> p g n", g=NG)
            SCj = SC.rearrange("p (m j) -> p m j", j=S)
            flat = lambda a: a[:].rearrange("p g n -> p (g n)")

            def per_row(v):
                return v[:].unsqueeze(2).to_broadcast([P, NG * BT, S])

            with nc.Block() as block:
                @block.gpsimd
                def _(pool):
                    nc.gpsimd.memset(QD[:], 0.0).then_inc(s["zeroed"], 1)
                    with pool.Fori(0, NT) as n:
                        pool.wait_ge(s["k_turned"], 2 * n + 2)
                        nc.gpsimd.tensor_copy(allow[:, 0, :], mask_bytes[:, n, :]).then_inc(s["pool_steps"], 1)
                        pool.wait_ge(s["pool_steps"], n + 1)
                        pool.sem_inc(s["held"], 1)
                        nc.gpsimd.tensor_scalar(forbid[:], allow[:], -1.0, BIG, ALU.add,
                                                ALU.mult).then_inc(s["mask_ready"], 1)

                @block.vector
                def _(dve):
                    def hidden(n, dst, done):
                        nc.vector.scalar_tensor_tensor(dst[:], X[:, n, :], core.rstd[:, n, :], norm_row[:],
                                                       ALU.mult, ALU.mult).then_inc(s[done], 1)

                    def turn(step, n):
                        view = lambda a: a.rearrange("p (m i) -> p m i", i=S)
                        for k, (c, i) in enumerate((("cos_q", "sin_q"), ("cos_k", "sin_k"))):
                            dve.wait_ge(s["rot_ready"], 2 * n + k + 1)
                            if k == 1:
                                dve.wait_ge(s["q_turned"], n + 1)
                            bc = lambda a: tables[a][:, 0:S].unsqueeze(1).to_broadcast([P, NG * BT, S])
                            rope = Rope(nc, step, view(PS[:, k, :]), view(keep[:]), bc(c), bc(i), view(flat(QR)),
                                        SWAP_HALVES)
                            rope.first()
                            if k == 0:
                                rope.second().then_inc(s["q_turned"], 1)
                                continue
                            rope.partner_product()
                            for pair in range(2):
                                r = slice(64 * pair, 64 * pair + 64)
                                nc.vector.tensor_tensor(K[r, :, pair, :],
                                                        PS[r, 1, :].rearrange("p (g n) -> p g n", g=NG),
                                                        keep[r].rearrange("p (g n) -> p g n", g=NG),
                                                        ALU.add).then_inc(s["k_turned"], 1)

                    def add_out(step, n):
                        dve.wait_ge(s["out_ready"], n + 1)
                        nc.vector.tensor_tensor(X[:, n, :], X[:, n, :], PS[:, 5, 0:D], ALU.add)\
                          .then_inc(s["x_added"], 1)
                        dve.wait_ge(s["x_added"], n + 1)
                        step(nc.vector.tensor_tensor(X[:, n, :], X[:, n, :], bias_row[:], ALU.add))

                    def slot(m, parity, first, last):
                        if not last:
                            hidden(m + 1, H, "h_ready")
                        if not first:
                            hidden(m - 1, HV, "hv_ready")
                        step = Steps(dve, s["dve_steps"], ROPE + m * (ROPE + SOFTMAX + ADD) - (0 if first else ADD))
                        dve.wait_ge(s["scores_ready"], m + 1)
                        dve.wait_ge(s["mask_ready"], m + 1)
                        step(nc.vector.tensor_tensor(SC3, SC3, allow[:].to_broadcast([P, NG, P]), ALU.mult))
                        step(nc.vector.tensor_tensor(SC3, SC3, forbid[:].to_broadcast([P, NG, P]), ALU.add))
                        step(nc.vector.tensor_reduce(top[:], SCj, AX.X, ALU.max))
                        nc.vector.tensor_tensor(SCj, SCj, per_row(top), ALU.subtract).then_inc(s["shifted"], 1)
                        dve.wait_ge(s["exp_done"], m + 1)
                        step(nc.vector.tensor_reduce(total[:], SCj, AX.X, ALU.add))
                        step(nc.vector.reciprocal(inverse[:], total[:]))
                        nc.vector.tensor_tensor(PR[parity][:].rearrange("p g (b j) -> p (g b) j", j=S), SCj,
                                                per_row(inverse), ALU.mult).then_inc(s["probs_ready"], 1)
                        if not last:
                            turn(step, m + 1)
                        if not first:
                            add_out(step, m - 1)
                        assert step.n == SOFTMAX + ROPE * (not last) + ADD * (not first)

                    hidden(0, H, "h_ready")
                    turn(Steps(dve, s["dve_steps"], 0), 0)
                    in_slots(dve, slot)
                    hidden(NT - 1, HV, "hv_ready")
                    add_out(Steps(dve, s["dve_steps"], ROPE * NT + SOFTMAX * NT + ADD * (NT - 1)), NT - 1)

                @block.scalar
                def _(act):
                    def keep_hT(n):
                        act.wait_ge(s["hT_ready"], n + 1)
                        nc.scalar.activation(HT[:], PS[:, 5, 0:P], ACT.Copy).then_inc(s["hT_kept"], 1)

                    def plain_queries(n):
                        act.wait_ge(s["plain_ready"], 2 * n + 1)
                        for x in range(HG):
                            r = slice(32 * x, 32 * x + 32)
                            nc.scalar.activation(QD[r, :, (x // 2 + 1) % 2, :, x % 2, :], PS[r, 2, :].rearrange(
                                "p (g b i) -> p g b i", g=NG, b=BT), ACT.Copy, scale=DH ** -0.5)\
                              .then_inc(s["q_plain_spread"], 1)

                    def plain_keys(n):
                        act.wait_ge(s["plain_ready"], 2 * n + 2)
                        for pair in range(2):
                            r = slice(64 * (1 - pair), 64 * (1 - pair) + 64)
                            nc.scalar.activation(K[r, :, pair, :], PS[r, 3, :].rearrange("p (g n) -> p g n", g=NG),
                                                 ACT.Copy).then_inc(s["k_plain_kept"], 1)

                    def rotated(n):
                        act.wait_ge(s["q_turned"], n + 1)
                        for h in range(HG):
                            r = slice(32 * h, 32 * h + 32)
                            nc.scalar.activation(QD[r, :, h // 2, :, h % 2, :], QR[r].rearrange(
                                "p g (b i) -> p g b i", b=BT), ACT.Copy).then_inc(s["q_rot_spread"], 1)

                    def keep_pT(n):
                        act.wait_ge(s["pT_ready"], n + 1)
                        nc.scalar.activation(flat(PT), PS[:, 5, :], ACT.Copy).then_inc(s["pT_kept"], 1)

                    def keep_uT(n):
                        for b in range(BT):
                            act.wait_ge(s["uT_ready"], BT * n + b + 1)
                            nc.scalar.activation(UT[:, :, b, :], PS[:, 6 + b % 2, :].rearrange("p (h i) -> p h i", i=S),
                                                 ACT.Copy).then_inc(s["uT_kept"], 1)

                    def slot(m, parity, first, last):
                        if not last:
                            keep_hT(m + 1)
                            plain_queries(m + 1)
                        act.wait_ge(s["shifted"], m + 1)
                        nc.scalar.activation(SC, SC, ACT.Exp).then_inc(s["exp_done"], 1)
                        if not first:
                            keep_pT(m - 1)
                        if not last:
                            plain_keys(m + 1)
                        if not first:
                            keep_uT(m - 1)
                        if not last:
                            rotated(m + 1)

                    act.wait_ge(s["zeroed"], 1)
                    keep_hT(0)
                    plain_queries(0)
                    plain_keys(0)
                    rotated(0)
                    in_slots(act, slot)
                    keep_pT(NT - 1)
                    keep_uT(NT - 1)

                @block.tensor
                def _(pe):
                    def turn_h(n):
                        pe.wait_ge(s["h_ready"], n + 1)
                        nc.tensor.transpose(PS[:, 5, 0:P], H[:], core.ident[:]).then_inc(s["hT_ready"], 1)

                    def project(bank, w, done):
                        for g in range(NG):
                            ins = nc.tensor.matmul(PS[:, bank, g * P:(g + 1) * P], W[w][:, g * P:(g + 1) * P],
                                                   HT[:], start=True, stop=True)
                        ins.then_inc(s[done], 1)

                    def front(n):
                        pe.wait_ge(s["hT_kept"], n + 1)
                        project(2, "sqN", "plain_ready")
                        project(3, "skN", "plain_ready")
                        project(0, "sqR", "rot_ready")

                    def scores(n, last):
                        pe.wait_ge(s["q_plain_spread"], HG * n + HG)
                        pe.wait_ge(s["k_plain_kept"], 2 * n + 2)
                        pe.wait_ge(s["q_rot_spread"], HG * n + HG)
                        pe.wait_ge(s["k_turned"], 2 * n + 2)
                        for g in range(NG):
                            if g == 2 and not last:
                                turn_h(n + 1)
                            for pair in range(2):
                                for b in range(BT):
                                    ins = nc.tensor.matmul(
                                        PS[64 * pair:64 * pair + 64, 4, g * P + b * S:g * P + (b + 1) * S],
                                        QD[:, g, pair, b].rearrange("p h i -> p (h i)"),
                                        K[:, g, pair, b * S:(b + 1) * S], start=True, stop=True)
                        ins.then_inc(s["scores_ready"], 1)

                    def turn_probs(n, parity, last=False):
                        if last:
                            pe.wait_ge(s["x_added"], n)
                        pe.wait_ge(s["probs_ready"], n + 1)
                        for g in range(NG):
                            ins = nc.tensor.transpose(PS[:, 5, g * P:(g + 1) * P], PR[parity][:, g, :], core.ident[:])
                        ins.then_inc(s["pT_ready"], 1)

                    def output(n):
                        pe.wait_ge(s["hv_ready"], n + 1)
                        pe.wait_ge(s["pT_kept"], n + 1)
                        for b in range(BT):
                            if b >= 2:
                                pe.wait_ge(s["uT_kept"], BT * n + b - 1)
                            r = slice(b * S, (b + 1) * S)
                            nc.tensor.matmul(PS[:, 6 + b % 2, :], HV[r, :], flat(PT)[r],
                                             start=True, stop=True).then_inc(s["uT_ready"], 1)
                        pe.wait_ge(s["uT_kept"], BT * n + BT)
                        for h in range(NH):
                            ins = nc.tensor.matmul(PS[:, 5, 0:D], UT[:, h].rearrange("p b i -> p (b i)"), VO[:, h, :],
                                                   start=(h == 0), stop=(h == NH - 1))
                        ins.then_inc(s["out_ready"], 1)

                    def slot(m, parity, first, last):
                        scores(m, last)
                        if not last:
                            front(m + 1)
                        if not first:
                            turn_probs(m - 1, 1 - parity, last)
                        if not last:
                            project(1, "skR", "rot_ready")
                        if not first:
                            output(m - 1)

                    pe.wait_ge(s["zeroed"], 1)
                    turn_h(0)
                    front(0)
                    project(1, "skR", "rot_ready")
                    in_slots(pe, slot)
                    turn_probs(NT - 1, (NT - 1) % 2, True)
                    output(NT - 1)


class CrossAttention:

    def __init__(self, core):
        self.core = core
        names = ("h_ready", "hT_ready", "hT_kept", "rot_ready", "q_turned", "q_rot_spread", "q_plain_ready",
                 "q_plain_kept", "ctxT_ready", "ctxT_kept", "last_kept", "k_ready", "k_turned", "scores_ready",
                 "top_ready", "exp_done", "inverse_ready", "pT_ready", "pT_kept", "u_ready", "last_part_ready",
                 "u_normed", "uT_ready", "uT_kept", "out_ready", "x_added", "dve_steps", "zeroed", "held")
        self.sems = {n: core.sem("cross_" + n) for n in names}
        self.sems["ctx_loaded"] = [core.sem(f"cross_ctx_loaded{b}") for b in range(BT)]

    def run(self, W, VO, QK, norm_row, bias_row, tables, last_rows_T):
        core, nc, PS, X, s = self.core, self.core.nc, self.core.PS, self.core.X, self.sems
        NS = BT * NG
        NK = 2 * BT
        KEEP_Q, KEEP_K, ADD = 3, 3, 1
        TILE_STEPS = NK * KEEP_K + KEEP_Q + ADD
        ctx = core.dram["ctx"]
        with ExitStack() as st:
            def buf(name, shape):
                return core.buffer(st, "cross_" + name, shape)

            H, HT = buf("H", [P, D]), buf("HT", [P, P])
            C = [buf(f"C{b}", [P, 2, D]) for b in range(BT)]
            last_bc = [buf(f"last_bc{b}", [P, D]) for b in range(BT)]
            ctxT = buf("ctxT", [P, BT, SK])
            KR = [buf(f"KR{i}", [P, NG, SK]) for i in range(2)]
            keep, keep_q = buf("keep", [P, 2, SK]), buf("keep_q", [P, NG * P])
            QR = buf("QR", [P, NG, P])
            QRd = [buf(f"QRd{i}", [P, NG, BT, HG, S]) for i in range(2)]
            QN = [buf(f"QN{i}", [P, NG, BT, HG, S]) for i in range(2)]
            PR = [buf(f"PR{i}", [P, SK]) for i in range(4)]
            PT = [buf(f"PT{i}", [P, 2, P]) for i in range(2)]
            last_part = [buf(f"last_part{i}", [P, D]) for i in range(2)]
            U = [buf(f"U{i}", [P, D]) for i in range(2)]
            UT = buf("UT", [P, NH, BT, S])
            minus_top, total, inverse = buf("minus_top", [P, NS]), buf("total", [P, NS]), buf("inverse", [P, NS])

            def pair(src):
                return tables[src][:].unsqueeze(1).to_broadcast([P, 2, SK])

            def wait(eng, name, value):
                if not (isinstance(value, int) and value <= 0):
                    eng.wait_ge(s[name], value)

            with nc.Block() as block:
                @block.sync
                def _(sp):
                    def load(t, b):
                        row = BT * t + b
                        sp.dma_start(C[b][:], ctx[row, 0:2 * P, :].rearrange("(c p) d -> p c d", p=P))\
                          .then_inc(s["ctx_loaded"][b], 16)
                        sp.dma_start(last_bc[b][:], ctx[row, SK - 1, :].partition_broadcast(P))\
                          .then_inc(s["ctx_loaded"][b], 16)
                    for b in range(BT):
                        load(0, b)
                    with sp.Fori(0, NT - 1) as t:
                        for b in range(BT):
                            sp.wait_ge(s["u_normed"], t * NS + NG * (b + 1))
                            load(t + 1, b)

                @block.gpsimd
                def _(pool):
                    for i in range(2):
                        nc.gpsimd.memset(QRd[i][:], 0.0).then_inc(s["zeroed"], 1)

                    def last_column(n, b):
                        pool.wait_ge(s["ctxT_ready"], BT * n + b + 1)
                        pool.sem_inc(s["held"], 1)
                        nc.gpsimd.tensor_copy(ctxT[:, b % BT, SK - 1:SK],
                                              last_rows_T[:, n + b // BT, b % BT:b % BT + 1]).then_inc(s["last_kept"], 1)

                    def tile(n, parity, first, last):
                        for q in range(NS):
                            b, g = divmod(q, NG)
                            if g == 0:
                                pool.wait_ge(s["ctx_loaded"][b], 32 * n + 32)
                            if q in (2, 6, 11, 14):
                                k = (2, 6, 11, 14).index(q) + 2
                                if not (last and k >= BT):
                                    last_column(n, k)
                            pool.wait_ge(s["inverse_ready"], NS * n + q + 1)
                            wait(pool, "u_normed", NS * n + q - 1)
                            pool.sem_inc(s["held"], 1)
                            nc.gpsimd.tensor_scalar(last_part[q % 2][:], last_bc[b][:], PR[q % 4][:, SK - 1:SK],
                                                    inverse[:, q:q + 1], ALU.mult, ALU.mult)\
                              .then_inc(s["last_part_ready"], 1)

                    last_column(0, 0)
                    last_column(0, 1)
                    in_slots(pool, tile)

                @block.vector
                def _(dve):
                    def hidden(n):
                        nc.vector.scalar_tensor_tensor(H[:], X[:, n, :], core.rstd[:, n, :], norm_row[:],
                                                       ALU.mult, ALU.mult).then_inc(s["h_ready"], 1)

                    def key_rope(step, b, half):
                        return Rope(nc, step, PS[:, 0:2, 0:SK], keep[:], pair("cos_k"), pair("sin_k"),
                                    KR[b % 2][:, 2 * half:2 * half + 2, :], SWAP_HALVES)

                    def keys_first(step, n, b, half):
                        dve.wait_ge(s["k_ready"], NK * n + 2 * b + half + 1)
                        wait(dve, "k_turned", NK * n + 2 * b + half)
                        key_rope(step, b, half).first()

                    def keys_second(step, n, b, half):
                        key_rope(step, b, half).second().then_inc(s["k_turned"], 1)

                    def query_rope(step, bank):
                        view = lambda a: a.rearrange("p (m i) -> p m i", i=S)
                        bc = lambda a: tables[a][:].unsqueeze(1).to_broadcast([P, NG * BT, S])
                        return Rope(nc, step, view(PS[:, bank, :]), view(keep_q[:]), bc("cos_q"), bc("sin_q"),
                                    view(QR[:].rearrange("p g n -> p (g n)")), SWAP_HALVES)

                    def add_out(step, n):
                        dve.wait_ge(s["out_ready"], n + 1)
                        nc.vector.tensor_tensor(X[:, n, :], X[:, n, :], PS[:, 6, 0:D], ALU.add)\
                          .then_inc(s["x_added"], 1)
                        dve.wait_ge(s["x_added"], n + 1)
                        step.go(nc.vector.tensor_tensor(X[:, n, :], X[:, n, :], bias_row[:], ALU.add))

                    def tile(n, parity, first, last):
                        step = Steps(dve, s["dve_steps"], 2 * KEEP_K + KEEP_Q + n * TILE_STEPS - (0 if first else ADD))
                        for q in range(NS + 2 * last):
                            b, g = divmod(q, NG)
                            if q < NS:
                                dve.wait_ge(s["scores_ready"], NS * n + q + 1)
                                nc.vector.tensor_reduce(minus_top[:, q:q + 1], PS[:, 2 + q % 2, 0:SK], AX.X, ALU.max,
                                                        negate=True).then_inc(s["top_ready"], 1)
                            if (q >= 1 or not first) and q <= NS:
                                r = (q - 1) % NS
                                dve.wait_ge(s["exp_done"], NS * n + q)
                                nc.vector.reciprocal(inverse[:, r:r + 1], total[:, r:r + 1])\
                                  .then_inc(s["inverse_ready"], 1)
                            if not last and q == 8:
                                dve.wait_ge(s["rot_ready"], n + 2)
                                query_rope(step, 6).product()
                            if not last and q == 10:
                                query_rope(step, 6).partner_product()
                            if q >= 2 or not first:
                                r = (q - 2) % NS
                                dve.wait_ge(s["u_ready"], NS * n + q - 1)
                                dve.wait_ge(s["last_part_ready"], NS * n + q - 1)
                                dve.wait_ge(s["inverse_ready"], NS * n + q - 1)
                                wait(dve, "uT_ready", NS * n + q - 3)
                                nc.vector.scalar_tensor_tensor(U[q % 2][:], PS[:, 5, 0:D], inverse[:, r:r + 1],
                                                               last_part[q % 2][:], ALU.mult,
                                                               ALU.add).then_inc(s["u_normed"], 1)
                            if not last and q == 8:
                                query_rope(step, 6).partner()
                            if not last and q == 10:
                                query_rope(step, 6).sum().then_inc(s["q_turned"], 1)
                            if q < NS and not (last and b + 1 == BT):
                                (keys_first, keys_second)[g % 2](step, n, b + 1, g // 2)
                            if q == 0 and not last:
                                hidden(n + 1)
                            if q == 3 and not first:
                                add_out(step, n - 1)
                        assert step.n == TILE_STEPS - ADD * first - (2 * KEEP_K + KEEP_Q) * last

                    step = Steps(dve, s["dve_steps"], 0)
                    hidden(0)
                    keys_first(step, 0, 0, 0)
                    keys_second(step, 0, 0, 0)
                    dve.wait_ge(s["rot_ready"], 1)
                    query_rope(step, 5).first()
                    query_rope(step, 5).second().then_inc(s["q_turned"], 1)
                    keys_first(step, 0, 0, 1)
                    keys_second(step, 0, 0, 1)
                    in_slots(dve, tile)
                    add_out(step, NT - 1)

                @block.scalar
                def _(act):
                    def keep_ctxT(n, b):
                        act.wait_ge(s["ctxT_ready"], BT * n + b + 1)
                        nc.scalar.activation(ctxT[:, b % BT, 0:2 * P], PS[:, 6, 0:2 * P],
                                             ACT.Copy).then_inc(s["ctxT_kept"], 1)

                    def keep_hT(n, bank):
                        act.wait_ge(s["hT_ready"], n + 1)
                        nc.scalar.activation(HT[:], PS[:, bank, 0:P], ACT.Copy).then_inc(s["hT_kept"], 1)

                    def keep_plain(n, parity, g, bank):
                        act.wait_ge(s["q_plain_ready"], NG * n + g + 1)
                        nc.scalar.activation(QN[parity][:, g].rearrange("p b h i -> p h b i"),
                                             PS[:, bank, :].rearrange("p (h b i) -> p h b i", h=HG, b=BT),
                                             ACT.Copy, scale=DH ** -0.5).then_inc(s["q_plain_kept"], 1)

                    def spread(n, parity, h):
                        act.wait_ge(s["q_turned"], n + 1)
                        r = slice(32 * h, 32 * h + 32)
                        nc.scalar.activation(QRd[parity][r, :, :, h, :], QR[r].rearrange(
                            "p g (b i) -> p g b i", b=BT), ACT.Copy).then_inc(s["q_rot_spread"], 1)

                    def tile(n, parity, first, last):
                        for q in range(NS + 3 * last):
                            b, g = divmod(q, NG)
                            if (1 <= q or not first) and q <= NS:
                                act.wait_ge(s["pT_ready"], NS * n + q)
                                wait(act, "u_ready", NS * n + q - 2)
                                nc.scalar.activation(PT[(q - 1) % 2][:].rearrange("p c n -> p (c n)"),
                                                     PS[:, 4, 0:2 * P], ACT.Copy).then_inc(s["pT_kept"], 1)
                            if q < NS:
                                act.wait_ge(s["top_ready"], NS * n + q + 1)
                                wait(act, "pT_ready", NS * n + q - 3)
                                wait(act, "last_part_ready", NS * n + q - 3)
                                nc.scalar.activation(PR[q % 4][:], PS[:, 2 + q % 2, 0:SK], ACT.Exp,
                                                     bias=minus_top[:, q:q + 1],
                                                     accum_out=total[:, q:q + 1]).then_inc(s["exp_done"], 1)
                            if q >= 3 or not first:
                                act.wait_ge(s["uT_ready"], NS * n + q - 2)
                                pb, pg = divmod((q - 3) % NS, NG)
                                nc.scalar.activation(UT[:, pg * HG:(pg + 1) * HG, pb, :],
                                                     PS[:, 7, 0:P].rearrange("p (h i) -> p h i", i=S),
                                                     ACT.Copy).then_inc(s["uT_kept"], 1)
                            if q in CTX_AT:
                                k = CTX_AT.index(q) + 2
                                if not (last and k >= BT):
                                    keep_ctxT(n, k)
                            if not last:
                                if q == 1:
                                    keep_hT(n + 1, 6)
                                if q in PLAIN_AT:
                                    keep_plain(n + 1, 1 - parity, PLAIN_AT.index(q), 6)
                                if 11 <= q < 11 + HG:
                                    spread(n + 1, 1 - parity, q - 11)

                    act.wait_ge(s["zeroed"], 2)
                    keep_ctxT(0, 0)
                    keep_hT(0, 7)
                    for g in range(NG):
                        keep_plain(0, 0, g, (2, 3, 4, 7)[g])
                    for h in range(HG):
                        spread(0, 0, h)
                    keep_ctxT(0, 1)
                    in_slots(act, tile)

                @block.tensor
                def _(pe):
                    def turn_ctx(n, b):
                        pe.wait_ge(s["ctx_loaded"][b % BT], 32 * (n + b // BT) + 32)
                        for c in range(2):
                            ins = nc.tensor.transpose(PS[:, 6, c * P:(c + 1) * P], C[b % BT][:, c, :], core.ident[:])
                        ins.then_inc(s["ctxT_ready"], 1)

                    def keys(n, b, half):
                        pe.wait_ge(s["ctxT_kept"], BT * n + b + 1)
                        pe.wait_ge(s["last_kept"], BT * n + b + 1)
                        wait(pe, "k_turned", NK * n + 2 * b + half)
                        for i in range(2):
                            g = 2 * half + i
                            ins = nc.tensor.matmul(PS[:, i, 0:SK], W["ckR"][:, g * P:(g + 1) * P],
                                                   ctxT[:, b % BT, :], start=True, stop=True)
                        ins.then_inc(s["k_ready"], 1)

                    def turn_h(n, bank):
                        pe.wait_ge(s["h_ready"], n + 1)
                        nc.tensor.transpose(PS[:, bank, 0:P], H[:], core.ident[:]).then_inc(s["hT_ready"], 1)

                    def rotary_queries(bank):
                        for g in range(NG):
                            ins = nc.tensor.matmul(PS[:, bank, g * P:(g + 1) * P], W["cqR"][:, g * P:(g + 1) * P],
                                                   HT[:], start=True, stop=True)
                        ins.then_inc(s["rot_ready"], 1)

                    def plain_queries(g, bank):
                        for h in range(HG):
                            ins = nc.tensor.matmul(PS[:, bank, h * P:(h + 1) * P], QK[:, g * HG + h, :], HT[:],
                                                   start=True, stop=True)
                        ins.then_inc(s["q_plain_ready"], 1)

                    def out_tile(n):
                        pe.wait_ge(s["uT_kept"], NS * n + NS)
                        for h in range(NH):
                            ins = nc.tensor.matmul(PS[:, 6, 0:D], UT[:, h].rearrange("p b i -> p (b i)"),
                                                   VO[:, h, :], start=(h == 0), stop=(h == NH - 1))
                        ins.then_inc(s["out_ready"], 1)

                    def bank6(n, q, first, last):
                        if q == 0:
                            pe.wait_ge(s["ctxT_kept"], BT * n + 2)
                            turn_ctx(n, 2)
                        if q == 4:
                            if first:
                                pe.wait_ge(s["q_plain_kept"], NG * (n + 1) + 1)
                            else:
                                pe.wait_ge(s["x_added"], n)
                            turn_ctx(n, 3)
                        if last:
                            return
                        if q == 1:
                            pe.wait_ge(s["ctxT_kept"], BT * n + 3)
                            turn_h(n + 1, 6)
                        if q == 6:
                            pe.wait_ge(s["q_plain_kept"], NG * (n + 1) + 2)
                            rotary_queries(6)
                        if q == 11:
                            pe.wait_ge(s["q_turned"], n + 2)
                            turn_ctx(n, 4)
                        if q == 14:
                            pe.wait_ge(s["q_plain_kept"], NG * (n + 1) + 4)
                            turn_ctx(n, 5)
                        if q in PLAIN_AT:
                            g = PLAIN_AT.index(q)
                            if g == 0:
                                pe.wait_ge(s["hT_kept"], n + 2)
                            elif g == 3:
                                pe.wait_ge(s["q_plain_kept"], NG * (n + 1) + 3)
                            else:
                                pe.wait_ge(s["ctxT_kept"], BT * n + 3 + g)
                            plain_queries(g, 6)

                    def tile(n, parity, first, last):
                        for q in range(NS + 3 * last):
                            b, g = divmod(q, NG)
                            if q < NS:
                                if q == 0:
                                    pe.wait_ge(s["q_rot_spread"], HG * n + HG)
                                if first and q == 0:
                                    pe.wait_ge(s["q_plain_kept"], NG)
                                elif b == 0:
                                    pe.wait_ge(s["q_plain_kept"], NG * n + g + 1)
                                if g % 2 == 0:
                                    pe.wait_ge(s["k_turned"], NK * n + 2 * b + g // 2 + 1)
                                wait(pe, "exp_done", NS * n + q - 1)
                                out = PS[:, 2 + q % 2, 0:SK]
                                nc.tensor.matmul(out, QN[parity][:, g, b].rearrange("p h i -> p (h i)"),
                                                 ctxT[:, b, :], start=True, stop=False)
                                nc.tensor.matmul(out, QRd[parity][:, g, b].rearrange("p h i -> p (h i)"),
                                                 KR[b % 2][:, g, :], start=False, stop=True)\
                                  .then_inc(s["scores_ready"], 1)
                            if (1 <= q or not first) and q <= NS:
                                pe.wait_ge(s["exp_done"], NS * n + q)
                                wait(pe, "pT_kept", NS * n + q - 1)
                                for c in range(2):
                                    ins = nc.tensor.transpose(PS[:, 4, c * P:(c + 1) * P],
                                                              PR[(q - 1) % 4][:, c * P:(c + 1) * P], core.ident[:])
                                ins.then_inc(s["pT_ready"], 1)
                            if (2 <= q or not first) and q <= NS + 1:
                                pe.wait_ge(s["pT_kept"], NS * n + q - 1)
                                wait(pe, "u_normed", NS * n + q - 2)
                                for c in range(2):
                                    ins = nc.tensor.matmul(PS[:, 5, 0:D], PT[q % 2][:, c, :],
                                                           C[(q - 2) % NS // NG][:, c, :], start=(c == 0),
                                                           stop=(c == 1))
                                ins.then_inc(s["u_ready"], 1)
                            if q == 3 and not first:
                                if last:
                                    pe.wait_ge(s["ctxT_kept"], BT * n + 3)
                                else:
                                    pe.wait_ge(s["q_plain_kept"], NG * (n + 1) + 1)
                                out_tile(n - 1)
                            if q >= 3 or not first:
                                pe.wait_ge(s["u_normed"], NS * n + q - 2)
                                wait(pe, "uT_kept", NS * n + q - 3)
                                nc.tensor.transpose(PS[:, 7, 0:P], U[(q - 3) % 2][:], core.ident[:])\
                                  .then_inc(s["uT_ready"], 1)
                            if q < NS:
                                if g % 2 == 0 and not (last and b + 1 == BT):
                                    keys(n, b + 1, g // 2)
                                bank6(n, q, first, last)

                    pe.wait_ge(s["zeroed"], 2)
                    turn_ctx(0, 0)
                    turn_h(0, 7)
                    keys(0, 0, 0)
                    pe.wait_ge(s["hT_kept"], 1)
                    rotary_queries(5)
                    for g in range(NG):
                        plain_queries(g, (2, 3, 4, 7)[g])
                    turn_ctx(0, 1)
                    keys(0, 0, 1)
                    in_slots(pe, tile)
                    pe.wait_ge(s["ctxT_kept"], BT * NT)
                    out_tile(NT - 1)


class FeedForward:

    def __init__(self, core):
        self.core = core
        names = ("h_ready", "hT_ready", "hT_kept", "hidden_ready", "gelu_done", "out_ready", "added", "done")
        self.sems = {n: core.sem("ffn_" + n) for n in names}

    def run(self, W1, W2, b1, norm_row, bias_row):
        core, nc, PS, s = self.core, self.core.nc, self.core.PS, self.sems
        NU = NT // 4
        X4 = core.X[:].rearrange("p (u j) d -> p u j d", j=4)
        R4 = core.rstd[:].rearrange("p (u j) o -> p u j o", j=4)
        with ExitStack() as st:
            H = core.buffer(st, "ffn_H", [P, 4, D])
            HT = core.buffer(st, "ffn_HT", [P, 4 * P])
            G = [core.buffer(st, f"ffn_G{i}", [P, FC, 4 * P]) for i in range(2)]
            with nc.Block() as block:
                @block.vector
                def _(dve):
                    def front(n):
                        for j in range(4):
                            nc.vector.scalar_tensor_tensor(H[:, j, :], X4[:, n, j, :], R4[:, n, j, :], norm_row[:],
                                                           ALU.mult, ALU.mult).then_inc(s["h_ready"], 1)
                        dve.wait_ge(s["hT_ready"], n + 1)
                        nc.vector.tensor_copy(HT[:], PS[:, 0, :]).then_inc(s["hT_kept"], 1)

                    def tile(n, parity, last):
                        if not last:
                            front(n + 1)
                        dve.wait_ge(s["out_ready"], n + 1)
                        nc.vector.tensor_tensor(X4[:, n], X4[:, n], PS[:, 5, :].rearrange("p (j d) -> p j d", j=4),
                                                ALU.add).then_inc(s["added"], 1)
                        dve.wait_ge(s["added"], n + 1)
                        nc.vector.tensor_tensor(X4[:, n], X4[:, n], bias_row[:].unsqueeze(1).to_broadcast([P, 4, D]),
                                                ALU.add).then_inc(s["done"], 1)

                    front(0)
                    in_pairs(dve, NU, tile)
                    dve.wait_ge(s["done"], NU)

                @block.scalar
                def _(act):
                    def tile(n, parity, last):
                        for c in range(FC):
                            act.wait_ge(s["hidden_ready"], FC * n + c + 1)
                            nc.scalar.activation(G[parity][:, c, :], PS[:, 1 + c, :], ACT.Gelu,
                                                 bias=b1[:, c:c + 1]).then_inc(s["gelu_done"], 1)

                    in_pairs(act, NU, tile)

                @block.tensor
                def _(pe):
                    def front(n, first):
                        pe.wait_ge(s["h_ready"], 4 * n + 4)
                        for j in range(4):
                            ins = nc.tensor.transpose(PS[:, 0, j * P:(j + 1) * P], H[:, j, :], core.ident[:])
                        ins.then_inc(s["hT_ready"], 1)
                        pe.wait_ge(s["hT_kept"], n + 1)
                        for c in range(FC):
                            if not first:
                                pe.wait_ge(s["gelu_done"], FC * (n - 1) + c + 1)
                            nc.tensor.matmul(PS[:, 1 + c, :], W1[:, c * P:(c + 1) * P], HT[:],
                                             start=True, stop=True).then_inc(s["hidden_ready"], 1)

                    def tile(n, parity, last):
                        if not last:
                            front(n + 1, False)
                        else:
                            pe.wait_ge(s["added"], n)
                        pe.wait_ge(s["gelu_done"], FC * n + FC)
                        for j in range(4):
                            for c in range(FC):
                                ins = nc.tensor.matmul(PS[:, 5, j * D:(j + 1) * D],
                                                       G[parity][:, c, j * P:(j + 1) * P],
                                                       W2[:, c, :], start=(c == 0), stop=(c == FC - 1))
                        ins.then_inc(s["out_ready"], 1)

                    front(0, True)
                    in_pairs(pe, NU, tile)


def project(core, st, HB):
    nc, PS, dram = core.nc, core.PS, core.dram
    NU = NT // 4
    Statistics(core, "rms_out").run(core.X, True)
    X4 = core.X[:].rearrange("p (u j) d -> p u j d", j=4)
    B4 = HB[:].rearrange("p (u j) d -> p u j d", j=4)
    R4 = core.rstd[:].rearrange("p (u j) o -> p u j o", j=4)
    loaded, h_ready, hT_ready, hT_kept, out_ready, added, done = (
        core.sem("proj_" + n) for n in ("loaded", "h_ready", "hT_ready", "hT_kept", "out_ready", "added", "done"))
    H = core.buffer(st, "proj_H", [P, 4, D])
    HT = core.buffer(st, "proj_HT", [P, 4 * P])
    Wp = core.buffer(st, "proj_W", [P, D])
    norm_row, bias_row = core.buffer(st, "proj_norm", [P, D]), core.buffer(st, "proj_bias", [P, D])
    with nc.Block() as block:
        @block.sync
        def _(sp):
            for dst, src in ((norm_row[:], dram["norm_out_w"].partition_broadcast(P)), (Wp[:], dram["proj_w"]),
                             (bias_row[:], dram["proj_b"].partition_broadcast(P)), (HB[:], core.x_tiles)):
                sp.dma_start(dst, src).then_inc(loaded, 16)
            sp.wait_ge(loaded, 64)

        @block.vector
        def _(dve):
            dve.wait_ge(loaded, 64)
            with dve.Fori(0, NU) as u:
                for j in range(4):
                    nc.vector.scalar_tensor_tensor(H[:, j, :], X4[:, u, j, :], R4[:, u, j, :], norm_row[:],
                                                   ALU.mult, ALU.mult).then_inc(h_ready, 1)
                dve.wait_ge(h_ready, 4 * u + 4)
                dve.wait_ge(out_ready, u + 1)
                nc.vector.tensor_tensor(X4[:, u], B4[:, u], PS[:, 1, :].rearrange("p (j d) -> p j d", j=4),
                                        ALU.add).then_inc(added, 1)
                dve.wait_ge(added, u + 1)
                nc.vector.tensor_tensor(X4[:, u], X4[:, u], bias_row[:].unsqueeze(1).to_broadcast([P, 4, D]),
                                        ALU.add).then_inc(done, 1)
                dve.wait_ge(done, u + 1)

        @block.scalar
        def _(act):
            with act.Fori(0, NU) as u:
                act.wait_ge(hT_ready, u + 1)
                nc.scalar.activation(HT[:], PS[:, 0, :], ACT.Copy).then_inc(hT_kept, 1)

        @block.tensor
        def _(pe):
            pe.wait_ge(loaded, 64)
            with pe.Fori(0, NU) as u:
                pe.wait_ge(h_ready, 4 * u + 4)
                for j in range(4):
                    ins = nc.tensor.transpose(PS[:, 0, j * P:(j + 1) * P], H[:, j, :], core.ident[:])
                ins.then_inc(hT_ready, 1)
                pe.wait_ge(hT_kept, u + 1)
                for j in range(4):
                    ins = nc.tensor.matmul(PS[:, 1, j * D:(j + 1) * D], HT[:, j * P:(j + 1) * P], Wp[:],
                                           start=True, stop=True)
                ins.then_inc(out_ready, 1)


class SmallAttention:

    def __init__(self, core, st):
        self.core = core
        buf = lambda name, shape: core.buffer(st, "small_" + name, shape)
        self.W = {n: buf("W" + n, [P, D]) for n in "qkvo"}
        self.rows = {n: buf("row_" + n, [P, D]) for n in ("bv", "bo", "g", "b")}
        self.cols = buf("cols", [P, 2])
        self.tables = {n: buf(n, [P, S]) for n in ("cos8_q", "sin8_q", "cos8_k", "sin8_k")}
        self.pick = buf("pick", [P, HG])
        self.H, self.HT = buf("H", [P, D]), buf("HT", [P, P])
        self.Q, self.K, self.keep = (buf(n, [P, P]) for n in ("Q", "K", "keep"))
        self.V = [buf(f"V{i}", [P, P]) for i in range(2)]
        self.QZ = buf("QZ", [P, NG, BT, HG, S])
        self.Qd = buf("Qd", [P, BT, HG, S])
        self.top, self.total, self.inverse = (buf(n, [P, NG, BT]) for n in ("top", "total", "inverse"))
        self.PR, self.PT = buf("PR", [P, NG, P]), buf("PT", [P, NG, P])
        self.picked, self.OT = buf("picked", [P, BT, HG, S]), buf("OT", [P, BT, S])

    def run(self, X, rotary):
        core, nc, PS, dram = self.core, self.core.nc, self.core.PS, self.core.dram
        name = "b_" if rotary else "c_"
        (loaded, h_ready, hT_ready, hT_kept, qkv_ready, q_spread, k_ready, v_kept, scores_ready, shifted, exp_done,
         probs_ready, pT_ready, pT_kept, o_ready, o_picked, out_ready, steps, held, zeroed, qz_ready) = (core.sem(name + n) for n in (
             "loaded", "h_ready", "hT_ready", "hT_kept", "qkv_ready", "q_spread", "k_ready", "v_kept", "scores_ready",
             "shifted", "exp_done", "probs_ready", "pT_ready", "pT_kept", "o_ready", "o_picked", "out_ready", "steps", "held",
             "zeroed", "qz_ready"))
        W, rows, tables, H, HT = self.W, self.rows, self.tables, self.H, self.HT
        loads = [(W[n][:], dram[name + "W" + n]) for n in "qkvo"]
        if rotary:
            loads += [(tables[n][:], dram[n]) for n in tables] + [(self.pick[:], dram["pick"])]
        else:
            loads += [(rows[n][:], dram["c_row_" + n].partition_broadcast(P)) for n in rows]
            loads += [(self.cols[:], dram["c_cols"])]
        need = 16 * len(loads)
        SC = PS[:, 4, :].rearrange("p (g b j) -> p g b j", g=NG, j=S)
        FRONT, SOFTMAX, PICK, ADD = (7, 3, 1, 1) if rotary else (3, 3, 1, 2)

        def per_row(v):
            return v[:].unsqueeze(3).to_broadcast([P, NG, BT, S])

        def slots(eng, slot):
            slot(0, 0, 0, False)
            slot(1, 1, 1, False)
            with eng.Fori(0, NT // 2 - 2) as u:
                slot(2 * u + 2, 0, 2, False)
                slot(2 * u + 3, 1, 2, False)
            slot(NT - 2, 0, 2, False)
            slot(NT - 1, 1, 2, True)

        with nc.Block() as block:
            @block.sync
            def _(sp):
                for dst, src in loads:
                    sp.dma_start(dst, src).then_inc(loaded, 16)

            @block.gpsimd
            def _(pool):
                nc.gpsimd.memset(self.QZ[:], 0.0).then_inc(zeroed, 1)

            @block.vector
            def _(dve):
                def hidden(step, n):
                    norm = nc.vector.tensor_scalar(H[:], X[:, n, :], core.mean_var[:, n, 0:1], core.rstd[:, n, :],
                                                   ALU.subtract, ALU.mult)
                    if rotary:
                        norm.then_inc(h_ready, 1)
                    else:
                        step(norm)
                        step(nc.vector.tensor_tensor(H[:], H[:], rows["g"][:], ALU.mult))
                        nc.vector.tensor_tensor(H[:], H[:], rows["b"][:], ALU.add).then_inc(h_ready, 1)

                view = lambda a: a.rearrange("p (b i) -> p b i", i=S)

                def turned(step, k, out):
                    raw = PS[:, 6, k * P:(k + 1) * P]
                    if not rotary:
                        return nc.vector.tensor_scalar(out[:], raw, self.cols[:, k:k + 1],
                                                       HD8 ** -0.5 if k == 0 else 1.0, ALU.add, ALU.mult)
                    bc = lambda a: tables[a][:].unsqueeze(1).to_broadcast([P, BT, S])
                    rope = Rope(nc, step, view(raw), view(self.keep[:]), bc("cos8_" + "qk"[k]),
                                bc("sin8_" + "qk"[k]), view(out[:]), SWAP_PAIRS)
                    rope.first()
                    return rope.second()

                def queries(step, n):
                    dve.wait_ge(qkv_ready, n + 1)
                    step(turned(step, 0, self.Q))
                    for h in range(HG):
                        nc.vector.tensor_scalar(self.Qd[:, :, h, :], view(self.Q[:]), self.pick[:, h:h + 1],
                                                None, ALU.mult).then_inc(q_spread, 1)

                def keys(step, n):
                    turned(step, 1, self.K).then_inc(k_ready, 1)

                def values(n, parity):
                    raw = PS[:, 6, 2 * P:3 * P]
                    if rotary:
                        nc.vector.tensor_copy(self.V[parity][:], raw).then_inc(v_kept, 1)
                    else:
                        nc.vector.tensor_tensor(self.V[parity][:], raw, rows["bv"][:], ALU.add).then_inc(v_kept, 1)

                def pick_heads(step, n):
                    dve.wait_ge(o_ready, n + 1)
                    step(nc.vector.tensor_tensor(self.picked[:], PS[:, 0:4, 0:P].rearrange("p b (h i) -> p b h i", i=S),
                                                 self.pick[:].unsqueeze(1).unsqueeze(3).to_broadcast([P, BT, HG, S]),
                                                 ALU.mult))
                    nc.vector.tensor_reduce(self.OT[:], self.picked[:].rearrange("p b h i -> p b i h"), AX.X,
                                            ALU.add).then_inc(o_picked, 1)

                def add_out(step, n):
                    dve.wait_ge(out_ready, n + 1)
                    step(nc.vector.tensor_tensor(X[:, n, :], X[:, n, :], PS[:, 7, 0:D], ALU.add))
                    if not rotary:
                        step(nc.vector.tensor_tensor(X[:, n, :], X[:, n, :], rows["bo"][:], ALU.add))

                def slot(m, parity, behind, last):
                    step = Steps(dve, steps, FRONT + m * (FRONT + SOFTMAX + PICK + ADD)
                                 - PICK * (behind > 0) - ADD * behind)
                    if not last:
                        hidden(step, m + 1)
                    dve.wait_ge(scores_ready, m + 1)
                    step(nc.vector.tensor_reduce(self.top[:], SC, AX.X, ALU.max))
                    nc.vector.tensor_tensor(SC, SC, per_row(self.top), ALU.subtract).then_inc(shifted, 1)
                    if not last:
                        queries(step, m + 1)
                    dve.wait_ge(exp_done, m + 1)
                    step(nc.vector.tensor_reduce(self.total[:], SC, AX.X, ALU.add))
                    step(nc.vector.reciprocal(self.inverse[:], self.total[:]))
                    if behind:
                        dve.wait_ge(pT_ready, m)
                    nc.vector.tensor_tensor(self.PR[:].rearrange("p g (b j) -> p g b j", j=S), SC,
                                            per_row(self.inverse), ALU.mult).then_inc(probs_ready, 1)
                    if not last:
                        keys(step, m + 1)
                    if behind > 1:
                        add_out(step, m - 2)
                    if behind:
                        pick_heads(step, m - 1)
                    if not last:
                        values(m + 1, 1 - parity)
                    assert step.n == SOFTMAX + PICK * (behind > 0) + ADD * (behind > 1) + FRONT * (not last)

                dve.wait_ge(loaded, need)
                step = Steps(dve, steps, 0)
                hidden(step, 0)
                queries(step, 0)
                keys(step, 0)
                values(0, 0)
                slots(dve, slot)
                step = Steps(dve, steps, FRONT * NT + SOFTMAX * NT + PICK * (NT - 1) + ADD * (NT - 2))
                add_out(step, NT - 2)
                pick_heads(step, NT - 1)
                add_out(step, NT - 1)

            @block.scalar
            def _(act):
                def keep_hT(n):
                    act.wait_ge(hT_ready, n + 1)
                    nc.scalar.activation(HT[:], PS[:, 5, 0:P], ACT.Copy).then_inc(hT_kept, 1)

                def spread(n):
                    act.wait_ge(q_spread, HG * n + HG)
                    for g in range(NG):
                        r = slice(32 * g, 32 * g + 32)
                        nc.scalar.activation(self.QZ[r, g], self.Qd[r], ACT.Copy).then_inc(qz_ready, 1)

                def keep_pT(n):
                    act.wait_ge(pT_ready, n + 1)
                    nc.scalar.activation(self.PT[:].rearrange("p g n -> p (g n)"), PS[:, 5, :],
                                         ACT.Copy).then_inc(pT_kept, 1)

                def slot(m, parity, behind, last):
                    if not last:
                        keep_hT(m + 1)
                    if behind:
                        keep_pT(m - 1)
                    act.wait_ge(shifted, m + 1)
                    nc.scalar.activation(SC, SC, ACT.Exp).then_inc(exp_done, 1)
                    if not last:
                        spread(m + 1)

                act.wait_ge(zeroed, 1)
                keep_hT(0)
                spread(0)
                slots(act, slot)
                keep_pT(NT - 1)

            @block.tensor
            def _(pe):
                def turn_h(n):
                    pe.wait_ge(h_ready, n + 1)
                    nc.tensor.transpose(PS[:, 5, 0:P], H[:], core.ident[:]).then_inc(hT_ready, 1)

                def project(n):
                    pe.wait_ge(hT_kept, n + 1)
                    nc.tensor.matmul(PS[:, 6, 0:P], W["q"][:], HT[:], start=True, stop=True)
                    nc.tensor.matmul(PS[:, 6, P:2 * P], W["k"][:], HT[:], start=True, stop=True)
                    nc.tensor.matmul(PS[:, 6, 2 * P:3 * P], HT[:], W["v"][:], start=True,
                                     stop=True).then_inc(qkv_ready, 1)

                def scores(n, last):
                    pe.wait_ge(qz_ready, NG * n + NG)
                    pe.wait_ge(k_ready, n + 1)
                    for g in range(NG):
                        if g == 2 and not last:
                            turn_h(n + 1)
                        for b in range(BT):
                            ins = nc.tensor.matmul(PS[:, 4, g * P + b * S:g * P + (b + 1) * S],
                                                   self.QZ[:, g, b].rearrange("p h i -> p (h i)"),
                                                   self.K[:, b * S:(b + 1) * S], start=True, stop=True)
                    ins.then_inc(scores_ready, 1)

                def turn_probs(n):
                    pe.wait_ge(probs_ready, n + 1)
                    for g in range(NG):
                        ins = nc.tensor.transpose(PS[:, 5, g * P:(g + 1) * P], self.PR[:, g, :], core.ident[:])
                    ins.then_inc(pT_ready, 1)

                def results(n, parity):
                    pe.wait_ge(v_kept, n + 1)
                    pe.wait_ge(pT_kept, n + 1)
                    pe.sem_inc(held, 1)
                    for g in range(NG):
                        for b in range(BT):
                            r, c = slice(32 * b, 32 * b + 32), slice(32 * g, 32 * g + 32)
                            ins = nc.tensor.matmul(PS[c, b, 0:P], self.V[parity][r, c], self.PT[r, g, :],
                                                   start=True, stop=True)
                    ins.then_inc(o_ready, 1)

                def output(n):
                    pe.wait_ge(o_picked, n + 1)
                    nc.tensor.matmul(PS[:, 7, 0:D], self.OT[:].rearrange("p b i -> p (b i)"), W["o"][:],
                                     start=True, stop=True).then_inc(out_ready, 1)

                def slot(m, parity, behind, last):
                    scores(m, last)
                    if behind > 1:
                        output(m - 2)
                    if not last:
                        if behind:
                            pe.wait_ge(v_kept, m + 1)
                        project(m + 1)
                    if behind:
                        turn_probs(m - 1)
                        results(m - 1, 1 - parity)

                pe.wait_ge(loaded, need)
                pe.wait_ge(zeroed, 1)
                turn_h(0)
                project(0)
                slots(pe, slot)
                output(NT - 2)
                turn_probs(NT - 1)
                results(NT - 1, 1)
                output(NT - 1)


def experts(core, st, HB):
    nc, PS, dram, X = core.nc, core.PS, core.dram, core.X
    buf = lambda name, shape: core.buffer(st, "moe_" + name, shape)
    H2T = buf("H2T", [P, NT, P])
    W1, W2 = buf("W1", [P, NE, FF]), buf("W2", [P, NE, FC, D])
    b1, b2 = buf("b1", [P, NE, FC]), buf("b2", [NE, D])
    Wr = buf("Wr", [P, NE])
    g_col, b_col = buf("g_col", [P, 1]), buf("b_col", [P, 1])
    upto, ones = buf("upto", [P, P]), buf("ones", [P, P])
    order = buf("order", [P, NE])
    H, HT = buf("H", [P, 4, D]), buf("HT", [P, 4 * P])
    L, E, PRB, EQ, M1, M2, C1, C2, A, A2, V1 = (buf(n, [P, NT, NE]) for n in (
        "logits", "exps", "probs", "equal", "first", "second", "place1", "place2", "scan_a", "scan_b", "kept"))
    GATE = buf("gate", [P, NT, NE])
    row, row2, row3 = buf("row", [P, NT]), buf("row2", [P, NT]), buf("row3", [P, NT])
    sems = {n: core.sem("moe_" + n) for n in (
        "loaded", "experts_loaded", "h_ready", "hT_ready", "hT_kept", "hT_kept_all", "logits_ready", "logits_kept",
        "shifted", "exp_done", "steps", "masks_ready", "counts_ready", "gates_ready",
        "gT_ready", "gT_kept", "base_ready", "base_added", "base_all", "hidden_ready", "relu_act", "relu_dve",
        "y_ready", "y_added", "stored")}
    S_ = lambda n: sems[n]
    expert_loads = [(b1[:], dram["e_b1T"]), (b2[:], dram["e_b2"]),
                    (W1[:], dram["e_w1"].rearrange("e d f -> d e f")),
                    (W2[:], dram["e_w2"].rearrange("e (c p) d -> p e c d", p=P))]
    loads = [(Wr[:], dram["wr"]), (g_col[:], dram["ln2_g"]), (b_col[:], dram["ln2_b"]),
             (upto[:], dram["upto"]), (ones[:], dram["ones"]), (order[:], dram["order"])]

    NU = NT // 4
    HT4 = H2T[:].rearrange("p (u j) n -> p u (j n)", j=4)
    X4 = X[:].rearrange("p (u j) d -> p u j d", j=4)
    HB4 = HB[:].rearrange("p (u j) d -> p u j d", j=4)
    G4, L4 = (a[:].rearrange("p (u j) e -> p u j e", j=4) for a in (GATE, L))
    MV4, R4 = (a[:].rearrange("p (u j) o -> p u j o", j=4) for a in (core.mean_var, core.rstd))

    with nc.Block() as block:
        @block.sync
        def _(sp):
            for dst, src in loads:
                sp.dma_start(dst, src).then_inc(S_("loaded"), 16)
            for dst, src in expert_loads:
                sp.dma_start(dst, src).then_inc(S_("experts_loaded"), 16)
            sp.wait_ge(S_("loaded"), 16 * len(loads))

        @block.vector
        def _(dve):
            dve.wait_ge(S_("loaded"), 16 * len(loads))
            with dve.Fori(0, NU) as u:
                for j in range(4):
                    nc.vector.tensor_scalar(H[:, j, :], HB4[:, u, j, :], MV4[:, u, j, :], R4[:, u, j, :],
                                            ALU.subtract, ALU.mult).then_inc(S_("h_ready"), 1)
                dve.wait_ge(S_("hT_ready"), u + 1)
                nc.vector.tensor_scalar(HT[:], PS[:, 0, :], g_col[:], b_col[:], ALU.mult,
                                        ALU.add).then_inc(S_("hT_kept"), 1)
                dve.wait_ge(S_("logits_ready"), u + 1)
                nc.vector.tensor_copy(L4[:, u], PS[:, 1, 0:4 * NE].rearrange("p (j e) -> p j e", j=4))\
                  .then_inc(S_("logits_kept"), 1)
                dve.wait_ge(S_("hT_kept_all"), u + 1)
                dve.wait_ge(S_("logits_kept"), u + 1)

        @block.scalar
        def _(act):
            with act.Fori(0, NU) as u:
                act.wait_ge(S_("hT_kept"), u + 1)
                nc.scalar.activation(HT4[:, u, :], HT[:], ACT.Copy).then_inc(S_("hT_kept_all"), 1)

        @block.tensor
        def _(pe):
            pe.wait_ge(S_("loaded"), 16 * len(loads))
            with pe.Fori(0, NU) as u:
                pe.wait_ge(S_("h_ready"), 4 * u + 4)
                for j in range(4):
                    ins = nc.tensor.transpose(PS[:, 0, j * P:(j + 1) * P], H[:, j, :], core.ident[:])
                ins.then_inc(S_("hT_ready"), 1)
                pe.wait_ge(S_("hT_kept"), u + 1)
                for j in range(4):
                    ins = nc.tensor.matmul(PS[:, 1, j * NE:(j + 1) * NE], HT[:, j * P:(j + 1) * P], Wr[:],
                                           start=True, stop=True)
                ins.then_inc(S_("logits_ready"), 1)

    def each(v):
        return v[:].unsqueeze(2).to_broadcast([P, NT, NE])

    with nc.Block() as block:
        @block.vector
        def _(dve):
            step = Steps(dve, S_("steps"), 0)
            tt = lambda o, a, b, op: step(nc.vector.tensor_tensor(o, a, b, op))
            orders = order[:].unsqueeze(1).to_broadcast([P, NT, NE])

            def one_hot(dst, values):
                step(nc.vector.tensor_reduce(row[:], values, AX.X, ALU.max))
                tt(EQ[:], values, each(row), ALU.is_equal)
                tt(EQ[:], EQ[:], orders, ALU.mult)
                step(nc.vector.tensor_reduce(row[:], EQ[:], AX.X, ALU.max))
                tt(dst, EQ[:], each(row), ALU.is_equal)

            step(nc.vector.tensor_reduce(row[:], L[:], AX.X, ALU.max))
            nc.vector.tensor_tensor(E[:], L[:], each(row), ALU.subtract).then_inc(S_("shifted"), 1)
            dve.wait_ge(S_("exp_done"), 1)
            step(nc.vector.tensor_reduce(row[:], E[:], AX.X, ALU.add))
            step(nc.vector.reciprocal(row2[:], row[:]))
            tt(PRB[:], E[:], each(row2), ALU.mult)
            one_hot(M1[:], PRB[:])
            step(nc.vector.tensor_scalar(EQ[:], M1[:], -3.0e38, None, ALU.mult))
            tt(L[:], L[:], EQ[:], ALU.add)
            one_hot(M2[:], L[:])
            dve.wait_ge(S_("steps"), step.n)
            nc.vector.tensor_copy(V1[:], M2[:]).then_inc(S_("masks_ready"), 1)
            dve.wait_ge(S_("counts_ready"), 1)

            def places(dst, k):
                step(nc.vector.tensor_copy(A[:], PS[:, 2 * k + 1, 0:NT * NE]))
                a, b = A, A2
                shift = 1
                while shift < NT:
                    step(nc.vector.tensor_copy(b[:, 0:shift, :], a[:, 0:shift, :]))
                    tt(b[:, shift:NT, :], a[:, shift:NT, :], a[:, 0:NT - shift, :], ALU.add)
                    a, b = b, a
                    shift *= 2
                tt(dst, a[:], PS[:, 2 * k + 1, 0:NT * NE].rearrange("p (t e) -> p t e", e=NE), ALU.subtract)
                tt(dst, dst, PS[:, 2 * k, 0:NT * NE].rearrange("p (t e) -> p t e", e=NE), ALU.add)
                return a

            a = places(C1[:], 0)
            step(nc.vector.tensor_copy(V1[:, 0, :], a[:, NT - 1, :]))
            places(C2[:], 1)
            tt(C2[:], C2[:], V1[:, 0:1, :].to_broadcast([P, NT, NE]), ALU.add)
            for m, c in ((M1, C1), (M2, C2)):
                step(nc.vector.tensor_scalar(c[:], c[:], float(CAP), None, ALU.is_le))
                tt(m[:], m[:], c[:], ALU.mult)
            for m, r in ((M1, row2), (M2, row3)):
                tt(EQ[:], PRB[:], m[:], ALU.mult)
                step(nc.vector.tensor_reduce(r[:], EQ[:], AX.X, ALU.add))
            tt(row[:], row2[:], row3[:], ALU.add)
            step(nc.vector.tensor_scalar(row[:], row[:], float(np.finfo(np.float32).eps), None, ALU.max))
            step(nc.vector.reciprocal(row[:], row[:]))
            for m, r in ((M1, row2), (M2, row3)):
                tt(r[:], r[:], row[:], ALU.mult)
                tt(m[:], m[:], each(r), ALU.mult)
            tt(GATE[:], M1[:], M2[:], ALU.add)
            step(nc.vector.tensor_scalar(GATE[:], GATE[:], 1.0 - 0.2, None, ALU.mult))

        @block.scalar
        def _(act):
            act.wait_ge(S_("shifted"), 1)
            nc.scalar.activation(E[:], E[:], ACT.Exp).then_inc(S_("exp_done"), 1)

        @block.tensor
        def _(pe):
            pe.wait_ge(S_("masks_ready"), 1)
            for k, m in enumerate((M1, M2)):
                flat = m[:].rearrange("p t e -> p (t e)")
                nc.tensor.matmul(PS[:, 2 * k, 0:NT * NE], upto[:], flat, start=True, stop=True)
                ins = nc.tensor.matmul(PS[:, 2 * k + 1, 0:NT * NE], ones[:], flat, start=True, stop=True)
            ins.then_inc(S_("counts_ready"), 1)

    GT = buf("gT", [NE, 4 * P])
    G8 = buf("g8", [P, 4, NE])
    with nc.Block() as block:
        @block.vector
        def _(dve):
            with dve.Fori(0, NU) as u:
                nc.vector.tensor_copy(G8[:], G4[:, u]).then_inc(S_("gates_ready"), 1)
                nc.vector.tensor_tensor(X4[:, u], X4[:, u], HB4[:, u], ALU.add).then_inc(S_("base_added"), 1)
                dve.wait_ge(S_("base_added"), u + 1)
                dve.wait_ge(S_("base_ready"), u + 1)
                nc.vector.tensor_tensor(X4[:, u], X4[:, u], PS[:, 1, :].rearrange("p (j d) -> p j d", j=4),
                                        ALU.add).then_inc(S_("base_all"), 1)
                dve.wait_ge(S_("base_all"), u + 1)

        @block.scalar
        def _(act):
            with act.Fori(0, NU) as u:
                act.wait_ge(S_("gT_ready"), u + 1)
                nc.scalar.activation(GT[:], PS[0:NE, 0, :], ACT.Copy).then_inc(S_("gT_kept"), 1)

        @block.tensor
        def _(pe):
            pe.wait_ge(S_("experts_loaded"), 16 * len(expert_loads))
            with pe.Fori(0, NU) as u:
                pe.wait_ge(S_("gates_ready"), u + 1)
                for j in range(4):
                    ins = nc.tensor.transpose(PS[0:NE, 0, j * P:(j + 1) * P], G8[:, j, :], core.ident[:])
                ins.then_inc(S_("gT_ready"), 1)
                pe.wait_ge(S_("gT_kept"), u + 1)
                for j in range(4):
                    ins = nc.tensor.matmul(PS[:, 1, j * D:(j + 1) * D], GT[:, j * P:(j + 1) * P], b2[:],
                                           start=True, stop=True)
                ins.then_inc(S_("base_ready"), 1)

    out4 = dram["out"].rearrange("(u j b) s d -> u (b s) j d", j=4, b=BT)
    G = [buf(f"hidden{i}", [P, FC, 4 * P]) for i in range(2)]
    with nc.Block() as block:
        @block.tensor
        def _(pe):
            with pe.Fori(0, NU) as u:
                def up(e):
                    for c in range(FC):
                        if e >= 1:
                            pe.wait_ge(S_(("relu_act", "relu_dve")[c % 2]), 2 * NE * u + 2 * (e - 1) + c // 2 + 1)
                        nc.tensor.matmul(PS[:, 2 + c, :], W1[:, e, c * P:(c + 1) * P], HT4[:, u, :],
                                         start=True, stop=True).then_inc(S_("hidden_ready"), 1)
                up(0)
                for e in range(NE):
                    if e + 1 < NE:
                        up(e + 1)
                    pe.wait_ge(S_("relu_act"), 2 * NE * u + 2 * e + 2)
                    pe.wait_ge(S_("relu_dve"), 2 * NE * u + 2 * e + 2)
                    if e >= 2:
                        pe.wait_ge(S_("y_added"), 4 * (NE * u + e - 1))
                    for j in range(4):
                        for c in range(FC):
                            ins = nc.tensor.matmul(PS[:, 6 + e % 2, j * D:(j + 1) * D],
                                                   G[e % 2][:, c, j * P:(j + 1) * P], W2[:, e, c, :],
                                                   start=(c == 0), stop=(c == FC - 1))
                    ins.then_inc(S_("y_ready"), 1)
                pe.wait_ge(S_("y_added"), 4 * NE * (u + 1))

        @block.scalar
        def _(act):
            with act.Fori(0, NU) as u:
                for e in range(NE):
                    for c in (0, 2):
                        act.wait_ge(S_("hidden_ready"), FC * (NE * u + e) + c + 1)
                        if e >= 2:
                            act.wait_ge(S_("y_ready"), NE * u + e - 1)
                        nc.scalar.activation(G[e % 2][:, c, :], PS[:, 2 + c, :], ACT.Relu,
                                             bias=b1[:, e, c:c + 1]).then_inc(S_("relu_act"), 1)

        @block.vector
        def _(dve):
            with dve.Fori(0, NU) as u:
                for e in range(NE + 1):
                    for c in (1, 3):
                        if e < NE:
                            dve.wait_ge(S_("hidden_ready"), FC * (NE * u + e) + c + 1)
                            if e >= 2:
                                dve.wait_ge(S_("y_ready"), NE * u + e - 1)
                            nc.vector.tensor_scalar(G[e % 2][:, c, :], PS[:, 2 + c, :], b1[:, e, c:c + 1], 0.0,
                                                    ALU.add, ALU.max).then_inc(S_("relu_dve"), 1)
                    if e:
                        dve.wait_ge(S_("y_ready"), NE * u + e)
                        if e >= 2:
                            dve.wait_ge(S_("y_added"), 4 * (NE * u + e - 1))
                        for j in range(4):
                            nc.vector.scalar_tensor_tensor(X4[:, u, j, :], PS[:, 6 + (e - 1) % 2, j * D:(j + 1) * D],
                                                           G4[:, u, j, e - 1:e], X4[:, u, j, :], ALU.mult,
                                                           ALU.add).then_inc(S_("y_added"), 1)

        @block.sync
        def _(sp):
            with sp.Fori(0, NU) as u:
                sp.wait_ge(S_("y_added"), 4 * NE * (u + 1))
                sp.dma_start(out4[u], X4[:, u]).then_inc(S_("stored"), 16)
            sp.wait_ge(S_("stored"), 16 * NU)


def tables():
    f32 = np.float32
    t = {"ident": np.eye(P, dtype=f32), "ones": np.ones((P, P), f32),
         "upto": np.triu(np.ones((P, P), f32)),
         "order": np.tile(np.arange(NE, 0, -1, dtype=f32), (P, 1))}
    lanes = np.arange(P)
    c = lanes % 32
    inv = (1.0 / f32(10000.0) ** (np.arange(0, ROT, 2, dtype=f32) / f32(ROT))).astype(f32)
    angle = (np.arange(SK, dtype=f32)[:, None] * inv[None, :]).astype(f32)[:, c % 16].T
    sign = np.where(c < 16, -1.0, 1.0).astype(f32)[:, None]
    t["cos_k"], t["sin_k"] = np.cos(angle).astype(f32), (np.sin(angle) * sign).astype(f32)
    t["cos_q"] = (t["cos_k"][:, :S] * f32(DH ** -0.5)).astype(f32)
    t["sin_q"] = (t["sin_k"][:, :S] * f32(DH ** -0.5)).astype(f32)
    c = lanes % HD8
    inv = (1.0 / f32(10000.0) ** (np.arange(0, HD8, 2, dtype=f32) / f32(HD8))).astype(f32)
    angle = (np.arange(S, dtype=f32)[:, None] * inv[None, :]).astype(f32)[:, c % 4].T
    sign = np.where(c < 4, -1.0, 1.0).astype(f32)[:, None]
    t["cos8_k"], t["sin8_k"] = np.cos(angle).astype(f32), (np.sin(angle) * sign).astype(f32)
    t["cos8_q"] = (t["cos8_k"] / f32(HD8 ** -0.5)).astype(f32)
    t["sin8_q"] = (t["sin8_k"] / f32(HD8 ** -0.5)).astype(f32)
    t["pick"] = (lanes[:, None] % 32 // HD8 == np.arange(HG)[None, :]).astype(f32)
    return t


def lay_out(i):
    def heads(w, rotated):
        w = w.reshape(LAYERS, D, NH, DH)
        return (w[..., :ROT] if rotated else w[..., ROT:]).reshape(LAYERS, D, NH * ROT)

    def pairs_swapped(w):
        w = w.reshape(LAYERS, D, NG, 2, 2 * ROT)
        return w[:, :, :, ::-1].reshape(LAYERS, D, NH * ROT)

    x = "L0_xattn_"
    a = {"x": i["x"], "ctx": i["ctx_1024"], "mask": i["mask_BxS_bf1"].view(np.uint8).reshape(-1)}
    a["sqR"], a["skR"] = heads(i[x + "Wq"], True), heads(i[x + "Wk"], True)
    a["sqN"], a["skN"] = (pairs_swapped(heads(i[x + n], False)) for n in ("Wq", "Wk"))
    a["cqR"], a["ckR"] = heads(i[x + "cWq"], True), heads(i[x + "cWk"], True)
    a["cqNT"] = heads(i[x + "cWq"], False).transpose(0, 2, 1)
    a["ckNT"] = heads(i[x + "cWk"], False).transpose(0, 2, 1)
    a["sWvT"], a["cWvT"] = i[x + "Wv"].transpose(0, 2, 1), i[x + "cWv"].transpose(0, 2, 1)
    a["sWo"], a["cWo"] = i[x + "Wo"], i[x + "cWo"]
    a["w1"], a["w2"] = i[x + "ff_w1"], i[x + "ff_w2"]
    a["b1T"] = i[x + "ff_b1"].reshape(LAYERS, FC, P).transpose(0, 2, 1)
    for n, src in (("sw", "attn_norm_w"), ("cw", "cross_norm_w"), ("fw", "ff_norm_w"), ("sbo", "bo"),
                   ("cbo", "cbo"), ("fb2", "ff_b2")):
        a["row_" + n] = i[x + src]
    for n in ("norm_out_w", "proj_w", "proj_b"):
        a[n] = i[x + n]
    for n in "qkvo":
        a["b_W" + n] = i["L0_attn_W" + n].T
        a["c_W" + n] = i["L0_ffn_w" + n]
    for n, src in (("bv", "bv"), ("bo", "bo"), ("g", "ln1_g"), ("b", "ln1_b")):
        a["c_row_" + n] = i["L0_ffn_" + src]
    a["c_cols"] = np.stack([i["L0_ffn_bq"], i["L0_ffn_bk"]], axis=1)
    a["e_w1"], a["e_w2"], a["e_b2"], a["wr"] = (i["L0_ffn_" + n] for n in ("w1", "w2", "b2", "wr"))
    a["e_b1T"] = i["L0_ffn_b1"].reshape(NE, FC, P).transpose(2, 0, 1)
    a["ln2_g"], a["ln2_b"] = i["L0_ffn_ln2_g"][:, None], i["L0_ffn_ln2_b"][:, None]
    return a


def kernel(**inputs):
    import concourse.bacc as bacc
    from concourse.bass_utils import run_bass_kernel_spmd

    nc = bacc.Bacc("TRN2", target_bir_lowering=False, num_devices=1)
    arrays = {n: np.ascontiguousarray(a) for n, a in lay_out({k: np.asarray(v) for k, v in inputs.items()}).items()}
    arrays.update({n: np.ascontiguousarray(a) for n, a in tables().items()})
    dram = {n: nc.dram_tensor("in_" + n, a.shape, mybir.dt.from_np(a.dtype), kind="ExternalInput").ap()
            for n, a in arrays.items()}
    dram["out"] = nc.dram_tensor("out", (B, S, D), F32, kind="ExternalOutput").ap()
    build(nc, dram)
    r = run_bass_kernel_spmd(nc, [{"in_" + n: a for n, a in arrays.items()}], core_ids=[0])
    return r.results[0]["out"]
```
